# Optimizing a Trainium2 kernel written in Bass

```python
import numpy as np
import jax
import jax.numpy as jnp

def _softmax(x, axis=-1):
    return jax.nn.softmax(x, axis=axis)

def _gelu(x):
    return jax.nn.gelu(x, approximate=True)

def _silu(x):
    return jax.nn.silu(x)

def _sigmoid(x):
    return jax.nn.sigmoid(x)

def _layernorm(x, axis=-1, eps=1e-05):
    m = jnp.mean(x, axis=axis, keepdims=True)
    v = jnp.var(x, axis=axis, keepdims=True)
    return (x - m) / jnp.sqrt(v + eps)

def _scatter_add(tgt, idx, src, axis=0):
    return tgt.at[idx].add(src)

def _segment_sum(src, seg, n):
    return jax.ops.segment_sum(src, seg, n)
kernel_name = 'mk_cond_resid_d4_seqx_r2_c4d35f'

def setup_inputs(seed: int=0):
    np.random.seed(seed)
    _w = jnp.asarray

    def _rec_inputs():
        import jax
        import jax.numpy as jnp
        _rk = jax.random.key(seed)
        x = -0.000125 + 0.9999 * jax.random.normal(jax.random.fold_in(_rk, 1), (16, 512, 512), jnp.float32)
        _lenS = 512 - jax.random.randint(jax.random.fold_in(_rk, 7), (16,), 0, max(1, 512 // 4) + 1, jnp.int32)
        _lenS2 = 512 - jax.random.randint(jax.random.fold_in(_rk, 8), (16,), 0, max(1, 512 // 4) + 1, jnp.int32)
        cond_1024 = 0.00782532 + 1.00527 * jax.random.normal(jax.random.fold_in(_rk, 11), (16, 512), jnp.float32)
        return (x, cond_1024)
    x, cond_1024 = _rec_inputs()

    def _L0_cond_setup():
        import jax, jax.numpy as jnp
        import numpy as np
        INV_SQRT2 = 0.7071067811865476
        key = jax.random.key(seed)
        k1, k2, k3, k4 = jax.random.split(key, 4)
        B, N, d = (8, 2048, 512)
        scale = 1.0 / np.sqrt(d)
        return {'v': jax.random.normal(k1, (B, N, d), dtype=jnp.float32), 'q_pool': jax.random.normal(k2, (B, d), dtype=jnp.float32), 'W1': jax.random.normal(k3, (d, d), dtype=jnp.float32) * scale, 'b1': jnp.zeros((d,), dtype=jnp.float32), 'W2': jax.random.normal(k4, (d, d), dtype=jnp.float32) * scale, 'b2': jnp.zeros((d,), dtype=jnp.float32)}
    _L0_cond_all = _L0_cond_setup()
    _L0_cond_in = {k: v for k, v in _L0_cond_all.items() if k in ('W1', 'b1', 'W2', 'b2')}
    del _L0_cond_all

    def _L1_cond_setup():
        import jax, jax.numpy as jnp
        import numpy as np
        import math
        N, T, D, H = (128, 256, 512, 512)
        key = jax.random.key(seed)
        k1, k2, k3, k4 = jax.random.split(key, 4)
        x = jax.random.normal(k1, (N, T, D), dtype=jnp.float32)
        h0 = jax.random.normal(k2, (N, H), dtype=jnp.float32)
        Wx = jax.random.normal(k3, (D, H), dtype=jnp.float32) / math.sqrt(D)
        Wh = jax.random.normal(k4, (H, H), dtype=jnp.float32) / math.sqrt(H)
        b = jnp.zeros((H,), dtype=jnp.float32)
        return {'x': x, 'h0': h0, 'Wx': Wx, 'Wh': Wh, 'b': b}
    _L1_cond_all = _L1_cond_setup()
    _L1_cond_in = {k: v for k, v in _L1_cond_all.items() if k in ('Wx', 'Wh', 'b')}
    del _L1_cond_all

    def _L2_cond_setup():
        import jax, jax.numpy as jnp
        import numpy as np
        EPS = 1e-08
        key = jax.random.key(seed)
        ks = jax.random.split(key, 8)
        B, S, D, H = (8, 1024, 512, 512)
        scale = 1.0 / np.sqrt(D)
        return {'input_seq': jax.random.normal(ks[0], (B, S, D), dtype=jnp.float32), 'initial_hidden': jax.random.normal(ks[1], (B, H), dtype=jnp.float32), 'W_f': jax.random.normal(ks[2], (H, D), dtype=jnp.float32) * scale, 'b_f': jnp.zeros((H,), dtype=jnp.float32), 'W_i': jax.random.normal(ks[3], (H, D), dtype=jnp.float32) * scale, 'b_i': jnp.zeros((H,), dtype=jnp.float32), 'W_h': jax.random.normal(ks[4], (H, D), dtype=jnp.float32) * scale, 'b_h': jnp.zeros((H,), dtype=jnp.float32)}
    _L2_cond_all = _L2_cond_setup()
    _L2_cond_in = {k: v for k, v in _L2_cond_all.items() if k in ('W_f', 'b_f', 'W_i', 'b_i', 'W_h', 'b_h')}
    del _L2_cond_all

    def _L3_cond_setup():
        import jax, jax.numpy as jnp
        import numpy as np
        B, T, D = (128, 32, 512)
        ADA, INTER, RANK = (512, 512, 8)
        LN_EPS = 1e-05

        def _layernorm(x, g, b):
            mu = jnp.mean(x, axis=-1, keepdims=True)
            var = jnp.var(x, axis=-1, keepdims=True)
            return (x - mu) * jax.lax.rsqrt(var + LN_EPS) * g + b
        key = jax.random.key(seed)
        ks = jax.random.split(key, 9)
        return {'x': jax.random.normal(ks[0], (B, T, D), dtype=jnp.float32), 'ada_emb': jax.random.normal(ks[1], (B, ADA), dtype=jnp.float32), 'base_layer': jax.random.normal(ks[2], (D, D), dtype=jnp.float32), 'w1': jax.random.normal(ks[3], (ADA, INTER), dtype=jnp.float32) * 0.02, 'b1': jnp.zeros((INTER,), dtype=jnp.float32), 'w2': jax.random.normal(ks[4], (INTER, 2 * D * RANK), dtype=jnp.float32) * 0.02, 'b2': jnp.zeros((2 * D * RANK,), dtype=jnp.float32), 'ln_g': jnp.ones((ADA,), dtype=jnp.float32), 'ln_b': jnp.zeros((ADA,), dtype=jnp.float32)}
    _L3_cond_all = _L3_cond_setup()
    _L3_cond_in = {k: v for k, v in _L3_cond_all.items() if k in ('base_layer', 'w1', 'b1', 'w2', 'b2', 'ln_g', 'ln_b')}
    del _L3_cond_all
    return {'x': x, 'cond_1024': cond_1024, 'L0_cond_W1': _L0_cond_in['W1'], 'L0_cond_b1': _L0_cond_in['b1'], 'L0_cond_W2': _L0_cond_in['W2'], 'L0_cond_b2': _L0_cond_in['b2'], 'L1_cond_Wx': _L1_cond_in['Wx'], 'L1_cond_Wh': _L1_cond_in['Wh'], 'L1_cond_b': _L1_cond_in['b'], 'L2_cond_W_f': _L2_cond_in['W_f'], 'L2_cond_b_f': _L2_cond_in['b_f'], 'L2_cond_W_i': _L2_cond_in['W_i'], 'L2_cond_b_i': _L2_cond_in['b_i'], 'L2_cond_W_h': _L2_cond_in['W_h'], 'L2_cond_b_h': _L2_cond_in['b_h'], 'L3_cond_base_layer': _L3_cond_in['base_layer'], 'L3_cond_w1': _L3_cond_in['w1'], 'L3_cond_b1': _L3_cond_in['b1'], 'L3_cond_w2': _L3_cond_in['w2'], 'L3_cond_b2': _L3_cond_in['b2'], 'L3_cond_ln_g': _L3_cond_in['ln_g'], 'L3_cond_ln_b': _L3_cond_in['ln_b']}

def reference(x, cond_1024, L0_cond_W1, L0_cond_b1, L0_cond_W2, L0_cond_b2, L1_cond_Wx, L1_cond_Wh, L1_cond_b, L2_cond_W_f, L2_cond_b_f, L2_cond_W_i, L2_cond_b_i, L2_cond_W_h, L2_cond_b_h, L3_cond_base_layer, L3_cond_w1, L3_cond_b1, L3_cond_w2, L3_cond_b2, L3_cond_ln_g, L3_cond_ln_b):
    import jax
    import jax.numpy as jnp

    def _L0_cond_ref(v, q_pool, W1, b1, W2, b2):
        import jax, jax.numpy as jnp
        import numpy as np
        INV_SQRT2 = 0.7071067811865476
        B, N, d = v.shape
        h = jax.nn.silu(q_pool @ W1.T + b1)
        gate = jax.nn.sigmoid(h @ W2.T + b2)[:, None, :]
        levels = int(np.log2(N))
        a = v
        details = []
        for _ in range(levels):
            e, o = (a[:, 0::2], a[:, 1::2])
            details.append((e - o) * INV_SQRT2)
            a = (e + o) * INV_SQRT2
        a = a * gate
        for dc in reversed(details):
            dc = dc * gate
            e = (a + dc) * INV_SQRT2
            o = (a - dc) * INV_SQRT2
            n = e.shape[1]
            a = jnp.stack([e, o], axis=2).reshape(B, 2 * n, d)
        return v + a

    def _L1_cond_ref(x, h0, Wx, Wh, b):
        import jax, jax.numpy as jnp
        import numpy as np
        import math
        N, T, D, H = (128, 256, 512, 512)
        xw = jnp.einsum('ntd,dh->nth', x, Wx) + b

        def step(h_prev, xw_t):
            h_next = jnp.tanh(xw_t + h_prev @ Wh)
            return (h_next, h_next)
        _, hs = jax.lax.scan(step, h0, jnp.swapaxes(xw, 0, 1))
        return jnp.swapaxes(hs, 0, 1)

    def _L2_cond_ref(input_seq, initial_hidden, W_f, b_f, W_i, b_i, W_h, b_h):
        import jax, jax.numpy as jnp
        import numpy as np
        EPS = 1e-08
        forget_gate = jax.nn.sigmoid(jnp.einsum('bsd,hd->bsh', input_seq, W_f) + b_f)
        input_gate = jax.nn.sigmoid(jnp.einsum('bsd,hd->bsh', input_seq, W_i) + b_i)
        gate_sum = forget_gate + input_gate + EPS
        forget_norm = forget_gate / gate_sum
        input_norm = input_gate / gate_sum
        candidate = jnp.einsum('bsd,hd->bsh', input_seq, W_h) + b_h
        new_info = input_norm * candidate
        log_ret = jnp.log(forget_norm + EPS)
        log_cumprod = jnp.cumsum(log_ret, axis=1)
        B, _, H = log_cumprod.shape
        padded = jnp.concatenate([jnp.zeros((B, 1, H), dtype=log_cumprod.dtype), log_cumprod], axis=1)
        scaling = jnp.exp(log_cumprod[:, -1:, :] - padded[:, :-1, :])
        hidden = jnp.cumsum(scaling * new_info, axis=1)
        hidden = hidden + jnp.exp(log_cumprod) * initial_hidden[:, None, :]
        return hidden

    def _L3_cond_ref(x, ada_emb, base_layer, w1, b1, w2, b2, ln_g, ln_b):
        import jax, jax.numpy as jnp
        import numpy as np
        B, T, D = (128, 32, 512)
        ADA, INTER, RANK = (512, 512, 8)
        LN_EPS = 1e-05

        def _layernorm(x, g, b):
            mu = jnp.mean(x, axis=-1, keepdims=True)
            var = jnp.var(x, axis=-1, keepdims=True)
            return (x - mu) * jax.lax.rsqrt(var + LN_EPS) * g + b
        b, t, d = x.shape
        ae = _layernorm(ada_emb, ln_g, ln_b)
        h = jax.nn.gelu(ae @ w1 + b1, approximate=False)
        xw = h @ w2 + b2
        x_a, x_b = jnp.split(xw, 2, axis=-1)
        x_a = x_a.reshape(b, d, RANK)
        x_b = x_b.reshape(b, d, RANK)
        layer = base_layer[None, :, :] + jnp.einsum('bdr,bkr->bdk', x_a, x_b)
        out = jnp.einsum('btc,bco->bto', x, layer)
        return x + out
    x = x + _L0_cond_ref(x, cond_1024, L0_cond_W1, L0_cond_b1, L0_cond_W2, L0_cond_b2)
    x = x + _L1_cond_ref(x, cond_1024, L1_cond_Wx, L1_cond_Wh, L1_cond_b)
    x = x + _L2_cond_ref(x, cond_1024, L2_cond_W_f, L2_cond_b_f, L2_cond_W_i, L2_cond_b_i, L2_cond_W_h, L2_cond_b_h)
    x = x + _L3_cond_ref(x, cond_1024, L3_cond_base_layer, L3_cond_w1, L3_cond_b1, L3_cond_w2, L3_cond_b2, L3_cond_ln_g, L3_cond_ln_b)
    return x

_drawn_inputs = setup_inputs


def setup_inputs(seed=0):
    import zlib

    import numpy as np

    out = dict(_drawn_inputs(seed))
    spreads = {'L0_cond_b1': (0.0, 0.8),
     'L0_cond_b2': (0.0, 0.8),
     'L1_cond_b': (0.0, 0.487),
     'L2_cond_b_f': (0.0, 0.8),
     'L2_cond_b_i': (0.0, 0.8),
     'L2_cond_b_h': (0.0, 0.8),
     'L3_cond_b1': (0.0, 0.507),
     'L3_cond_b2': (0.0, 0.1),
     'L3_cond_ln_g': (1.0, 0.6),
     'L3_cond_ln_b': (0.0, 0.8)}
    factors = {'L2_cond_W_f': 6.925, 'L2_cond_W_i': 7.051, 'L2_cond_W_h': 4.689}
    for name, (base, spread) in spreads.items():
        noise = np.random.default_rng([zlib.crc32(name.encode()), seed]).standard_normal(out[name].shape)
        drawn = base * np.exp(spread * noise) if base else spread * noise
        out[name] = jnp.asarray(drawn.astype(out[name].dtype))
    for name, factor in factors.items():
        out[name] = (out[name] * factor).astype(out[name].dtype)
    return out
```

```python
from contextlib import ExitStack

import concourse.bass as bass
from concourse import mybir

P = 128
B, T, D = 16, 512, 512
C = D // P
TS = 32
NBLK = T // TS
TOK = B * TS
RANK = 8
EPS2 = 1e-8
LN_EPS = 1e-5
PIECES = 8
PW = TOK // PIECES
STAGE = 8
F32, F32R, F16, I32 = mybir.dt.float32, mybir.dt.float32r, mybir.dt.float16, mybir.dt.int32
ALU, ACT, AX = mybir.AluOpType, mybir.ActivationFunctionType, mybir.AxisListType


def mm_groups():
    return [("f", 0), ("i", 0), ("f", 1), ("i", 1), ("c", 0), ("f", 2), ("i", 2), ("c", 1), ("f", 3),
            ("x", 0), ("x", 1), ("i", 3), ("c", 2), ("x", 2), ("x", 3), ("c", 3)]


PE_QUOTA = [0, 0, 0] + [7] * 5 + [4] * 4 + [7] * 19 + [8]
ACT_WORK = {0: [("x2h", 0), ("x2h", 1)], 1: [("x2h", 2), ("x2h", 3)], 5: [("f", 0)], 7: [("i", 0)], 9: [("f", 1)],
            10: [("x1h", 0)], 11: [("x1h", 1)], 12: [("i", 1), ("x1h", 2)], 13: [("x1h", 3)], 14: [("g", 0)],
            15: [("f", 2)], 17: [("i", 2)], 18: [("g", 1)], 21: [("f", 3)], 22: [("x", 0)], 23: [("g", 2)],
            24: [("x", 1)], 26: [("i", 3)], 29: [("x", 2)], 31: [("x", 3), ("g", 3)]}
DVE_EARLY = {9: [("r", 0, 0)], 10: [("r", 0, 2)], 11: [("r", 0, 4)], 12: [("r", 0, 6)],
             14: [("r", 1, 0)], 15: [("r", 1, 1)], 16: [("r", 1, 4)], 17: [("r", 1, 7)],
             19: [("r", 2, 0)], 20: [("r", 2, 1)], 21: [("r", 2, 4)], 22: [("r", 2, 7)],
             27: [("s", 3)], 28: [("r", 3, 0)], 29: [("r", 3, 3)], 30: [("r", 3, 6)]}
DVE_LATE = {8: [("s", 0)], 9: [("x1", 0), ("r", 0, 1)], 10: [("x1", 1), ("r", 0, 3)], 11: [("x1", 2), ("r", 0, 5)],
            12: [("x1", 3), ("r", 0, 7)], 13: [("s", 1)], 14: [("n", 0)], 15: [("r", 1, 2), ("r", 1, 3)],
            16: [("r", 1, 5), ("r", 1, 6)], 18: [("s", 2)], 19: [("n", 1)], 20: [("r", 2, 2), ("r", 2, 3)],
            21: [("r", 2, 5), ("r", 2, 6)], 27: [("n", 2)], 28: [("r", 3, 1), ("r", 3, 2)],
            29: [("r", 3, 4), ("r", 3, 5)], 30: [("r", 3, 7)], 31: [("n", 3)]}


def build(nc, x, cond, W1, b1, W2, b2, Wx, Wh, bx, Wf, bf, Wi, bi, Wc, bc, base, w1, c1, w2, c2, ln_g, ln_b, out):
    keep = ExitStack()
    with keep:
        def sb(name, shape, dt=F32, at=keep):
            return at.enter_context(nc.sbuf_tensor(name, shape, dt))

        ident = sb("ident", [P, P])
        condT = sb("condT", [P, C, B])
        XA = sb("XA", [P, D])
        XB = sb("XB", [P, D])
        rowmask = sb("rowmask", [P, B])
        x2_d, g_d, n_d = (nc.dram_tensor(s, [B, P, C, TS + T], F32, kind="Internal").ap() for s in ("x2_d", "g_d", "n_d"))

        with ExitStack() as mid:
            gate2 = sb("gate2", [P, C, B], at=mid)
            split = {k: (sb(f"{k}_hi", [P, C, D], F32R, mid), sb(f"{k}_lo", [P, C, D], F32R, mid)) for k in "xfic"}
            wh_hi, wh_lo = sb("wh_hi", [P, C, D], F16, mid), sb("wh_lo", [P, C, D], F16, mid)
            whs = sb("whs", [P, 4], at=mid)
            sbx = sb("sbx", [P, C], at=mid)
            bias = {k: sb(f"bias_{k}", [P, C], at=mid) for k in "fic"}
            h0wh = sb("h0wh", [P, C, B], at=mid)
            prologue(nc, locals())
            recurrence(nc, locals())
        tail(nc, locals())


def prologue(nc, v):
    ident, condT, XA, XB, rowmask = v["ident"], v["condT"], v["XA"], v["XB"], v["rowmask"]
    gate2, split, wh_hi, wh_lo, whs, sbx, bias, h0wh = (v[k] for k in "gate2 split wh_hi wh_lo whs sbx bias h0wh".split())
    with ExitStack() as ctx:
        def sb(name, shape, dt=F32):
            return ctx.enter_context(nc.sbuf_tensor(name, shape, dt))

        def ps(name, shape):
            return ctx.enter_context(nc.psum_tensor(name, shape, F32))

        def sem(name):
            return ctx.enter_context(nc.semaphore(name))

        raw = {k: sb(f"raw_{k}", [P, C, D]) for k in ("1", "f", "i", "c")}
        raw["2"] = raw["1"]
        wT1, wT2 = sb("wT1", [P, C, D]), sb("wT2", [P, C, D])
        wh, wx = wT1, wT2
        w1s = raw["1"]
        row = sb("row", [1, 3, D])
        ones = sb("ones", [1, B])
        crow = sb("crow", [B, D])
        ae, t16, aeT, hg = sb("ae", [B, D]), sb("t16", [B, D]), sb("aeT", [P, C, B]), sb("hg", [B, D])
        lng, lnb = sb("lng", [B, D]), sb("lnb", [B, D])
        stat = sb("stat", [B, 4])
        hT, hgT = sb("hT", [P, C, B]), sb("hgT", [P, C, B])
        z16, sg = sb("z16", [B, D]), sb("sg", [B, D])
        lr = sb("lr", [B, 2, RANK, D])
        w2s = sb("w2s", [P, 2, C, D])
        c2s = sb("c2s", [B, 2, D])
        trp = [ps(f"trp{i}", [P, D]) for i in range(2)]
        small = ps("small", [P, C, B])
        zz = ps("zz", [P, D])
        lrp = [ps(f"lrp{i}", [P, D]) for i in range(2)]
        h0p = ps("h0p", [P, C, B])

        (d_cond, d_w1, d_w2, d_fic, d_rows, d_ln, d_wh, d_wx, d_h1, d_bias, d_lr) = (
            sem("p_" + s) for s in "d_cond d_w1 d_w2 d_fic d_rows d_ln d_wh d_wx d_h1 d_bias d_lr".split())
        d_s, d_c2 = [sem(f"p_d_s{i}") for i in range(2)], [sem(f"p_d_c2{i}") for i in range(2)]
        (s_id, s_one, s_ct, s_ctc, s_tr, s_hi, s_lo, s_z, s_v, s_sg, s_hT, s_hTc, s_ae, s_a, s_mx, s_amx, s_wh, s_h0, s_lr,
         s_lrv, s_mask, s_wx, s_sb) = (
            sem("p_" + s) for s in ("s_id s_one s_ct s_ctc s_tr s_hi s_lo s_z s_v s_sg s_hT s_hTc s_ae s_a s_mx s_amx s_wh s_h0 s_lr "
                                    "s_lrv s_mask s_wx s_sb").split())
        NQ = 2 * D * RANK // D

        block = ctx.enter_context(nc.Block())

        @block.sync
        def _(sp):
            sp.dma_start(crow[:], v["cond"]).then_inc(d_cond, 16)
            sp.dma_start(raw["1"][:], v["W1"].rearrange("(c p) d -> p c d", p=P)).then_inc(d_w1, 16)
            for n, k in enumerate(("b1", "b2", "c1")):
                sp.dma_start(row[:, n, :], v[k].rearrange("(a d) -> a d", a=1)).then_inc(d_rows, 16)
            for k, w in (("f", "Wf"), ("i", "Wi"), ("c", "Wc")):
                sp.dma_start(raw[k][:], v[w].rearrange("(c p) d -> p c d", p=P)).then_inc(d_fic, 16)
            sp.dma_start(lng[:], v["ln_g"].rearrange("(a d) -> a d", a=1).to_broadcast([B, D])).then_inc(d_ln, 16)
            sp.dma_start(lnb[:], v["ln_b"].rearrange("(a d) -> a d", a=1).to_broadcast([B, D])).then_inc(d_ln, 16)
            for k, w in (("f", "bf"), ("i", "bi"), ("c", "bc")):
                sp.dma_start(bias[k][:], v[w].rearrange("(c p) -> p c", p=P), allow_slow_non_contiguous=True).then_inc(d_bias, 16)
            sp.dma_start(sbx[:], v["bx"].rearrange("(c p) -> p c", p=P), allow_slow_non_contiguous=True).then_inc(d_bias, 16)
            sp.wait_ge(s_tr, C)
            sp.dma_start(raw["2"][:], v["W2"].rearrange("(c p) d -> p c d", p=P)).then_inc(d_w2, 16)

            def low_rank_piece(q):
                if q >= 2:
                    sp.wait_ge(s_lrv, q - 1)
                sp.dma_start(w2s[:, q % 2], v["w2"][:, q * D:(q + 1) * D].rearrange("(c p) d -> p c d", p=P)).then_inc(d_s[q % 2], 16)
                sp.dma_start(c2s[:, q % 2], v["c2"][q * D:(q + 1) * D].rearrange("(a d) -> a d", a=1).to_broadcast([B, D])).then_inc(d_c2[q % 2], 16)

            low_rank_piece(0)
            low_rank_piece(1)
            sp.wait_ge(s_z, 1)
            sp.dma_start(wh[:], v["Wh"].rearrange("(c p) d -> p c d", p=P)).then_inc(d_wh, 16)
            sp.wait_ge(s_tr, 2 * C)
            sp.dma_start(w1s[:], v["w1"].rearrange("(c p) d -> p c d", p=P)).then_inc(d_h1, 16)
            sp.wait_ge(s_z, 2)
            sp.dma_start(wx[:], v["Wx"].rearrange("(c p) d -> p c d", p=P)).then_inc(d_wx, 16)
            for q in range(2, NQ):
                low_rank_piece(q)
            sp.wait_ge(s_lrv, NQ)
            for half, dst in ((0, XA), (1, XB)):
                for r in range(RANK):
                    sp.dma_start(dst[r * B:(r + 1) * B, :], lr[:, half, r, :]).then_inc(d_lr, 16)
            sp.wait_ge(d_lr, 16 * 2 * RANK)
            sp.wait_ge(d_bias, 64)

        @block.gpsimd
        def _(pool):
            nc.gpsimd.memset(ident[:], 0.0).then_inc(s_id, 1)
            nc.gpsimd.memset(ones[:], 1.0).then_inc(s_one, 1)
            pool.wait_ge(s_id, 1)
            nc.gpsimd.affine_select(out=ident[:], in_=ident[:], compare_op=ALU.not_equal, fill=1.0, base=0,
                                    pattern=[[-1, P]], channel_multiplier=1).then_inc(s_id, 1)
            pool.wait_ge(s_mx, 1)
            nc.gpsimd.partition_all_reduce(whs[:, 1:2], whs[:, 0:1], P, bass.bass_isa.ReduceOp.max).then_inc(s_amx, 1)

        @block.tensor
        def _(pe):
            pe.wait_ge(s_id, 2)
            pe.wait_ge(d_cond, 16)

            def rows_to_cols(src, done):
                for c in range(C):
                    last = nc.tensor.transpose(small[:, c, :], src[:, c * P:(c + 1) * P], ident[0:B, 0:B])
                last.then_inc(done, 1)

            rounds = [0]

            def transpose_weight(k):
                for c in range(C):
                    n = rounds[0]
                    if n >= 2:
                        pe.wait_ge(s_hi, n - 1)
                        if n - 2 >= 2 * C:
                            pe.wait_ge(s_lo, n - 1 - 2 * C)
                    for r in range(C):
                        last = nc.tensor.transpose(trp[n % 2][:, r * P:(r + 1) * P], raw[k][:, r, c * P:(c + 1) * P], ident[:])
                    last.then_inc(s_tr, 1)
                    rounds[0] += 1

            def dense16(lhs, w, n):
                for c in range(C):
                    nc.tensor.matmul(zz[0:B, :], lhs[:, c, :], w[:, c, :], start=(c == 0), stop=False)
                nc.tensor.matmul(zz[0:B, :], ones[:], row[:, n, :], start=False, stop=True).then_inc(s_z, 1)

            rows_to_cols(crow, s_ct)
            pe.wait_ge(d_w1, 16)
            transpose_weight("1")
            pe.wait_ge(s_ctc, 1)
            pe.wait_ge(s_hi, C)
            pe.wait_ge(d_rows, 48)
            pe.wait_ge(s_one, 1)
            dense16(condT, wT1, 0)
            pe.wait_ge(d_w2, 16)
            transpose_weight("2")
            pe.wait_ge(s_v, 1)
            rows_to_cols(hg, s_hT)
            pe.wait_ge(s_hTc, 1)
            pe.wait_ge(s_hi, 2 * C)
            dense16(hT, wT2, 1)
            pe.wait_ge(s_ae, 1)
            rows_to_cols(ae, s_hT)
            pe.wait_ge(s_hTc, 2)
            pe.wait_ge(d_h1, 16)
            pe.wait_ge(s_sg, 2)
            dense16(aeT, w1s, 2)
            pe.wait_ge(d_fic, 48)
            for k in "fic":
                transpose_weight(k)
            rows_to_cols(sg, s_hT)
            pe.wait_ge(s_hTc, 3)
            pe.wait_ge(s_sg, 3)
            rows_to_cols(hg, s_hT)
            pe.wait_ge(s_hTc, 4)
            pe.wait_ge(d_wh, 16)
            for m in range(C):
                for c in range(C):
                    last = nc.tensor.matmul(h0p[:, m, :], wh[:, c, m * P:(m + 1) * P], condT[:, c, :],
                                            start=(c == 0), stop=(c == C - 1))
            last.then_inc(s_h0, 1)
            for q in range(NQ):
                pe.wait_ge(d_s[q % 2], 16 * (q // 2 + 1))
                if q >= 2:
                    pe.wait_ge(s_lrv, q - 1)
                for c in range(C):
                    last = nc.tensor.matmul(lrp[q % 2][0:B, :], hgT[:, c, :], w2s[:, q % 2, c, :],
                                            start=(c == 0), stop=(c == C - 1))
                last.then_inc(s_lr, 1)

        @block.scalar
        def _(act):
            for n in range(2 * C):
                act.wait_ge(s_tr, n + 1)
                nc.scalar.copy((wT1 if n < C else wT2)[:, n % C, :], trp[n % 2][:]).then_inc(s_hi, 1)
                if n == C - 1:
                    act.wait_ge(s_sb, 1)
                    nc.scalar.activation(sg[:], zz[0:B, :], ACT.Sigmoid).then_inc(s_sg, 1)
            act.wait_ge(s_z, 2)
            act.wait_ge(s_v, 1)
            nc.scalar.activation(sg[:], zz[0:B, :], ACT.Sigmoid).then_inc(s_sg, 1)
            act.wait_ge(s_a, 2)
            nc.scalar.activation(t16[:], ae[:], ACT.Square, accum_out=stat[:, 1:2]).then_inc(s_a, 1)
            act.wait_ge(s_a, 4)
            nc.scalar.activation(stat[:, 3:4], stat[:, 2:3], ACT.Sqrt).then_inc(s_a, 1)
            act.wait_ge(s_z, 3)
            act.wait_ge(s_hT, 1)
            nc.scalar.activation(hg[:], zz[0:B, :], ACT.Gelu).then_inc(s_sg, 1)
            for n, k in enumerate("fic"):
                for c in range(C):
                    act.wait_ge(s_tr, 2 * C + n * C + c + 1)
                    nc.scalar.copy(split[k][0][:, c, :], trp[(n * C + c) % 2][:]).then_inc(s_hi, 1)
            act.wait_ge(d_wx, 16)
            nc.scalar.copy(split["x"][0][:], wx[:]).then_inc(s_wx, 1)

        @block.vector
        def _(dve):
            dve.wait_ge(s_ct, 1)
            nc.vector.tensor_copy(condT[:], small[:]).then_inc(s_ctc, 1)
            dve.wait_ge(s_id, 2)
            nc.vector.tensor_reduce(rowmask[:], ident[:].rearrange("p (r b) -> p b r", b=B), axis=AX.X, op=ALU.add).then_inc(s_mask, 1)
            dve.wait_ge(d_cond, 16)
            nc.vector.tensor_reduce(stat[:, 0:1], crow[:], axis=AX.X, op=ALU.add).then_inc(s_a, 1)
            dve.wait_ge(s_a, 1)
            nc.vector.scalar_tensor_tensor(ae[:], stat[:, 0:1].to_broadcast([B, D]), -1.0 / D, crow[:], ALU.mult, ALU.add).then_inc(s_a, 1)
            dve.wait_ge(s_z, 1)
            nc.vector.tensor_copy(z16[:], zz[0:B, :]).then_inc(s_sb, 1)
            dve.wait_ge(s_sg, 1)
            dve.wait_ge(s_sb, 1)
            nc.vector.tensor_tensor(hg[:], z16[:], sg[:], ALU.mult).then_inc(s_v, 1)
            dve.wait_ge(s_hT, 1)
            nc.vector.tensor_copy(hT[:], small[:]).then_inc(s_hTc, 1)
            dve.wait_ge(s_a, 3)
            nc.vector.tensor_scalar(stat[:, 2:3], stat[:, 1:2], 1.0 / D, LN_EPS, ALU.mult, ALU.add).then_inc(s_a, 1)
            dve.wait_ge(s_a, 5)
            nc.vector.reciprocal(stat[:, 0:1], stat[:, 3:4]).then_inc(s_a, 1)
            dve.wait_ge(s_a, 6)
            dve.wait_ge(d_ln, 32)
            nc.vector.scalar_tensor_tensor(t16[:], ae[:], stat[:, 0:1], lng[:], ALU.mult, ALU.mult).then_inc(s_a, 1)
            dve.wait_ge(s_a, 7)
            nc.vector.tensor_tensor(ae[:], t16[:], lnb[:], ALU.add).then_inc(s_ae, 1)
            dve.wait_ge(s_hT, 2)
            nc.vector.tensor_copy(aeT[:], small[:]).then_inc(s_hTc, 1)
            for n, k in enumerate("fic"):
                for c in range(C):
                    dve.wait_ge(s_hi, 2 * C + n * C + c + 1)
                    nc.vector.tensor_tensor(split[k][1][:, c, :], trp[(n * C + c) % 2][:],
                                            split[k][0][:, c, :].bitcast(F32), ALU.subtract).then_inc(s_lo, 1)
            dve.wait_ge(s_hT, 3)
            nc.vector.tensor_scalar(gate2[:], small[:], 2.0, None, ALU.add).then_inc(s_hTc, 1)
            dve.wait_ge(s_hT, 4)
            nc.vector.tensor_copy(hgT[:], small[:]).then_inc(s_hTc, 1)
            dve.wait_ge(d_wh, 16)
            nc.vector.tensor_reduce(whs[:, 0:1], wh[:], axis=AX.XY, op=ALU.max, apply_absolute_value=True).then_inc(s_mx, 1)
            dve.wait_ge(s_amx, 1)
            nc.vector.tensor_scalar(whs[:, 2:3].bitcast(I32), whs[:, 1:2].bitcast(I32), 0x7F800000, None, ALU.bitwise_and).then_inc(s_wh, 1)
            dve.wait_ge(s_wh, 1)
            nc.vector.tensor_scalar(whs[:, 0:1], whs[:, 2:3], 2.0 ** -100, 2.0 ** 120, ALU.max, ALU.min).then_inc(s_wh, 1)
            dve.wait_ge(s_wh, 2)
            nc.vector.tensor_scalar(whs[:, 3:4], whs[:, 0:1], 2.0 ** -14, None, ALU.mult).then_inc(s_wh, 1)
            nc.vector.tensor_scalar(whs[:, 1:2].bitcast(I32), whs[:, 0:1].bitcast(I32), -1, 254 << 23, ALU.mult, ALU.add).then_inc(s_wh, 1)
            dve.wait_ge(s_wh, 4)
            nc.vector.tensor_scalar(whs[:, 2:3], whs[:, 1:2], 2.0 ** 14, None, ALU.mult).then_inc(s_wh, 1)
            dve.wait_ge(s_wh, 5)
            nc.vector.tensor_scalar(wh_hi[:], wh[:], whs[:, 2:3], None, ALU.mult).then_inc(s_wh, 1)
            dve.wait_ge(s_wh, 6)
            for c in range(C):
                nc.vector.scalar_tensor_tensor(wh_lo[:, c, :], wh[:, c, :], whs[:, 2:3], wh_hi[:, c, :], ALU.mult, ALU.subtract).then_inc(s_wh, 1)
            dve.wait_ge(s_h0, 1)
            nc.vector.tensor_scalar(h0wh[:], h0p[:], whs[:, 2:3], None, ALU.mult).then_inc(s_wh, 1)
            dve.wait_ge(d_bias, 64)
            nc.vector.tensor_scalar(sbx[:], sbx[:], whs[:, 2:3], None, ALU.mult).then_inc(s_wh, 1)
            dve.wait_ge(s_wx, 1)
            for c in range(C):
                nc.vector.tensor_tensor(split["x"][1][:, c, :], wx[:, c, :], split["x"][0][:, c, :].bitcast(F32), ALU.subtract).then_inc(s_wx, 1)
            for q in range(2 * D * RANK // D):
                half, d0 = q // RANK, q % RANK * (D // RANK)
                dve.wait_ge(s_lr, q + 1)
                dve.wait_ge(d_c2[q % 2], 16 * (q // 2 + 1))
                nc.vector.tensor_tensor(lr[:, half, :, d0:d0 + D // RANK], lrp[q % 2][0:B, :].rearrange("p (d r) -> p r d", r=RANK),
                                        c2s[:, q % 2, :].rearrange("p (d r) -> p r d", r=RANK), ALU.add).then_inc(s_lrv, 1)


def recurrence(nc, v):
    x, ident = v["x"], v["ident"]
    gate2, split, wh_hi, wh_lo, whs, sbx, bias, h0wh = (v[k] for k in "gate2 split wh_hi wh_lo whs sbx bias h0wh".split())
    x2_d, g_d, n_d = v["x2_d"], v["g_d"], v["n_d"]
    GROUPS = mm_groups()
    with ExitStack() as ctx:
        def sb(name, shape, dt=F32):
            return ctx.enter_context(nc.sbuf_tensor(name, shape, dt))

        def ps(name, shape):
            return ctx.enter_context(nc.psum_tensor(name, shape, F32))

        def sem(name):
            return ctx.enter_context(nc.semaphore(name))

        xnat = sb("xnat", [P, C, D])
        xt = [sb(f"xt{q}", [P, C, TOK]) for q in range(2)]
        x1hi, x1lo = sb("x1hi", [P, C, TOK], F32R), sb("x1lo", [P, C, TOK], F32R)
        x2hi, x2lo = sb("x2hi", [P, C, TOK], F32R), sb("x2lo", [P, C, TOK], F32R)
        xw = [sb(f"xw{q}", [P, TS, C, B]) for q in range(2)]
        hbuf = sb("hbuf", [P, TS, C, B])
        hs = sb("hs", [P, C, 2, B], F16)
        pre0, pre = sb("pre0", [P, C, B]), sb("pre", [P, C, B])
        fbuf, ibuf, rbuf = (sb(s, [P, 2, TOK]) for s in ("fbuf", "ibuf", "rbuf"))
        gst, nst = sb("gst", [P, C, TOK]), sb("nst", [P, C, TOK])
        bank = [ps(f"bank{i}", [P, TOK]) for i in range(4)]
        trb = [ps(f"trb{i}", [P, TOK]) for i in range(2)]
        rec = ps("rec", [P, C, 2, B])

        (d_x, d_x2, d_g, d_n) = (sem("r_" + s) for s in ("d_x", "d_x2", "d_g", "d_n"))
        (s_tr, s_x1, s_x1h, s_x1l, s_xp, s_xw, s_rec, s_pre0, s_pre, s_h, s_hs, s_x2, s_x2h, s_x2l, s_f, s_i, s_c, s_fs, s_is,
         s_gs, s_r, s_fr, s_in, s_g, s_n) = (
            sem("r_" + s) for s in ("s_tr s_x1 s_x1h s_x1l s_xp s_xw s_rec s_pre0 s_pre s_h s_hs s_x2 s_x2h s_x2l s_f s_i s_c s_fs s_is "
                                    "s_gs s_r s_fr s_in s_g s_n").split())
        s_h0 = sem("r_s_h0")

        def cnt(j, per, pos):
            i, q = j
            return i * (2 * per) + (q * per + pos)

        def nxt(j):
            return (j[0], 1) if j[1] == 0 else (j[0] + 1, 0)

        def bank_free(eng, j, n, groups=GROUPS):
            kind, m = groups[n - 4] if n >= 4 else GROUPS[12 + n]
            off = 0 if n >= 4 else -4
            if kind == "f":
                eng.wait_ge(s_fs, cnt(j, 4, m + 1 + off))
            elif kind == "i":
                eng.wait_ge(s_is, cnt(j, 4, m + 1 + off))
            elif kind == "c":
                eng.wait_ge(s_n, cnt(j, 4, 4 + m + 1 + off))
            else:
                eng.wait_ge(s_xw, cnt(j, 4, 4 + m + 1 + off))

        def group_mms(kind, m):
            hi, lo = split[kind]
            ahi, alo = (x1hi, x1lo) if kind == "x" else (x2hi, x2lo)
            return [(w[:, k, m * P:(m + 1) * P], a[:, k, :]) for k in range(C) for w, a in ((hi, ahi), (lo, ahi), (hi, alo))]

        block = ctx.enter_context(nc.Block())

        @block.sync
        def _(sp):
            def load_x(t0):
                for b in range(B):
                    sp.dma_start(xnat[b % 4 * TS:(b % 4 + 1) * TS, b // 4, :], x[b, bass.ds(t0, TS), :]).then_inc(d_x, 16)

            def spill(dst, src, t0, m, done):
                sp.dma_start(dst[:, :, m, bass.ds(t0, TS)].rearrange("b p t -> p b t"),
                             src.rearrange("p (b t) -> p b t", t=TS)).then_inc(done, 16)

            def spill_x2(j, q, t0):
                sp.wait_ge(s_x2, cnt(j, 4, 4))
                for m in range(C):
                    spill(x2_d, xt[1 - q][:, m, :], t0, m, d_x2)

            def spill_gn(j, t0, m):
                sp.wait_ge(s_g, cnt(j, 4, m + 1))
                spill(g_d, gst[:, m, :], t0, m, d_g)
                sp.wait_ge(s_n, cnt(j, 4, 4 + m + 1))
                spill(n_d, nst[:, m, :], t0, m, d_n)

            def body(i, q, ahead):
                j = (i, q)
                t0 = i * (2 * TS) + q * TS
                spill_x2(j, q, t0)
                sp.wait_ge(s_tr, cnt(nxt(j), 4, 4))
                load_x(ahead)
                for m in range(C):
                    spill_gn(j, t0, m)

            load_x(0)
            sp.wait_ge(s_tr, 4)
            load_x(TS)
            with sp.Fori(0, NBLK // 2 - 1) as i:
                for q in range(2):
                    body(i, q, i * (2 * TS) + (q + 2) * TS)
            for q in range(2):
                body(NBLK // 2 - 1, q, q * TS)
            spill_x2((NBLK // 2, 0), 0, T)
            for m in range(C):
                spill_gn((NBLK // 2, 0), T, m)
            sp.wait_ge(d_x2, 64 * (NBLK + 1))
            sp.wait_ge(d_g, 64 * (NBLK + 2))
            sp.wait_ge(d_n, 64 * (NBLK + 2))
            sp.wait_ge(d_x, 256 * (NBLK + 2))

        @block.tensor
        def _(pe):
            def transposes(p, m, first=False):
                if m == 0:
                    pe.wait_ge(d_x, cnt(p, 256, 256))
                if m >= 2 or not first:
                    pe.wait_ge(s_x1, cnt(p, 4, m - 1))
                for a in range(C):
                    last = nc.tensor.transpose(trb[m % 2][:, a * P:(a + 1) * P], xnat[:, a, m * P:(m + 1) * P], ident[:])
                last.then_inc(s_tr, 1)

            def step(j, t):
                pe.wait_ge(s_hs, cnt(j, TS, t + 1))
                for k in range(C):
                    for m in range(C):
                        for w in (wh_hi, wh_lo):
                            last = nc.tensor.matmul(rec[:, m].rearrange("p a b -> p (a b)"), w[:, k, m * P:(m + 1) * P],
                                                    hs[:, k].rearrange("p a b -> p (a b)"),
                                                    start=(k == 0 and m == 0 and w is wh_hi), stop=(k == C - 1),
                                                    skip_group_check=True)
                last.then_inc(s_rec, 1)

            def group_part(j, p, n, groups, lo, hi):
                kind, m = groups[n]
                if lo == 0:
                    bank_free(pe, j, n, groups)
                    if kind == "x":
                        pe.wait_ge(s_x1h, cnt(p, 4, 4))
                        pe.wait_ge(s_x1l, cnt(p, 4, 4))
                    else:
                        pe.wait_ge(s_x2h, cnt(j, 4, 4))
                        pe.wait_ge(s_x2l, cnt(j, 4, 4))
                mms = group_mms(kind, m)
                for e in range(lo, hi):
                    last = nc.tensor.matmul(bank[n % 4][:], mms[e][0], mms[e][1], start=(e == 0), stop=(e == len(mms) - 1))
                if hi == len(mms):
                    last.then_inc({"x": s_xp, "f": s_f, "i": s_i, "c": s_c}[kind], 1)

            GM = 3 * C
            for m in range(C):
                transposes((0, 0), m, True)
            for m in range(C):
                if m == 0:
                    pe.wait_ge(s_x1h, 4)
                    pe.wait_ge(s_x1l, 4)
                mms = group_mms("x", m)
                for e in range(GM):
                    last = nc.tensor.matmul(bank[m][:], mms[e][0], mms[e][1], start=(e == 0), stop=(e == GM - 1))
                last.then_inc(s_xp, 1)
            with pe.Fori(0, NBLK // 2) as i:
                for q in range(2):
                    j = (i, q)
                    at = 0
                    for t in range(TS):
                        step(j, t)
                        if 8 <= t < 8 + C:
                            transposes(nxt(j), t - 8)
                        end = at + PE_QUOTA[t]
                        while at < end:
                            n, lo = at // GM, at % GM
                            hi = min(GM, lo + end - at)
                            group_part(j, nxt(j), n, GROUPS, lo, hi)
                            at += hi - lo
            last_groups = [g for g in GROUPS if g[0] != "x"]
            for n in range(len(last_groups)):
                group_part((NBLK // 2, 0), None, n, last_groups, 0, GM)

        @block.scalar
        def _(act):
            unscale = act.alloc_register("unscale")
            act.reg_load(unscale, whs[0:1, 3:4].bitcast(I32))

            def tanh(j, t, hb):
                act.wait_ge(s_pre, cnt(j, TS, t + 1))
                if t % STAGE == 0:
                    act.wait_ge(s_x2, cnt(j, 4, t // STAGE + 1))
                nc.scalar.activation(hs[:, :, 0, :], pre[:], ACT.Tanh, scale=unscale).then_inc(s_h, 1)
                nc.scalar.activation(hb, pre[:], ACT.Tanh, scale=unscale).then_inc(s_h, 1)

            def x1_high(p, q, m):
                act.wait_ge(s_x1, cnt(p, 4, m + 1))
                act.wait_ge(s_xp, cnt(p, 4, 0))
                nc.scalar.copy(x1hi[:, m, :], xt[q][:, m, :]).then_inc(s_x1h, 1)

            def x2_high(j, q, m):
                act.wait_ge(s_x2, cnt(j, 4, 4))
                act.wait_ge(s_n, cnt(j, 4, 4))
                nc.scalar.copy(x2hi[:, m, :], xt[1 - q][:, m, :]).then_inc(s_x2h, 1)

            def input_products(p, q, m, src):
                act.wait_ge(s_xp, cnt(p, 4, m + 1))
                nc.scalar.activation(xw[q][:, :, m, :].rearrange("p t b -> p b t"), src[:].rearrange("p (b t) -> p b t", t=TS),
                                     ACT.Identity, bias=sbx[:, m:m + 1], scale=whs[:, 2:3]).then_inc(s_xw, 1)

            def gate(j, n, groups):
                kind, m = groups[n]
                made, done, buf = (s_f, s_fs, fbuf) if kind == "f" else (s_i, s_is, ibuf)
                act.wait_ge(made, cnt(j, 4, m + 1))
                if kind == "f" and m < 2:
                    act.wait_ge(d_g, cnt(j, 64, 64))
                elif kind == "f":
                    act.wait_ge(s_g, cnt(j, 4, m - 1))
                else:
                    act.wait_ge(s_n, cnt(j, 4, 4 + m - 1))
                nc.scalar.activation(buf[:, m % 2, :], bank[n % 4][:], ACT.Sigmoid, bias=bias[kind][:, m:m + 1]).then_inc(done, 1)

            def forget_share(j, m):
                act.wait_ge(s_fr, cnt(j, 4, m + 1))
                act.wait_ge(d_g, cnt(j, 64, 64 + 16 * m))
                nc.scalar.activation(gst[:, m, :], fbuf[:, m % 2, :], ACT.Copy, bias=EPS2).then_inc(s_g, 1)

            def work(j, item):
                kind, m = item
                if kind == "x2h":
                    x2_high(j, j[1], m)
                elif kind == "x1h":
                    x1_high(nxt(j), 1 - j[1], m)
                elif kind == "x":
                    input_products(nxt(j), 1 - j[1], m, bank[GROUPS.index(item) % 4])
                elif kind == "g":
                    forget_share(j, m)
                else:
                    gate(j, GROUPS.index(item), GROUPS)

            for m in range(C):
                x1_high((0, 0), 0, m)
            for m in range(C):
                input_products((0, 0), 0, m, bank[m])
            with act.Fori(0, NBLK // 2) as i:
                for q in range(2):
                    for t in range(TS):
                        tanh((i, q), t, hbuf[:, t])
                        for item in ACT_WORK.get(t, []):
                            work((i, q), item)
            end = (NBLK // 2, 0)
            last_groups = [g for g in GROUPS if g[0] != "x"]
            for m in range(C):
                x2_high(end, 0, m)
            for kind, m in last_groups:
                if kind != "c":
                    gate(end, last_groups.index((kind, m)), last_groups)
                else:
                    forget_share(end, m)

        @block.gpsimd
        def _(pool):
            def x1_low(p, q, m):
                pool.wait_ge(s_x1h, cnt(p, 4, m + 1))
                nc.gpsimd.tensor_tensor(x1lo[:, m, :], xt[q][:, m, :], x1hi[:, m, :].bitcast(F32), ALU.subtract).then_inc(s_x1l, 1)

            def x2_low(j, q, m):
                pool.wait_ge(s_x2h, cnt(j, 4, m + 1))
                nc.gpsimd.tensor_tensor(x2lo[:, m, :], xt[1 - q][:, m, :], x2hi[:, m, :].bitcast(F32), ALU.subtract).then_inc(s_x2l, 1)

            def add_h(j, q, s):
                pool.wait_ge(s_h, cnt(j, 2 * TS, 2 * STAGE * (s + 1)))
                if s == 0:
                    pool.wait_ge(s_x1l, cnt(j, 4, 4))
                xs = xt[q][:].rearrange("p c (b t) -> p c b t", t=TS)[:, :, :, s * STAGE:(s + 1) * STAGE]
                nc.gpsimd.tensor_tensor(xs, xs, hbuf[:, s * STAGE:(s + 1) * STAGE].rearrange("p t c b -> p c b t"), ALU.add).then_inc(s_x2, 1)

            def shares(j, m):
                pool.wait_ge(s_r, cnt(j, 4 * PIECES, PIECES * (m + 1)))
                nc.gpsimd.tensor_tensor(fbuf[:, m % 2, :], fbuf[:, m % 2, :], rbuf[:, m % 2, :], ALU.mult).then_inc(s_fr, 1)
                nc.gpsimd.tensor_tensor(ibuf[:, m % 2, :], ibuf[:, m % 2, :], rbuf[:, m % 2, :], ALU.mult).then_inc(s_in, 1)

            for m in range(C):
                nc.gpsimd.memset(xt[1][:, m, :], 0.0).then_inc(s_x2, 1)
            for m in range(C):
                x1_low((0, 0), 0, m)
            with pool.Fori(0, NBLK // 2) as i:
                for q in range(2):
                    j = (i, q)
                    for m in range(C):
                        x2_low(j, q, m)
                    add_h(j, q, 0)
                    for m in range(C):
                        x1_low(nxt(j), 1 - q, m)
                    shares(j, 0)
                    add_h(j, q, 1)
                    shares(j, 1)
                    shares(j, 2)
                    add_h(j, q, 2)
                    shares(j, 3)
                    add_h(j, q, 3)
            end = (NBLK // 2, 0)
            for m in range(C):
                x2_low(end, 0, m)
            for m in range(C):
                shares(end, m)

        @block.vector
        def _(dve):
            def x1_gated(p, q, m, j=None):
                dve.wait_ge(s_tr, cnt(p, 4, m + 1))
                if j is not None and m == 0:
                    dve.wait_ge(s_x2h, cnt(j, 4, 4))
                    dve.wait_ge(s_x2l, cnt(j, 4, 4))
                    dve.wait_ge(d_x2, cnt(j, 64, 64))
                nc.vector.tensor_tensor(xt[q][:, m, :].rearrange("p (b t) -> p b t", t=TS), trb[m % 2][:].rearrange("p (b t) -> p b t", t=TS),
                                        gate2[:, m, :].unsqueeze(2).to_broadcast([P, B, TS]), ALU.mult).then_inc(s_x1, 1)

            def gate_sum(j, m):
                dve.wait_ge(s_fs, cnt(j, 4, m + 1))
                dve.wait_ge(s_is, cnt(j, 4, m + 1))
                if m < 2:
                    dve.wait_ge(s_n, cnt(j, 4, 4))
                else:
                    dve.wait_ge(s_in, cnt(j, 4, m - 1))
                nc.vector.scalar_tensor_tensor(rbuf[:, m % 2, :], fbuf[:, m % 2, :], EPS2, ibuf[:, m % 2, :], ALU.add, ALU.add).then_inc(s_gs, 1)

            def recip(j, m, e):
                if e == 0:
                    dve.wait_ge(s_gs, cnt(j, 4, m + 1))
                piece = rbuf[:, m % 2, e * PW:(e + 1) * PW]
                nc.vector.reciprocal(piece, piece).then_inc(s_r, 1)

            def new_info(j, n, groups):
                m = groups[n][1]
                dve.wait_ge(s_c, cnt(j, 4, m + 1))
                dve.wait_ge(s_in, cnt(j, 4, m + 1))
                dve.wait_ge(d_n, cnt(j, 64, 64 + 16 * m))
                nc.vector.scalar_tensor_tensor(nst[:, m, :], bank[n % 4][:], bias["c"][:, m:m + 1], ibuf[:, m % 2, :],
                                               ALU.add, ALU.mult).then_inc(s_n, 1)

            def work(j, item):
                if item[0] == "x1":
                    x1_gated(nxt(j), 1 - j[1], item[1], j)
                elif item[0] == "s":
                    gate_sum(j, item[1])
                elif item[0] == "r":
                    recip(j, item[1], item[2])
                else:
                    new_info(j, GROUPS.index(("c", item[1])), GROUPS)

            nc.vector.memset(hs[:], 0.0).then_inc(s_hs, 1)
            nc.vector.memset(pre[:, 0, :], 0.0).then_inc(s_n, 4)
            nc.vector.memset(pre[:, 1, :], 0.0).then_inc(d_g, 64)
            nc.vector.memset(pre[:, 2, :], 0.0).then_inc(d_n, 64)
            for m in range(C):
                x1_gated((0, 0), 0, m)
            dve.wait_ge(s_xw, 4)
            nc.vector.tensor_tensor(xw[0][:, 0], xw[0][:, 0], h0wh[:], ALU.add).then_inc(s_h0, 1)
            dve.wait_ge(s_h0, 1)
            with dve.Fori(0, NBLK // 2) as i:
                for q in range(2):
                    j = (i, q)
                    for t in range(TS):
                        if t == 0:
                            dve.wait_ge(s_xw, cnt(j, 4, 4))
                        dve.wait_ge(s_rec, cnt(j, TS, t + 1))
                        nc.vector.tensor_tensor(pre0[:], rec[:, :, 0, :], xw[q][:, t], ALU.add).then_inc(s_pre0, 1)
                        dve.wait_ge(s_pre0, cnt(j, TS, t + 1))
                        nc.vector.tensor_tensor(pre[:], rec[:, :, 1, :], pre0[:], ALU.add).then_inc(s_pre, 1)
                        for item in DVE_EARLY.get(t, []):
                            work(j, item)
                        dve.wait_ge(s_h, cnt(j, 2 * TS, 2 * t + 2))
                        nc.vector.tensor_tensor(hs[:, :, 1, :], hbuf[:, t], hs[:, :, 0, :], ALU.subtract).then_inc(s_hs, 1)
                        for item in DVE_LATE.get(t, []):
                            work(j, item)
            end = (NBLK // 2, 0)
            last_groups = [g for g in GROUPS if g[0] != "x"]
            for m in range(C):
                gate_sum(end, m)
                for e in range(PIECES):
                    recip(end, m, e)
                new_info(end, last_groups.index(("c", m)), last_groups)


def tail(nc, v):
    ident, condT, XA, XB, rowmask, out, base = (v[k] for k in "ident condT XA XB rowmask out base".split())
    x2_d, g_d, n_d = v["x2_d"], v["g_d"], v["n_d"]
    with ExitStack() as ctx:
        def sb(name, shape, dt=F32):
            return ctx.enter_context(nc.sbuf_tensor(name, shape, dt))

        def ps(name, shape):
            return ctx.enter_context(nc.psum_tensor(name, shape, F32))

        def sem(name):
            return ctx.enter_context(nc.semaphore(name))

        base2 = sb("base2", [P, C, D])
        one, zero = sb("one", [P, T]), sb("zero", [P, T])
        xin = [sb(f"xin{q}", [P, C, T]) for q in range(2)]
        gin = [sb(f"gin{q}", [P, C, T]) for q in range(2)]
        nin = [sb(f"nin{q}", [P, C, T]) for q in range(2)]
        Sb, Pb, Hb = (sb(s, [P, C, T]) for s in ("Sb", "Pb", "Hb"))
        x3hi = [sb(f"x3hi{q}", [P, C, T], F32R) for q in range(2)]
        x3lo = [sb(f"x3lo{q}", [P, C, T], F32R) for q in range(2)]
        lay = sb("lay", [P, C, D])
        layhi = [sb(f"layhi{q}", [P, C, D], F32R) for q in range(2)]
        laylo = [sb(f"laylo{q}", [P, C, D], F32R) for q in range(2)]
        xam = [sb(f"xam{q}", [P, D]) for q in range(2)]
        oout = sb("oout", [P, 4, D])
        layp = [ps(f"layp{i}", [P, D]) for i in range(4)]
        outp = [ps(f"outp{i}", [P, D]) for i in range(4)]
        d_base = sem("t_d_base")
        d_in = [sem(f"t_d_in{q}") for q in range(2)]
        d_out = [sem(f"t_d_out{q}") for q in range(4)]
        (s_b2, s_P, s_S, s_u, s_xp, s_H, s_x3, s_x3h, s_x3l, s_xam, s_lp, s_lay, s_lh, s_ll, s_op, s_o) = (
            sem("t_" + s) for s in "s_b2 s_P s_S s_u s_xp s_H s_x3 s_x3h s_x3l s_xam s_lp s_lay s_lh s_ll s_op s_o".split())
        NT = T // P

        def cnt(b, per, pos):
            i, q = b
            return i * (2 * per) + (q * per + pos)

        block = ctx.enter_context(nc.Block())

        @block.sync
        def _(sp):
            sp.dma_start(base2[:], base.rearrange("(c p) d -> p c d", p=P)).then_inc(d_base, 16)

            def load(q, b):
                for dst, src in ((gin, g_d), (nin, n_d), (xin, x2_d)):
                    sp.dma_start(dst[q][:], src[bass.ds(b, 1), :, :, TS:TS + T].rearrange("a p c t -> (a p) c t")).then_inc(d_in[q], 16)

            def store(i, q):
                for t in range(NT):
                    sp.wait_ge(s_o, cnt((i, q), NT, NT + t + 1))
                    sp.dma_start(out[bass.ds(i * 2 + q, 1), t * P:(t + 1) * P, :].rearrange("a p d -> (a p) d"), oout[:, t, :]).then_inc(d_out[t], 16)

            load(0, 0)
            load(1, 1)
            with sp.Fori(0, B // 2 - 1) as i:
                for q in range(2):
                    sp.wait_ge(s_x3l, cnt((i, q), 4, 4))
                    load(q, i * 2 + (q + 2))
                    store(i, q)
            for q in range(2):
                store(B // 2 - 1, q)
            for t in range(NT):
                sp.wait_ge(d_out[t], 16 * (B + 1))

        @block.vector
        def _(dve):
            nc.vector.memset(one[:], 1.0).then_inc(s_o, NT)
            for t in range(NT):
                nc.vector.memset(zero[:, t * P:(t + 1) * P], 0.0).then_inc(d_out[t], 16)
            dve.wait_ge(d_base, 16)
            for m in range(C):
                nc.vector.scalar_tensor_tensor(base2[:, m, m * P:(m + 1) * P], ident[:], 2.0, base2[:, m, m * P:(m + 1) * P],
                                               ALU.mult, ALU.add).then_inc(s_b2, 1)
            dve.wait_ge(s_b2, 4)
            dve.wait_ge(s_o, NT)
            for t in range(NT):
                dve.wait_ge(d_out[t], 16)
            with dve.Fori(0, B // 2) as i:
                for q in range(2):
                    b = (i, q)
                    dve.wait_ge(d_in[q], i * 48 + 48)
                    for m in range(C):
                        nc.vector.tensor_tensor_scan(Sb[:, m, ::-1], gin[q][:, m, ::-1], zero[:], 1.0, ALU.mult, ALU.add).then_inc(s_S, 1)
                        nc.vector.tensor_tensor_scan(Pb[:, m, :], gin[q][:, m, :], zero[:], condT[:, m, bass.ds(i * 2 + q, 1)],
                                                     ALU.mult, ALU.add).then_inc(s_P, 1)
                        dve.wait_ge(s_lp, cnt(b, 4, m + 1))
                        nc.vector.tensor_tensor(lay[:, m, :], layp[m][:], base2[:, m, :], ALU.add).then_inc(s_lay, 1)
                        dve.wait_ge(s_lh, cnt(b, 4, m + 1))
                        nc.vector.tensor_tensor(laylo[q][:, m, :], lay[:, m, :], layhi[q][:, m, :].bitcast(F32), ALU.subtract).then_inc(s_ll, 1)
                    for m in range(C):
                        dve.wait_ge(s_u, cnt(b, 4, m + 1))
                        nc.vector.tensor_tensor_scan(Hb[:, m, :], one[:], nin[q][:, m, :], 0.0, ALU.mult, ALU.add).then_inc(s_H, 1)
                        dve.wait_ge(s_xp, cnt(b, 4, m + 1))
                        dve.wait_ge(s_H, cnt(b, 4, m + 1))
                        nc.vector.tensor_tensor(xin[q][:, m, :], xin[q][:, m, :], Hb[:, m, :], ALU.add).then_inc(s_x3, 1)

        @block.gpsimd
        def _(pool):
            with pool.Fori(0, B // 2) as i:
                for q in range(2):
                    b = (i, q)
                    for m in range(C):
                        pool.wait_ge(s_S, cnt(b, 4, m + 1))
                        nc.gpsimd.tensor_tensor(nin[q][:, m, :], nin[q][:, m, :], Sb[:, m, :], ALU.mult).then_inc(s_u, 1)
                        pool.wait_ge(s_P, cnt(b, 4, m + 1))
                        nc.gpsimd.tensor_tensor(xin[q][:, m, :], xin[q][:, m, :], Pb[:, m, :], ALU.add).then_inc(s_xp, 1)
                    for m in range(C):
                        pool.wait_ge(s_x3h, cnt(b, 4, m + 1))
                        nc.gpsimd.tensor_tensor(x3lo[q][:, m, :], xin[q][:, m, :], x3hi[q][:, m, :].bitcast(F32), ALU.subtract).then_inc(s_x3l, 1)

        @block.scalar
        def _(act):
            def mask_rows(i, q):
                nc.scalar.activation(xam[q][:], XA[:], ACT.Copy, scale=rowmask[:, bass.ds(i * 2 + q, 1)]).then_inc(s_xam, 1)

            def put_out(i, q, t):
                act.wait_ge(s_op, cnt((i, q), NT, t + 1))
                act.wait_ge(d_out[t], i * 32 + (q * 16 + 16))
                nc.scalar.copy(oout[:, t, :], outp[t][:]).then_inc(s_o, 1)

            with act.Fori(0, B // 2) as i:
                for q in range(2):
                    b = (i, q)
                    mask_rows(i, q)
                    for m in range(C):
                        act.wait_ge(s_lay, cnt(b, 4, m + 1))
                        nc.scalar.copy(layhi[q][:, m, :], lay[:, m, :]).then_inc(s_lh, 1)
                    for m in range(C):
                        act.wait_ge(s_x3, cnt(b, 4, m + 1))
                        nc.scalar.copy(x3hi[q][:, m, :], xin[q][:, m, :]).then_inc(s_x3h, 1)
                    for t in range(NT):
                        put_out(i, q, t)

        @block.tensor
        def _(pe):
            with pe.Fori(0, B // 2) as i:
                for q in range(2):
                    b = (i, q)
                    pe.wait_ge(s_xam, cnt(b, 1, 1))
                    for m in range(C):
                        nc.tensor.matmul(layp[m][:], xam[q][:, m * P:(m + 1) * P], XB[:], start=True, stop=True).then_inc(s_lp, 1)
                    pe.wait_ge(s_lh, cnt(b, 4, 4))
                    pe.wait_ge(s_ll, cnt(b, 4, 4))
                    pe.wait_ge(s_x3h, cnt(b, 4, 4))
                    pe.wait_ge(s_x3l, cnt(b, 4, 4))
                    for t in range(NT):
                        pe.wait_ge(s_o, cnt(b, NT, t + 1))
                        tok = slice(t * P, (t + 1) * P)
                        for m in range(C):
                            for e, (a, w) in enumerate(((x3hi, layhi), (x3lo, layhi), (x3hi, laylo))):
                                last = nc.tensor.matmul(outp[t][:], a[q][:, m, tok], w[q][:, m, :],
                                                        start=(m == 0 and e == 0), stop=(m == C - 1 and e == 2))
                        last.then_inc(s_op, 1)


_INS = ['x', 'cond_1024', 'L0_cond_W1', 'L0_cond_b1', 'L0_cond_W2', 'L0_cond_b2', 'L1_cond_Wx', 'L1_cond_Wh', 'L1_cond_b',
        'L2_cond_W_f', 'L2_cond_b_f', 'L2_cond_W_i', 'L2_cond_b_i', 'L2_cond_W_h', 'L2_cond_b_h', 'L3_cond_base_layer',
        'L3_cond_w1', 'L3_cond_b1', 'L3_cond_w2', 'L3_cond_b2', 'L3_cond_ln_g', 'L3_cond_ln_b']


def kernel(**inputs):
    import numpy as _np
    import concourse.bacc as _bacc
    from concourse import mybir as _mybir
    from concourse.bass_utils import run_bass_kernel_spmd as _run

    nc = _bacc.Bacc("TRN2", target_bir_lowering=False, num_devices=1)
    arrays, args = {}, []
    for name in _INS:
        a = _np.ascontiguousarray(inputs[name])
        arrays[f"in_{name}"] = a
        args.append(nc.dram_tensor(f"in_{name}", a.shape, _mybir.dt.from_np(a.dtype), kind="ExternalInput").ap())
    args.append(nc.dram_tensor("out_0", (B, T, D), F32, kind="ExternalOutput").ap())
    build(nc, *args)
    r = _run(nc, [arrays], core_ids=[0])
    return r.results[0]["out_0"]
```

```python
from contextlib import ExitStack

import concourse.bass as bass
from concourse import mybir

P = 128
B, T, D = 16, 512, 512
C = D // P
TS = 32
NBLK = T // TS
TOK = B * TS
RANK = 8
EPS2 = 1e-8
LN_EPS = 1e-5
PIECES = 8
PW = TOK // PIECES
STAGE = 8
F32, F32R, F16, I32 = mybir.dt.float32, mybir.dt.float32r, mybir.dt.float16, mybir.dt.int32
ALU, ACT, AX = mybir.AluOpType, mybir.ActivationFunctionType, mybir.AxisListType


def mm_groups():
    return [("f", 0), ("i", 0), ("f", 1), ("i", 1), ("c", 0), ("f", 2), ("i", 2), ("c", 1), ("f", 3),
            ("x", 0), ("x", 1), ("i", 3), ("c", 2), ("x", 2), ("x", 3), ("c", 3)]


PE_QUOTA = [0, 0, 0] + [7] * 5 + [4] * 4 + [7] * 19 + [8]
ACT_WORK = {0: [("x2h", 0), ("x2h", 1)], 1: [("x2h", 2), ("x2h", 3)], 5: [("f", 0)], 7: [("i", 0)], 9: [("f", 1)],
            10: [("x1h", 0)], 11: [("x1h", 1)], 12: [("i", 1), ("x1h", 2)], 13: [("x1h", 3)], 14: [("g", 0)],
            15: [("f", 2)], 17: [("i", 2)], 18: [("g", 1)], 21: [("f", 3)], 22: [("x", 0)], 23: [("g", 2)],
            24: [("x", 1)], 26: [("i", 3)], 29: [("x", 2)], 31: [("x", 3), ("g", 3)]}
DVE_EARLY = {9: [("r", 0, 0)], 10: [("r", 0, 2)], 11: [("r", 0, 4)], 12: [("r", 0, 6)],
             14: [("r", 1, 0)], 15: [("r", 1, 1)], 16: [("r", 1, 4)], 17: [("r", 1, 7)],
             19: [("r", 2, 0)], 20: [("r", 2, 1)], 21: [("r", 2, 4)], 22: [("r", 2, 7)],
             27: [("s", 3)], 28: [("r", 3, 0)], 29: [("r", 3, 3)], 30: [("r", 3, 6)]}
DVE_LATE = {8: [("s", 0)], 9: [("x1", 0), ("r", 0, 1)], 10: [("x1", 1), ("r", 0, 3)], 11: [("x1", 2), ("r", 0, 5)],
            12: [("x1", 3), ("r", 0, 7)], 13: [("s", 1)], 14: [("n", 0)], 15: [("r", 1, 2), ("r", 1, 3)],
            16: [("r", 1, 5), ("r", 1, 6)], 18: [("s", 2)], 19: [("n", 1)], 20: [("r", 2, 2), ("r", 2, 3)],
            21: [("r", 2, 5), ("r", 2, 6)], 27: [("n", 2)], 28: [("r", 3, 1), ("r", 3, 2)],
            29: [("r", 3, 4), ("r", 3, 5)], 30: [("r", 3, 7)], 31: [("n", 3)]}


def build(nc, x, cond, W1, b1, W2, b2, Wx, Wh, bx, Wf, bf, Wi, bi, Wc, bc, base, w1, c1, w2, c2, ln_g, ln_b, out):
    keep = ExitStack()
    with keep:
        def sb(name, shape, dt=F32, at=keep):
            return at.enter_context(nc.sbuf_tensor(name, shape, dt))

        ident = sb("ident", [P, P])
        condT = sb("condT", [P, C, B])
        XA = sb("XA", [P, D])
        x2_d, g_d, n_d = (nc.dram_tensor(s, [B, P, C, TS + T], F32, kind="Internal").ap() for s in ("x2_d", "g_d", "n_d"))
        xb_d = nc.dram_tensor("xb_d", [B, 2 * RANK, D], F32, kind="Internal").ap()

        with ExitStack() as mid:
            gate2 = sb("gate2", [P, C, B], at=mid)
            split = {k: (sb(f"{k}_hi", [P, C, D], F32R, mid), sb(f"{k}_lo", [P, C, D], F32R, mid)) for k in "xfic"}
            wh_hi, wh_lo = sb("wh_hi", [P, C, D], F16, mid), sb("wh_lo", [P, C, D], F16, mid)
            whs = sb("whs", [P, 4], at=mid)
            sbx = sb("sbx", [P, C], at=mid)
            bias = {k: sb(f"bias_{k}", [P, C], at=mid) for k in "fic"}
            h0wh = sb("h0wh", [P, C, B], at=mid)
            prologue(nc, locals())
            recurrence(nc, locals())
        tail(nc, locals())


def prologue(nc, v):
    ident, condT, XA, xb_d = v["ident"], v["condT"], v["XA"], v["xb_d"]
    gate2, split, wh_hi, wh_lo, whs, sbx, bias, h0wh = (v[k] for k in "gate2 split wh_hi wh_lo whs sbx bias h0wh".split())
    with ExitStack() as ctx:
        def sb(name, shape, dt=F32):
            return ctx.enter_context(nc.sbuf_tensor(name, shape, dt))

        def ps(name, shape):
            return ctx.enter_context(nc.psum_tensor(name, shape, F32))

        def sem(name):
            return ctx.enter_context(nc.semaphore(name))

        raw = {k: sb(f"raw_{k}", [P, C, D]) for k in ("1", "f", "i", "c")}
        raw["2"] = raw["1"]
        wT1, wT2 = sb("wT1", [P, C, D]), sb("wT2", [P, C, D])
        wh, wx = wT1, wT2
        w1s = raw["1"]
        row = sb("row", [1, 3, D])
        ones = sb("ones", [1, B])
        crow = sb("crow", [B, D])
        ae, t16, aeT, hg = sb("ae", [B, D]), sb("t16", [B, D]), sb("aeT", [P, C, B]), sb("hg", [B, D])
        lng, lnb = sb("lng", [B, D]), sb("lnb", [B, D])
        stat = sb("stat", [B, 4])
        hT, hgT = sb("hT", [P, C, B]), sb("hgT", [P, C, B])
        z16, sg = sb("z16", [B, D]), sb("sg", [B, D])
        lr = sb("lr", [B, 2, RANK, D])
        w2s = sb("w2s", [P, 2, C, D])
        c2s = sb("c2s", [B, 2, D])
        trp = [ps(f"trp{i}", [P, D]) for i in range(2)]
        small = ps("small", [P, C, B])
        zz = ps("zz", [P, D])
        lrp = [ps(f"lrp{i}", [P, D]) for i in range(2)]
        h0p = ps("h0p", [P, C, B])

        (d_cond, d_w1, d_w2, d_fic, d_rows, d_ln, d_wh, d_wx, d_h1, d_bias, d_lr) = (
            sem("p_" + s) for s in "d_cond d_w1 d_w2 d_fic d_rows d_ln d_wh d_wx d_h1 d_bias d_lr".split())
        d_s, d_c2 = [sem(f"p_d_s{i}") for i in range(2)], [sem(f"p_d_c2{i}") for i in range(2)]
        (s_id, s_one, s_ct, s_ctc, s_tr, s_hi, s_lo, s_z, s_v, s_sg, s_hT, s_hTc, s_ae, s_a, s_mx, s_amx, s_wh, s_h0, s_lr,
         s_lrv, s_wx, s_sb) = (
            sem("p_" + s) for s in ("s_id s_one s_ct s_ctc s_tr s_hi s_lo s_z s_v s_sg s_hT s_hTc s_ae s_a s_mx s_amx s_wh s_h0 s_lr "
                                    "s_lrv s_wx s_sb").split())
        NQ = 2 * D * RANK // D

        block = ctx.enter_context(nc.Block())

        @block.sync
        def _(sp):
            sp.dma_start(crow[:], v["cond"]).then_inc(d_cond, 16)
            sp.dma_start(raw["1"][:], v["W1"].rearrange("(c p) d -> p c d", p=P)).then_inc(d_w1, 16)
            for n, k in enumerate(("b1", "b2", "c1")):
                sp.dma_start(row[:, n, :], v[k].rearrange("(a d) -> a d", a=1)).then_inc(d_rows, 16)
            for k, w in (("f", "Wf"), ("i", "Wi"), ("c", "Wc")):
                sp.dma_start(raw[k][:], v[w].rearrange("(c p) d -> p c d", p=P)).then_inc(d_fic, 16)
            sp.dma_start(lng[:], v["ln_g"].rearrange("(a d) -> a d", a=1).to_broadcast([B, D])).then_inc(d_ln, 16)
            sp.dma_start(lnb[:], v["ln_b"].rearrange("(a d) -> a d", a=1).to_broadcast([B, D])).then_inc(d_ln, 16)
            for k, w in (("f", "bf"), ("i", "bi"), ("c", "bc")):
                sp.dma_start(bias[k][:], v[w].rearrange("(c p) -> p c", p=P), allow_slow_non_contiguous=True).then_inc(d_bias, 16)
            sp.dma_start(sbx[:], v["bx"].rearrange("(c p) -> p c", p=P), allow_slow_non_contiguous=True).then_inc(d_bias, 16)
            sp.wait_ge(s_tr, C)
            sp.dma_start(raw["2"][:], v["W2"].rearrange("(c p) d -> p c d", p=P)).then_inc(d_w2, 16)

            def low_rank_piece(q):
                if q >= 2:
                    sp.wait_ge(s_lrv, q - 1)
                sp.dma_start(w2s[:, q % 2], v["w2"][:, q * D:(q + 1) * D].rearrange("(c p) d -> p c d", p=P)).then_inc(d_s[q % 2], 16)
                sp.dma_start(c2s[:, q % 2], v["c2"][q * D:(q + 1) * D].rearrange("(a d) -> a d", a=1).to_broadcast([B, D])).then_inc(d_c2[q % 2], 16)

            low_rank_piece(0)
            low_rank_piece(1)
            sp.wait_ge(s_z, 1)
            sp.dma_start(wh[:], v["Wh"].rearrange("(c p) d -> p c d", p=P)).then_inc(d_wh, 16)
            sp.wait_ge(s_tr, 2 * C)
            sp.dma_start(w1s[:], v["w1"].rearrange("(c p) d -> p c d", p=P)).then_inc(d_h1, 16)
            sp.wait_ge(s_z, 2)
            sp.dma_start(wx[:], v["Wx"].rearrange("(c p) d -> p c d", p=P)).then_inc(d_wx, 16)
            for q in range(2, NQ):
                low_rank_piece(q)
            sp.wait_ge(s_lrv, NQ)
            for r in range(RANK):
                sp.dma_start(XA[r * B:(r + 1) * B, :], lr[:, 0, r, :]).then_inc(d_lr, 16)
            for copy in range(2):
                sp.dma_start(xb_d[:, copy * RANK:(copy + 1) * RANK, :], lr[:, 1]).then_inc(d_lr, 16)
            sp.wait_ge(d_lr, 16 * (RANK + 2))
            sp.wait_ge(d_bias, 64)

        @block.gpsimd
        def _(pool):
            nc.gpsimd.memset(ident[:], 0.0).then_inc(s_id, 1)
            nc.gpsimd.memset(ones[:], 1.0).then_inc(s_one, 1)
            pool.wait_ge(s_id, 1)
            nc.gpsimd.affine_select(out=ident[:], in_=ident[:], compare_op=ALU.not_equal, fill=1.0, base=0,
                                    pattern=[[-1, P]], channel_multiplier=1).then_inc(s_id, 1)
            pool.wait_ge(s_mx, 1)
            nc.gpsimd.partition_all_reduce(whs[:, 1:2], whs[:, 0:1], P, bass.bass_isa.ReduceOp.max).then_inc(s_amx, 1)

        @block.tensor
        def _(pe):
            pe.wait_ge(s_id, 2)
            pe.wait_ge(d_cond, 16)

            def rows_to_cols(src, done):
                for c in range(C):
                    last = nc.tensor.transpose(small[:, c, :], src[:, c * P:(c + 1) * P], ident[0:B, 0:B])
                last.then_inc(done, 1)

            rounds = [0]

            def transpose_weight(k):
                for c in range(C):
                    n = rounds[0]
                    if n >= 2:
                        pe.wait_ge(s_hi, n - 1)
                        if n - 2 >= 2 * C:
                            pe.wait_ge(s_lo, n - 1 - 2 * C)
                    for r in range(C):
                        last = nc.tensor.transpose(trp[n % 2][:, r * P:(r + 1) * P], raw[k][:, r, c * P:(c + 1) * P], ident[:])
                    last.then_inc(s_tr, 1)
                    rounds[0] += 1

            def dense16(lhs, w, n):
                for c in range(C):
                    nc.tensor.matmul(zz[0:B, :], lhs[:, c, :], w[:, c, :], start=(c == 0), stop=False)
                nc.tensor.matmul(zz[0:B, :], ones[:], row[:, n, :], start=False, stop=True).then_inc(s_z, 1)

            rows_to_cols(crow, s_ct)
            pe.wait_ge(d_w1, 16)
            transpose_weight("1")
            pe.wait_ge(s_ctc, 1)
            pe.wait_ge(s_hi, C)
            pe.wait_ge(d_rows, 48)
            pe.wait_ge(s_one, 1)
            dense16(condT, wT1, 0)
            pe.wait_ge(d_w2, 16)
            transpose_weight("2")
            pe.wait_ge(s_v, 1)
            rows_to_cols(hg, s_hT)
            pe.wait_ge(s_hTc, 1)
            pe.wait_ge(s_hi, 2 * C)
            dense16(hT, wT2, 1)
            pe.wait_ge(s_ae, 1)
            rows_to_cols(ae, s_hT)
            pe.wait_ge(s_hTc, 2)
            pe.wait_ge(d_h1, 16)
            pe.wait_ge(s_sg, 2)
            dense16(aeT, w1s, 2)
            pe.wait_ge(d_fic, 48)
            for k in "fic":
                transpose_weight(k)
            rows_to_cols(sg, s_hT)
            pe.wait_ge(s_hTc, 3)
            pe.wait_ge(s_sg, 3)
            rows_to_cols(hg, s_hT)
            pe.wait_ge(s_hTc, 4)
            pe.wait_ge(d_wh, 16)
            for m in range(C):
                for c in range(C):
                    last = nc.tensor.matmul(h0p[:, m, :], wh[:, c, m * P:(m + 1) * P], condT[:, c, :],
                                            start=(c == 0), stop=(c == C - 1))
            last.then_inc(s_h0, 1)
            for q in range(NQ):
                pe.wait_ge(d_s[q % 2], 16 * (q // 2 + 1))
                if q >= 2:
                    pe.wait_ge(s_lrv, q - 1)
                for c in range(C):
                    last = nc.tensor.matmul(lrp[q % 2][0:B, :], hgT[:, c, :], w2s[:, q % 2, c, :],
                                            start=(c == 0), stop=(c == C - 1))
                last.then_inc(s_lr, 1)

        @block.scalar
        def _(act):
            for n in range(2 * C):
                act.wait_ge(s_tr, n + 1)
                nc.scalar.copy((wT1 if n < C else wT2)[:, n % C, :], trp[n % 2][:]).then_inc(s_hi, 1)
                if n == C - 1:
                    act.wait_ge(s_sb, 1)
                    nc.scalar.activation(sg[:], zz[0:B, :], ACT.Sigmoid).then_inc(s_sg, 1)
            act.wait_ge(s_z, 2)
            act.wait_ge(s_v, 1)
            nc.scalar.activation(sg[:], zz[0:B, :], ACT.Sigmoid).then_inc(s_sg, 1)
            act.wait_ge(s_a, 2)
            nc.scalar.activation(t16[:], ae[:], ACT.Square, accum_out=stat[:, 1:2]).then_inc(s_a, 1)
            act.wait_ge(s_a, 4)
            nc.scalar.activation(stat[:, 3:4], stat[:, 2:3], ACT.Sqrt).then_inc(s_a, 1)
            act.wait_ge(s_z, 3)
            act.wait_ge(s_hT, 1)
            nc.scalar.activation(hg[:], zz[0:B, :], ACT.Gelu).then_inc(s_sg, 1)
            for n, k in enumerate("fic"):
                for c in range(C):
                    act.wait_ge(s_tr, 2 * C + n * C + c + 1)
                    nc.scalar.copy(split[k][0][:, c, :], trp[(n * C + c) % 2][:]).then_inc(s_hi, 1)
            act.wait_ge(d_wx, 16)
            nc.scalar.copy(split["x"][0][:], wx[:]).then_inc(s_wx, 1)

        @block.vector
        def _(dve):
            dve.wait_ge(s_ct, 1)
            nc.vector.tensor_copy(condT[:], small[:]).then_inc(s_ctc, 1)
            dve.wait_ge(d_cond, 16)
            nc.vector.tensor_reduce(stat[:, 0:1], crow[:], axis=AX.X, op=ALU.add).then_inc(s_a, 1)
            dve.wait_ge(s_a, 1)
            nc.vector.scalar_tensor_tensor(ae[:], stat[:, 0:1].to_broadcast([B, D]), -1.0 / D, crow[:], ALU.mult, ALU.add).then_inc(s_a, 1)
            dve.wait_ge(s_z, 1)
            nc.vector.tensor_copy(z16[:], zz[0:B, :]).then_inc(s_sb, 1)
            dve.wait_ge(s_sg, 1)
            dve.wait_ge(s_sb, 1)
            nc.vector.tensor_tensor(hg[:], z16[:], sg[:], ALU.mult).then_inc(s_v, 1)
            dve.wait_ge(s_hT, 1)
            nc.vector.tensor_copy(hT[:], small[:]).then_inc(s_hTc, 1)
            dve.wait_ge(s_a, 3)
            nc.vector.tensor_scalar(stat[:, 2:3], stat[:, 1:2], 1.0 / D, LN_EPS, ALU.mult, ALU.add).then_inc(s_a, 1)
            dve.wait_ge(s_a, 5)
            nc.vector.reciprocal(stat[:, 0:1], stat[:, 3:4]).then_inc(s_a, 1)
            dve.wait_ge(s_a, 6)
            dve.wait_ge(d_ln, 32)
            nc.vector.scalar_tensor_tensor(t16[:], ae[:], stat[:, 0:1], lng[:], ALU.mult, ALU.mult).then_inc(s_a, 1)
            dve.wait_ge(s_a, 7)
            nc.vector.tensor_tensor(ae[:], t16[:], lnb[:], ALU.add).then_inc(s_ae, 1)
            dve.wait_ge(s_hT, 2)
            nc.vector.tensor_copy(aeT[:], small[:]).then_inc(s_hTc, 1)
            for n, k in enumerate("fic"):
                for c in range(C):
                    dve.wait_ge(s_hi, 2 * C + n * C + c + 1)
                    nc.vector.tensor_tensor(split[k][1][:, c, :], trp[(n * C + c) % 2][:],
                                            split[k][0][:, c, :].bitcast(F32), ALU.subtract).then_inc(s_lo, 1)
            dve.wait_ge(s_hT, 3)
            nc.vector.tensor_scalar(gate2[:], small[:], 2.0, None, ALU.add).then_inc(s_hTc, 1)
            dve.wait_ge(s_hT, 4)
            nc.vector.tensor_copy(hgT[:], small[:]).then_inc(s_hTc, 1)
            dve.wait_ge(d_wh, 16)
            nc.vector.tensor_reduce(whs[:, 0:1], wh[:], axis=AX.XY, op=ALU.max, apply_absolute_value=True).then_inc(s_mx, 1)
            dve.wait_ge(s_amx, 1)
            nc.vector.tensor_scalar(whs[:, 2:3].bitcast(I32), whs[:, 1:2].bitcast(I32), 0x7F800000, None, ALU.bitwise_and).then_inc(s_wh, 1)
            dve.wait_ge(s_wh, 1)
            nc.vector.tensor_scalar(whs[:, 0:1], whs[:, 2:3], 2.0 ** -100, 2.0 ** 120, ALU.max, ALU.min).then_inc(s_wh, 1)
            dve.wait_ge(s_wh, 2)
            nc.vector.tensor_scalar(whs[:, 3:4], whs[:, 0:1], 2.0 ** -14, None, ALU.mult).then_inc(s_wh, 1)
            nc.vector.tensor_scalar(whs[:, 1:2].bitcast(I32), whs[:, 0:1].bitcast(I32), -1, 254 << 23, ALU.mult, ALU.add).then_inc(s_wh, 1)
            dve.wait_ge(s_wh, 4)
            nc.vector.tensor_scalar(whs[:, 2:3], whs[:, 1:2], 2.0 ** 14, None, ALU.mult).then_inc(s_wh, 1)
            dve.wait_ge(s_wh, 5)
            nc.vector.tensor_scalar(wh_hi[:], wh[:], whs[:, 2:3], None, ALU.mult).then_inc(s_wh, 1)
            dve.wait_ge(s_wh, 6)
            for c in range(C):
                nc.vector.scalar_tensor_tensor(wh_lo[:, c, :], wh[:, c, :], whs[:, 2:3], wh_hi[:, c, :], ALU.mult, ALU.subtract).then_inc(s_wh, 1)
            dve.wait_ge(s_h0, 1)
            nc.vector.tensor_scalar(h0wh[:], h0p[:], whs[:, 2:3], None, ALU.mult).then_inc(s_wh, 1)
            dve.wait_ge(d_bias, 64)
            nc.vector.tensor_scalar(sbx[:], sbx[:], whs[:, 2:3], None, ALU.mult).then_inc(s_wh, 1)
            dve.wait_ge(s_wx, 1)
            for c in range(C):
                nc.vector.tensor_tensor(split["x"][1][:, c, :], wx[:, c, :], split["x"][0][:, c, :].bitcast(F32), ALU.subtract).then_inc(s_wx, 1)
            for q in range(2 * D * RANK // D):
                half, d0 = q // RANK, q % RANK * (D // RANK)
                dve.wait_ge(s_lr, q + 1)
                dve.wait_ge(d_c2[q % 2], 16 * (q // 2 + 1))
                nc.vector.tensor_tensor(lr[:, half, :, d0:d0 + D // RANK], lrp[q % 2][0:B, :].rearrange("p (d r) -> p r d", r=RANK),
                                        c2s[:, q % 2, :].rearrange("p (d r) -> p r d", r=RANK), ALU.add).then_inc(s_lrv, 1)


def recurrence(nc, v):
    x, ident = v["x"], v["ident"]
    gate2, split, wh_hi, wh_lo, whs, sbx, bias, h0wh = (v[k] for k in "gate2 split wh_hi wh_lo whs sbx bias h0wh".split())
    x2_d, g_d, n_d = v["x2_d"], v["g_d"], v["n_d"]
    GROUPS = mm_groups()
    with ExitStack() as ctx:
        def sb(name, shape, dt=F32):
            return ctx.enter_context(nc.sbuf_tensor(name, shape, dt))

        def ps(name, shape):
            return ctx.enter_context(nc.psum_tensor(name, shape, F32))

        def sem(name):
            return ctx.enter_context(nc.semaphore(name))

        xnat = sb("xnat", [P, C, D])
        xt = [sb(f"xt{q}", [P, C, TOK]) for q in range(2)]
        x1hi, x1lo = sb("x1hi", [P, C, TOK], F32R), sb("x1lo", [P, C, TOK], F32R)
        x2hi, x2lo = sb("x2hi", [P, C, TOK], F32R), sb("x2lo", [P, C, TOK], F32R)
        xw = [sb(f"xw{q}", [P, TS, C, B]) for q in range(2)]
        hbuf = sb("hbuf", [P, TS, C, B])
        hs = sb("hs", [P, C, 2, B], F16)
        pre0, pre = sb("pre0", [P, C, B]), sb("pre", [P, C, B])
        fbuf, ibuf, rbuf = (sb(s, [P, 2, TOK]) for s in ("fbuf", "ibuf", "rbuf"))
        gst, nst = sb("gst", [P, C, TOK]), sb("nst", [P, C, TOK])
        bank = [ps(f"bank{i}", [P, TOK]) for i in range(4)]
        trb = [ps(f"trb{i}", [P, TOK]) for i in range(2)]
        rec = ps("rec", [P, C, 2, B])

        (d_x, d_x2, d_g, d_n) = (sem("r_" + s) for s in ("d_x", "d_x2", "d_g", "d_n"))
        (s_tr, s_x1, s_x1h, s_x1l, s_xp, s_xw, s_rec, s_pre0, s_pre, s_h, s_hs, s_x2, s_x2h, s_x2l, s_f, s_i, s_c, s_fs, s_is,
         s_gs, s_r, s_fr, s_in, s_g, s_n) = (
            sem("r_" + s) for s in ("s_tr s_x1 s_x1h s_x1l s_xp s_xw s_rec s_pre0 s_pre s_h s_hs s_x2 s_x2h s_x2l s_f s_i s_c s_fs s_is "
                                    "s_gs s_r s_fr s_in s_g s_n").split())
        s_h0 = sem("r_s_h0")

        def cnt(j, per, pos):
            i, q = j
            return i * (2 * per) + (q * per + pos)

        def nxt(j):
            return (j[0], 1) if j[1] == 0 else (j[0] + 1, 0)

        def bank_free(eng, j, n, groups=GROUPS):
            kind, m = groups[n - 4] if n >= 4 else GROUPS[12 + n]
            off = 0 if n >= 4 else -4
            if kind == "f":
                eng.wait_ge(s_fs, cnt(j, 4, m + 1 + off))
            elif kind == "i":
                eng.wait_ge(s_is, cnt(j, 4, m + 1 + off))
            elif kind == "c":
                eng.wait_ge(s_n, cnt(j, 4, 4 + m + 1 + off))
            else:
                eng.wait_ge(s_xw, cnt(j, 4, 4 + m + 1 + off))

        def group_mms(kind, m):
            hi, lo = split[kind]
            ahi, alo = (x1hi, x1lo) if kind == "x" else (x2hi, x2lo)
            return [(w[:, k, m * P:(m + 1) * P], a[:, k, :]) for k in range(C) for w, a in ((hi, ahi), (lo, ahi), (hi, alo))]

        block = ctx.enter_context(nc.Block())

        @block.sync
        def _(sp):
            def load_x(t0):
                for b in range(B):
                    sp.dma_start(xnat[b % 4 * TS:(b % 4 + 1) * TS, b // 4, :], x[b, bass.ds(t0, TS), :]).then_inc(d_x, 16)

            def spill(dst, src, t0, m, done):
                sp.dma_start(dst[:, :, m, bass.ds(t0, TS)].rearrange("b p t -> p b t"),
                             src.rearrange("p (b t) -> p b t", t=TS)).then_inc(done, 16)

            def spill_x2(j, q, t0):
                sp.wait_ge(s_x2, cnt(j, 4, 4))
                for m in range(C):
                    spill(x2_d, xt[1 - q][:, m, :], t0, m, d_x2)

            def spill_gn(j, t0, m):
                sp.wait_ge(s_g, cnt(j, 4, m + 1))
                spill(g_d, gst[:, m, :], t0, m, d_g)
                sp.wait_ge(s_n, cnt(j, 4, 4 + m + 1))
                spill(n_d, nst[:, m, :], t0, m, d_n)

            def body(i, q, ahead):
                j = (i, q)
                t0 = i * (2 * TS) + q * TS
                spill_x2(j, q, t0)
                sp.wait_ge(s_tr, cnt(nxt(j), 4, 4))
                load_x(ahead)
                for m in range(C):
                    spill_gn(j, t0, m)

            load_x(0)
            sp.wait_ge(s_tr, 4)
            load_x(TS)
            with sp.Fori(0, NBLK // 2 - 1) as i:
                for q in range(2):
                    body(i, q, i * (2 * TS) + (q + 2) * TS)
            for q in range(2):
                body(NBLK // 2 - 1, q, q * TS)
            spill_x2((NBLK // 2, 0), 0, T)
            for m in range(C):
                spill_gn((NBLK // 2, 0), T, m)
            sp.wait_ge(d_x2, 64 * (NBLK + 1))
            sp.wait_ge(d_g, 64 * (NBLK + 2))
            sp.wait_ge(d_n, 64 * (NBLK + 2))
            sp.wait_ge(d_x, 256 * (NBLK + 2))

        @block.tensor
        def _(pe):
            def transposes(p, m, first=False):
                if m == 0:
                    pe.wait_ge(d_x, cnt(p, 256, 256))
                if m >= 2 or not first:
                    pe.wait_ge(s_x1, cnt(p, 4, m - 1))
                for a in range(C):
                    last = nc.tensor.transpose(trb[m % 2][:, a * P:(a + 1) * P], xnat[:, a, m * P:(m + 1) * P], ident[:])
                last.then_inc(s_tr, 1)

            def step(j, t):
                pe.wait_ge(s_hs, cnt(j, TS, t + 1))
                for k in range(C):
                    for m in range(C):
                        for w in (wh_hi, wh_lo):
                            last = nc.tensor.matmul(rec[:, m].rearrange("p a b -> p (a b)"), w[:, k, m * P:(m + 1) * P],
                                                    hs[:, k].rearrange("p a b -> p (a b)"),
                                                    start=(k == 0 and m == 0 and w is wh_hi), stop=(k == C - 1),
                                                    skip_group_check=True)
                last.then_inc(s_rec, 1)

            def group_part(j, p, n, groups, lo, hi):
                kind, m = groups[n]
                if lo == 0:
                    bank_free(pe, j, n, groups)
                    if kind == "x":
                        pe.wait_ge(s_x1h, cnt(p, 4, 4))
                        pe.wait_ge(s_x1l, cnt(p, 4, 4))
                    else:
                        pe.wait_ge(s_x2h, cnt(j, 4, 4))
                        pe.wait_ge(s_x2l, cnt(j, 4, 4))
                mms = group_mms(kind, m)
                for e in range(lo, hi):
                    last = nc.tensor.matmul(bank[n % 4][:], mms[e][0], mms[e][1], start=(e == 0), stop=(e == len(mms) - 1))
                if hi == len(mms):
                    last.then_inc({"x": s_xp, "f": s_f, "i": s_i, "c": s_c}[kind], 1)

            GM = 3 * C
            for m in range(C):
                transposes((0, 0), m, True)
            for m in range(C):
                if m == 0:
                    pe.wait_ge(s_x1h, 4)
                    pe.wait_ge(s_x1l, 4)
                mms = group_mms("x", m)
                for e in range(GM):
                    last = nc.tensor.matmul(bank[m][:], mms[e][0], mms[e][1], start=(e == 0), stop=(e == GM - 1))
                last.then_inc(s_xp, 1)
            with pe.Fori(0, NBLK // 2) as i:
                for q in range(2):
                    j = (i, q)
                    at = 0
                    for t in range(TS):
                        step(j, t)
                        if 8 <= t < 8 + C:
                            transposes(nxt(j), t - 8)
                        end = at + PE_QUOTA[t]
                        while at < end:
                            n, lo = at // GM, at % GM
                            hi = min(GM, lo + end - at)
                            group_part(j, nxt(j), n, GROUPS, lo, hi)
                            at += hi - lo
            last_groups = [g for g in GROUPS if g[0] != "x"]
            for n in range(len(last_groups)):
                group_part((NBLK // 2, 0), None, n, last_groups, 0, GM)

        @block.scalar
        def _(act):
            unscale = act.alloc_register("unscale")
            act.reg_load(unscale, whs[0:1, 3:4].bitcast(I32))

            def tanh(j, t, hb):
                act.wait_ge(s_pre, cnt(j, TS, t + 1))
                if t % STAGE == 0:
                    act.wait_ge(s_x2, cnt(j, 4, t // STAGE + 1))
                nc.scalar.activation(hs[:, :, 0, :], pre[:], ACT.Tanh, scale=unscale).then_inc(s_h, 1)
                nc.scalar.activation(hb, pre[:], ACT.Tanh, scale=unscale).then_inc(s_h, 1)

            def x1_high(p, q, m):
                act.wait_ge(s_x1, cnt(p, 4, m + 1))
                act.wait_ge(s_xp, cnt(p, 4, 0))
                nc.scalar.copy(x1hi[:, m, :], xt[q][:, m, :]).then_inc(s_x1h, 1)

            def x2_high(j, q, m):
                act.wait_ge(s_x2, cnt(j, 4, 4))
                act.wait_ge(s_n, cnt(j, 4, 4))
                nc.scalar.copy(x2hi[:, m, :], xt[1 - q][:, m, :]).then_inc(s_x2h, 1)

            def input_products(p, q, m, src):
                act.wait_ge(s_xp, cnt(p, 4, m + 1))
                nc.scalar.activation(xw[q][:, :, m, :].rearrange("p t b -> p b t"), src[:].rearrange("p (b t) -> p b t", t=TS),
                                     ACT.Identity, bias=sbx[:, m:m + 1], scale=whs[:, 2:3]).then_inc(s_xw, 1)

            def gate(j, n, groups):
                kind, m = groups[n]
                made, done, buf = (s_f, s_fs, fbuf) if kind == "f" else (s_i, s_is, ibuf)
                act.wait_ge(made, cnt(j, 4, m + 1))
                if kind == "f" and m < 2:
                    act.wait_ge(d_g, cnt(j, 64, 64))
                elif kind == "f":
                    act.wait_ge(s_g, cnt(j, 4, m - 1))
                else:
                    act.wait_ge(s_n, cnt(j, 4, 4 + m - 1))
                nc.scalar.activation(buf[:, m % 2, :], bank[n % 4][:], ACT.Sigmoid, bias=bias[kind][:, m:m + 1]).then_inc(done, 1)

            def forget_share(j, m):
                act.wait_ge(s_fr, cnt(j, 4, m + 1))
                act.wait_ge(d_g, cnt(j, 64, 64 + 16 * m))
                nc.scalar.activation(gst[:, m, :], fbuf[:, m % 2, :], ACT.Copy, bias=EPS2).then_inc(s_g, 1)

            def work(j, item):
                kind, m = item
                if kind == "x2h":
                    x2_high(j, j[1], m)
                elif kind == "x1h":
                    x1_high(nxt(j), 1 - j[1], m)
                elif kind == "x":
                    input_products(nxt(j), 1 - j[1], m, bank[GROUPS.index(item) % 4])
                elif kind == "g":
                    forget_share(j, m)
                else:
                    gate(j, GROUPS.index(item), GROUPS)

            for m in range(C):
                x1_high((0, 0), 0, m)
            for m in range(C):
                input_products((0, 0), 0, m, bank[m])
            with act.Fori(0, NBLK // 2) as i:
                for q in range(2):
                    for t in range(TS):
                        tanh((i, q), t, hbuf[:, t])
                        for item in ACT_WORK.get(t, []):
                            work((i, q), item)
            end = (NBLK // 2, 0)
            last_groups = [g for g in GROUPS if g[0] != "x"]
            for m in range(C):
                x2_high(end, 0, m)
            for kind, m in last_groups:
                if kind != "c":
                    gate(end, last_groups.index((kind, m)), last_groups)
                else:
                    forget_share(end, m)

        @block.gpsimd
        def _(pool):
            def x1_low(p, q, m):
                pool.wait_ge(s_x1h, cnt(p, 4, m + 1))
                nc.gpsimd.tensor_tensor(x1lo[:, m, :], xt[q][:, m, :], x1hi[:, m, :].bitcast(F32), ALU.subtract).then_inc(s_x1l, 1)

            def x2_low(j, q, m):
                pool.wait_ge(s_x2h, cnt(j, 4, m + 1))
                nc.gpsimd.tensor_tensor(x2lo[:, m, :], xt[1 - q][:, m, :], x2hi[:, m, :].bitcast(F32), ALU.subtract).then_inc(s_x2l, 1)

            def add_h(j, q, s):
                pool.wait_ge(s_h, cnt(j, 2 * TS, 2 * STAGE * (s + 1)))
                if s == 0:
                    pool.wait_ge(s_x1l, cnt(j, 4, 4))
                xs = xt[q][:].rearrange("p c (b t) -> p c b t", t=TS)[:, :, :, s * STAGE:(s + 1) * STAGE]
                nc.gpsimd.tensor_tensor(xs, xs, hbuf[:, s * STAGE:(s + 1) * STAGE].rearrange("p t c b -> p c b t"), ALU.add).then_inc(s_x2, 1)

            def shares(j, m):
                pool.wait_ge(s_r, cnt(j, 4 * PIECES, PIECES * (m + 1)))
                nc.gpsimd.tensor_tensor(fbuf[:, m % 2, :], fbuf[:, m % 2, :], rbuf[:, m % 2, :], ALU.mult).then_inc(s_fr, 1)
                nc.gpsimd.tensor_tensor(ibuf[:, m % 2, :], ibuf[:, m % 2, :], rbuf[:, m % 2, :], ALU.mult).then_inc(s_in, 1)

            for m in range(C):
                nc.gpsimd.memset(xt[1][:, m, :], 0.0).then_inc(s_x2, 1)
            for m in range(C):
                x1_low((0, 0), 0, m)
            with pool.Fori(0, NBLK // 2) as i:
                for q in range(2):
                    j = (i, q)
                    for m in range(C):
                        x2_low(j, q, m)
                    add_h(j, q, 0)
                    for m in range(C):
                        x1_low(nxt(j), 1 - q, m)
                    shares(j, 0)
                    add_h(j, q, 1)
                    shares(j, 1)
                    shares(j, 2)
                    add_h(j, q, 2)
                    shares(j, 3)
                    add_h(j, q, 3)
            end = (NBLK // 2, 0)
            for m in range(C):
                x2_low(end, 0, m)
            for m in range(C):
                shares(end, m)

        @block.vector
        def _(dve):
            def x1_gated(p, q, m, j=None):
                dve.wait_ge(s_tr, cnt(p, 4, m + 1))
                if j is not None and m == 0:
                    dve.wait_ge(s_x2h, cnt(j, 4, 4))
                    dve.wait_ge(s_x2l, cnt(j, 4, 4))
                    dve.wait_ge(d_x2, cnt(j, 64, 64))
                nc.vector.tensor_tensor(xt[q][:, m, :].rearrange("p (b t) -> p b t", t=TS), trb[m % 2][:].rearrange("p (b t) -> p b t", t=TS),
                                        gate2[:, m, :].unsqueeze(2).to_broadcast([P, B, TS]), ALU.mult).then_inc(s_x1, 1)

            def gate_sum(j, m):
                dve.wait_ge(s_fs, cnt(j, 4, m + 1))
                dve.wait_ge(s_is, cnt(j, 4, m + 1))
                if m < 2:
                    dve.wait_ge(s_n, cnt(j, 4, 4))
                else:
                    dve.wait_ge(s_in, cnt(j, 4, m - 1))
                nc.vector.scalar_tensor_tensor(rbuf[:, m % 2, :], fbuf[:, m % 2, :], EPS2, ibuf[:, m % 2, :], ALU.add, ALU.add).then_inc(s_gs, 1)

            def recip(j, m, e):
                if e == 0:
                    dve.wait_ge(s_gs, cnt(j, 4, m + 1))
                piece = rbuf[:, m % 2, e * PW:(e + 1) * PW]
                nc.vector.reciprocal(piece, piece).then_inc(s_r, 1)

            def new_info(j, n, groups):
                m = groups[n][1]
                dve.wait_ge(s_c, cnt(j, 4, m + 1))
                dve.wait_ge(s_in, cnt(j, 4, m + 1))
                dve.wait_ge(d_n, cnt(j, 64, 64 + 16 * m))
                nc.vector.scalar_tensor_tensor(nst[:, m, :], bank[n % 4][:], bias["c"][:, m:m + 1], ibuf[:, m % 2, :],
                                               ALU.add, ALU.mult).then_inc(s_n, 1)

            def work(j, item):
                if item[0] == "x1":
                    x1_gated(nxt(j), 1 - j[1], item[1], j)
                elif item[0] == "s":
                    gate_sum(j, item[1])
                elif item[0] == "r":
                    recip(j, item[1], item[2])
                else:
                    new_info(j, GROUPS.index(("c", item[1])), GROUPS)

            nc.vector.memset(hs[:], 0.0).then_inc(s_hs, 1)
            nc.vector.memset(pre[:, 0, :], 0.0).then_inc(s_n, 4)
            nc.vector.memset(pre[:, 1, :], 0.0).then_inc(d_g, 64)
            nc.vector.memset(pre[:, 2, :], 0.0).then_inc(d_n, 64)
            for m in range(C):
                x1_gated((0, 0), 0, m)
            dve.wait_ge(s_xw, 4)
            nc.vector.tensor_tensor(xw[0][:, 0], xw[0][:, 0], h0wh[:], ALU.add).then_inc(s_h0, 1)
            dve.wait_ge(s_h0, 1)
            with dve.Fori(0, NBLK // 2) as i:
                for q in range(2):
                    j = (i, q)
                    for t in range(TS):
                        if t == 0:
                            dve.wait_ge(s_xw, cnt(j, 4, 4))
                        dve.wait_ge(s_rec, cnt(j, TS, t + 1))
                        nc.vector.tensor_tensor(pre0[:], rec[:, :, 0, :], xw[q][:, t], ALU.add).then_inc(s_pre0, 1)
                        dve.wait_ge(s_pre0, cnt(j, TS, t + 1))
                        nc.vector.tensor_tensor(pre[:], rec[:, :, 1, :], pre0[:], ALU.add).then_inc(s_pre, 1)
                        for item in DVE_EARLY.get(t, []):
                            work(j, item)
                        dve.wait_ge(s_h, cnt(j, 2 * TS, 2 * t + 2))
                        nc.vector.tensor_tensor(hs[:, :, 1, :], hbuf[:, t], hs[:, :, 0, :], ALU.subtract).then_inc(s_hs, 1)
                        for item in DVE_LATE.get(t, []):
                            work(j, item)
            end = (NBLK // 2, 0)
            last_groups = [g for g in GROUPS if g[0] != "x"]
            for m in range(C):
                gate_sum(end, m)
                for e in range(PIECES):
                    recip(end, m, e)
                new_info(end, last_groups.index(("c", m)), last_groups)


def tail(nc, v):
    ident, condT, XA, out, base = (v[k] for k in "ident condT XA out base".split())
    x2_d, g_d, n_d, xb_d = v["x2_d"], v["g_d"], v["n_d"], v["xb_d"]
    with ExitStack() as ctx:
        def sb(name, shape, dt=F32):
            return ctx.enter_context(nc.sbuf_tensor(name, shape, dt))

        def ps(name, shape):
            return ctx.enter_context(nc.psum_tensor(name, shape, F32))

        def sem(name):
            return ctx.enter_context(nc.semaphore(name))

        NT = T // P
        PAIR = 2 * RANK
        GRP = 32
        YR = 2 * GRP + PAIR
        LOW_BY_DVE = 1
        bhi, blo = sb("bhi", [P, C, D], F32R), sb("blo", [P, C, D], F32R)
        one, zero = sb("one", [P, T]), sb("zero", [P, T])
        gin, nin, xin = ([sb(f"{s}in{q}", [P, C, T]) for q in range(2)] for s in "gnx")
        Sb, Pb = sb("Sb", [P, 2, T]), sb("Pb", [P, 2, T])
        U = [sb(f"U{q}", [P, C, T]) for q in range(2)]
        X = [sb(f"X{q}", [P, C, T]) for q in range(2)]
        braw = X[1]
        x3hi = [sb(f"x3hi{q}", [P, C, T], F32R) for q in range(2)]
        x3lo = [sb(f"x3lo{q}", [P, C, T], F32R) for q in range(2)]
        xa = sb("xa", [P, C, B, PAIR], F32R)
        xag = [sb(f"xag{q}", [P, C, 3 * GRP], F32R) for q in range(2)]
        xbr = [sb(f"xbr{q}", [YR, D]) for q in range(2)]
        xbs = [sb(f"xbs{q}", [YR, D], F32R) for q in range(2)]
        ys = [sb(f"ys{q}", [YR, T], F32R) for q in range(2)]
        oout = sb("oout", [P, NT, D])
        yp = [ps(f"yp{q}", [P, T]) for q in range(2)]
        outp = [ps(f"outp{i}", [P, D]) for i in range(NT)]
        xat = ps("xat", [P, C, RANK, B])
        d_base = sem("t_d_base")
        d_g, d_n, d_x, d_xb = ([sem(f"t_d_{s}{q}") for q in range(2)] for s in ("g", "n", "x", "xb"))
        d_out = [sem(f"t_d_out{t}") for t in range(NT)]
        (s_zero, s_b2, s_bh, s_bl, s_xat, s_xah, s_xal, s_xag, s_P, s_S, s_u, s_xp, s_H, s_x3, s_x3h, s_lowd, s_lowp, s_xbh, s_xbl,
         s_yp, s_yh, s_yl, s_op, s_o) = (
            sem("t_" + s) for s in ("s_zero s_b2 s_bh s_bl s_xat s_xah s_xal s_xag s_P s_S s_u s_xp s_H s_x3 s_x3h s_lowd s_lowp s_xbh s_xbl "
                                    "s_yp s_yh s_yl s_op s_o").split())

        def cnt(b, per, pos):
            i, q = b
            return i * (2 * per) + (q * per + pos)

        def nxt(b):
            return (b[0], 1) if b[1] == 0 else (b[0] + 1, 0)

        def number(b):
            return b[0] * 2 + b[1]

        def grp(tile, g, n=PAIR):
            return tile[g * GRP:g * GRP + n, :]

        block = ctx.enter_context(nc.Block())

        @block.sync
        def _(sp):
            def load(q, b):
                for dst, src, done in ((gin, g_d, d_g), (nin, n_d, d_n), (xin, x2_d, d_x)):
                    sp.dma_start(dst[q][:], src[bass.ds(b, 1), :, :, TS:TS + T].rearrange("a p c t -> (a p) c t")).then_inc(done[q], 16)
                for g in range(3):
                    sp.dma_start(grp(xbr[q], g), xb_d[bass.ds(b, 1), :, :].rearrange("a r d -> (a r) d")).then_inc(d_xb[q], 16)

            def load_ahead(b):
                sp.wait_ge(s_P, cnt(b, C, C))
                sp.wait_ge(s_S, cnt(b, C, C))
                sp.wait_ge(s_u, cnt(b, C, C))
                sp.wait_ge(s_xp, cnt(b, C, C))
                sp.wait_ge(s_xbl, cnt(b, 1, 1))
                load(b[1], number(b) + 2)

            def store(b):
                for t in range(NT):
                    sp.wait_ge(s_o, cnt(b, NT, NT + t + 1))
                    sp.dma_start(out[bass.ds(number(b), 1), t * P:(t + 1) * P, :].rearrange("a p d -> (a p) d"), oout[:, t, :]).then_inc(d_out[t], 16)

            sp.wait_ge(s_zero, 2)
            load(0, 0)
            sp.dma_start(braw[:], base.rearrange("(c p) d -> p c d", p=P)).then_inc(d_base, 16)
            load(1, 1)
            load_ahead((0, 0))
            with sp.Fori(0, B // 2 - 2) as i:
                for q in range(2):
                    load_ahead(nxt((i, q)))
                    store((i, q))
            load_ahead((B // 2 - 2, 1))
            for q in range(2):
                store((B // 2 - 2, q))
            for q in range(2):
                store((B // 2 - 1, q))
            for t in range(NT):
                sp.wait_ge(d_out[t], 16 * (B + 1))

        @block.vector
        def _(dve):
            def scans(b, m, first=False):
                q = b[1]
                if m == 0:
                    dve.wait_ge(d_g[q], b[0] * 16 + 16)
                if m >= 2 or not first:
                    dve.wait_ge(s_u, cnt(b, C, m - 1))
                nc.vector.tensor_tensor_scan(Sb[:, m % 2, ::-1], gin[q][:, m, ::-1], zero[:], 1.0, ALU.mult, ALU.add).then_inc(s_S, 1)
                if m >= 2 or not first:
                    dve.wait_ge(s_xp, cnt(b, C, m - 1))
                nc.vector.tensor_tensor_scan(Pb[:, m % 2, :], gin[q][:, m, :], zero[:], condT[:, m, bass.ds(number(b), 1)],
                                             ALU.mult, ALU.add).then_inc(s_P, 1)

            def sum_u(b, m):
                dve.wait_ge(s_u, cnt(b, C, m + 1))
                nc.vector.tensor_tensor_scan(U[b[1]][:, m, :], one[:], U[b[1]][:, m, :], 0.0, ALU.mult, ALU.add).then_inc(s_H, 1)

            def add_sum(b, m):
                dve.wait_ge(s_xp, cnt(b, C, m + 1))
                dve.wait_ge(s_H, cnt(b, C, m + 1))
                nc.vector.tensor_tensor(X[b[1]][:, m, :], X[b[1]][:, m, :], U[b[1]][:, m, :], ALU.add).then_inc(s_x3, 1)

            def x3_low(b, m):
                dve.wait_ge(s_x3h, cnt(b, C, m + 1))
                nc.vector.tensor_tensor(x3lo[b[1]][:, m, :], X[b[1]][:, m, :], x3hi[b[1]][:, m, :].bitcast(F32), ALU.subtract).then_inc(s_lowd, 1)

            def factor_low(b):
                dve.wait_ge(s_xbh, cnt(b, 1, 1))
                nc.vector.tensor_tensor(grp(xbs[b[1]], 1), grp(xbr[b[1]], 1), grp(xbs[b[1]], 1).bitcast(F32), ALU.subtract).then_inc(s_xbl, 1)

            def y_low(b):
                dve.wait_ge(s_yh, cnt(b, 1, 1))
                nc.vector.tensor_tensor(grp(ys[b[1]], 2), grp(yp[b[1]], 2), grp(ys[b[1]], 2).bitcast(F32), ALU.subtract).then_inc(s_yl, 1)

            def body(b, ahead=True, behind=None):
                for m in range(C):
                    if ahead:
                        scans(nxt(b), m)
                    sum_u(b, m)
                    if m == 0:
                        factor_low(b)
                    if m == 1 and behind:
                        y_low(behind)
                    add_sum(b, m)
                    if m == LOW_BY_DVE + 1:
                        x3_low(b, LOW_BY_DVE)

            for q in range(2):
                nc.vector.memset(xbr[q][:], 0.0).then_inc(s_zero, 1)
            nc.vector.memset(one[:], 1.0).then_inc(s_o, NT)
            for t in range(NT):
                nc.vector.memset(zero[:, t * P:(t + 1) * P], 0.0).then_inc(d_out[t], 16)
            nc.vector.memset(xag[0][:].bitcast(F32), 0.0).then_inc(s_op, 2 * NT)
            nc.vector.memset(xag[1][:].bitcast(F32), 0.0).then_inc(s_yl, 2)
            dve.wait_ge(s_o, NT)
            for t in range(NT):
                dve.wait_ge(d_out[t], 16)
            for m in range(C):
                scans((0, 0), m, True)
            dve.wait_ge(d_base, 16)
            for m in range(C):
                nc.vector.scalar_tensor_tensor(braw[:, m, m * P:(m + 1) * P], ident[:], 2.0, braw[:, m, m * P:(m + 1) * P],
                                               ALU.mult, ALU.add).then_inc(s_b2, 1)
            dve.wait_ge(s_xah, 1)
            nc.vector.tensor_tensor(xa[:, :, :, RANK:PAIR], xat[:].rearrange("p c r b -> p c b r"),
                                    xa[:, :, :, 0:RANK].bitcast(F32), ALU.subtract).then_inc(s_xal, 1)
            for m in range(C):
                dve.wait_ge(s_bh, m + 1)
                nc.vector.tensor_tensor(blo[:, m, :], braw[:, m, :], bhi[:, m, :].bitcast(F32), ALU.subtract).then_inc(s_bl, 1)
            body((0, 0))
            with dve.Fori(0, B // 2 - 1) as i:
                body((i, 1), True, (i, 0))
                body((i + 1, 0), True, (i, 1))
            body((B // 2 - 1, 1), False, (B // 2 - 1, 0))
            y_low((B // 2 - 1, 1))

        @block.gpsimd
        def _(pool):
            def times_n(b, m):
                q = b[1]
                if m == 0:
                    pool.wait_ge(d_n[q], b[0] * 16 + 16)
                pool.wait_ge(s_S, cnt(b, C, m + 1))
                nc.gpsimd.tensor_tensor(U[q][:, m, :], nin[q][:, m, :], Sb[:, m % 2, :], ALU.mult).then_inc(s_u, 1)

            def add_P(b, m):
                q = b[1]
                if m == 0:
                    pool.wait_ge(d_x[q], b[0] * 16 + 16)
                pool.wait_ge(s_P, cnt(b, C, m + 1))
                nc.gpsimd.tensor_tensor(X[q][:, m, :], xin[q][:, m, :], Pb[:, m % 2, :], ALU.add).then_inc(s_xp, 1)

            def x3_low(b, m):
                pool.wait_ge(s_x3h, cnt(b, C, m + 1))
                nc.gpsimd.tensor_tensor(x3lo[b[1]][:, m, :], X[b[1]][:, m, :], x3hi[b[1]][:, m, :].bitcast(F32), ALU.subtract).then_inc(s_lowp, 1)

            def body(b, ahead=True, before=None):
                if before:
                    pool.wait_ge(s_x3, cnt(before, C, C))
                    pool.wait_ge(s_lowd, cnt(before, 1, 1))
                for m in range(C):
                    if ahead:
                        times_n(nxt(b), m)
                        add_P(nxt(b), m)
                    if m != LOW_BY_DVE:
                        x3_low(b, m)

            for m in range(C):
                times_n((0, 0), m)
                add_P((0, 0), m)
            pool.wait_ge(s_bl, C)
            body((0, 0))
            with pool.Fori(0, B // 2 - 1) as i:
                body((i, 1), True, (i, 0))
                body((i + 1, 0), True, (i, 1))
            body((B // 2 - 1, 1), False)

        @block.scalar
        def _(act):
            def free(b):
                act.wait_ge(s_op, cnt(b, NT, NT))

            def x3_high(b, m):
                act.wait_ge(s_x3, cnt(b, C, m + 1))
                nc.scalar.copy(x3hi[b[1]][:, m, :], X[b[1]][:, m, :]).then_inc(s_x3h, 1)

            def factor_high(b):
                act.wait_ge(d_xb[b[1]], b[0] * 48 + 48)
                nc.scalar.copy(xbs[b[1]][:], xbr[b[1]][:]).then_inc(s_xbh, 1)

            def factor_groups(b):
                nc.scalar.copy(xag[b[1]][:].rearrange("p c (g r) -> p c g r", r=GRP)[:, :, :, 0:PAIR],
                               xa[:, :, bass.ds(number(b), 1), :].to_broadcast([P, C, 3, PAIR])).then_inc(s_xag, 1)

            def y_high(b):
                act.wait_ge(s_yp, cnt(b, 1, 1))
                nc.scalar.copy(ys[b[1]][:], yp[b[1]][0:YR, :]).then_inc(s_yh, 1)

            def put_out(b, t):
                act.wait_ge(s_op, cnt(b, NT, 2 * NT + t + 1))
                act.wait_ge(d_out[t], number(b) * 16 + 16)
                nc.scalar.copy(oout[:, t, :], outp[t][:]).then_inc(s_o, 1)

            def body(b, behind=None):
                free(b)
                factor_groups(b)
                factor_high(b)
                if behind:
                    y_high(behind)
                for m in range(C):
                    x3_high(b, m)
                    if behind:
                        put_out(behind, m)

            act.wait_ge(s_xat, 1)
            nc.scalar.copy(xa[:, :, :, 0:RANK], xat[:].rearrange("p c r b -> p c b r")).then_inc(s_xah, 1)
            act.wait_ge(s_yl, 2)
            act.wait_ge(s_xal, 1)
            for m in range(C):
                act.wait_ge(s_b2, m + 1)
                nc.scalar.copy(bhi[:, m, :], braw[:, m, :]).then_inc(s_bh, 1)
            body((0, 0))
            with act.Fori(0, B // 2 - 1) as i:
                body((i, 1), (i, 0))
                body((i + 1, 0), (i, 1))
            body((B // 2 - 1, 1), (B // 2 - 1, 0))
            y_high((B // 2 - 1, 1))
            for t in range(NT):
                put_out((B // 2 - 1, 1), t)

        @block.tensor
        def _(pe):
            def product(b, t):
                q = b[1]
                pe.wait_ge(s_o, cnt(b, NT, t + 1))
                tok = slice(t * P, (t + 1) * P)
                for m in range(C):
                    for e, (a, w) in enumerate(((x3hi[q], bhi), (x3lo[q], bhi), (x3hi[q], blo))):
                        nc.tensor.matmul(outp[t][:], a[:, m, tok], w[:, m, :], start=(m == 0 and e == 0), stop=False)

            def low_rank(b, t):
                q = b[1]
                nc.tensor.matmul(outp[t][:], ys[q][:, t * P:(t + 1) * P], xbs[q][:], start=False, stop=True).then_inc(s_op, 1)

            for c in range(C):
                last = nc.tensor.transpose(xat[:, c].rearrange("p r b -> p (r b)"), XA[:, c * P:(c + 1) * P], ident[:])
            last.then_inc(s_xat, 1)
            pe.wait_ge(s_bl, C)
            with pe.Fori(0, B // 2) as i:
                for q in range(2):
                    b = (i, q)
                    pe.wait_ge(s_xag, cnt(b, 1, 1))
                    pe.wait_ge(s_x3h, cnt(b, C, C))
                    pe.wait_ge(s_lowp, cnt(b, C - 1, C - 1))
                    pe.wait_ge(s_lowd, cnt(b, 1, 1))
                    pe.wait_ge(s_yl, cnt(b, 1, 1))
                    for m in range(C):
                        for a in (x3hi, x3lo):
                            last = nc.tensor.matmul(yp[q][0:YR, :], xag[q][:, m, 0:YR],
                                                    a[q][:, m, :], start=(m == 0 and a is x3hi), stop=(m == C - 1 and a is x3lo))
                    last.then_inc(s_yp, 1)
                    product(b, 0)
                    product(b, 1)
                    pe.wait_ge(s_yl, cnt(b, 1, 3))
                    pe.wait_ge(s_xbl, cnt(b, 1, 1))
                    low_rank(b, 0)
                    low_rank(b, 1)
                    for t in range(2, NT):
                        product(b, t)
                        low_rank(b, t)


_INS = ['x', 'cond_1024', 'L0_cond_W1', 'L0_cond_b1', 'L0_cond_W2', 'L0_cond_b2', 'L1_cond_Wx', 'L1_cond_Wh', 'L1_cond_b',
        'L2_cond_W_f', 'L2_cond_b_f', 'L2_cond_W_i', 'L2_cond_b_i', 'L2_cond_W_h', 'L2_cond_b_h', 'L3_cond_base_layer',
        'L3_cond_w1', 'L3_cond_b1', 'L3_cond_w2', 'L3_cond_b2', 'L3_cond_ln_g', 'L3_cond_ln_b']


def kernel(**inputs):
    import numpy as _np
    import concourse.bacc as _bacc
    from concourse import mybir as _mybir
    from concourse.bass_utils import run_bass_kernel_spmd as _run

    nc = _bacc.Bacc("TRN2", target_bir_lowering=False, num_devices=1)
    arrays, args = {}, []
    for name in _INS:
        a = _np.ascontiguousarray(inputs[name])
        arrays[f"in_{name}"] = a
        args.append(nc.dram_tensor(f"in_{name}", a.shape, _mybir.dt.from_np(a.dtype), kind="ExternalInput").ap())
    args.append(nc.dram_tensor("out_0", (B, T, D), F32, kind="ExternalOutput").ap())
    build(nc, *args)
    r = _run(nc, [arrays], core_ids=[0])
    return r.results[0]["out_0"]
```

```python
from contextlib import ExitStack

import concourse.bass as bass
from concourse import mybir

P = 128
B, T, D = 16, 512, 512
C = D // P
TS = 32
NBLK = T // TS
TOK = B * TS
RANK = 8
PADB = 32
PAIR = 2 * RANK
GRP = 32
LOW_BY_DVE = 3
EPS2 = 1e-8
LN_EPS = 1e-5
PIECES = 8
PW = TOK // PIECES
STAGE = 8
F32, F32R, F16, I32 = mybir.dt.float32, mybir.dt.float32r, mybir.dt.float16, mybir.dt.int32
ALU, ACT, AX = mybir.AluOpType, mybir.ActivationFunctionType, mybir.AxisListType


HEAD = 4
QUOTA = 6
GM = 3 * C
GROUPS = [("x", 0), ("x", 1), ("x", 2), ("x", 3), ("f", 0), ("i", 0), ("f", 1), ("i", 1), ("c", 0), ("f", 2), ("i", 2), ("c", 1),
          ("f", 3), ("i", 3), ("c", 2), ("c", 3)]
LAST_GROUPS = [("f", 0), ("i", 0), ("f", 1), ("i", 1), ("c", 0), ("f", 2), ("i", 2), ("c", 1), ("f", 3), ("i", 3), ("c", 2), ("c", 3)]
TR_STEP = 8
ACT_WORK = {1: [("x2h", 0), ("x2h", 1)], 2: [("x2h", 2), ("x2h", 3)], 3: [("x", 0), ("g", 3)], 4: [("x", 1)], 6: [("x", 2), ("mv", 0)],
            7: [("mv", 1)], 8: [("x", 3), ("mv", 2)], 9: [("mv", 3)], 10: [("f", 0)], 12: [("i", 0)], 13: [("x1h", 0)], 14: [("f", 1)],
            16: [("i", 1)], 17: [("x1h", 1)], 19: [("g", 0)], 20: [("f", 2)], 21: [("x1h", 2)], 22: [("i", 2)], 23: [("g", 1)],
            25: [("x1h", 3)], 26: [("f", 3)], 28: [("i", 3)], 29: [("g", 2)]}
DVE_EARLY = {0: [("r", 3, 6)], 14: [("r", 0, 0)], 15: [("r", 0, 3)], 16: [("r", 0, 6)], 18: [("r", 1, 0)], 19: [("r", 1, 3)],
             20: [("r", 1, 6)], 24: [("r", 2, 0)], 25: [("r", 2, 2)], 26: [("r", 2, 5)], 30: [("r", 3, 0)], 31: [("r", 3, 3)]}
DVE_LATE = {0: [("r", 3, 7)], 1: [("n", 2)], 3: [("n", 3)], 12: [("x1", 0)], 13: [("s", 0)], 14: [("r", 0, 1), ("r", 0, 2)],
            15: [("r", 0, 4), ("r", 0, 5)], 16: [("x1", 1), ("r", 0, 7)], 17: [("s", 1)], 18: [("r", 1, 1), ("r", 1, 2)],
            19: [("r", 1, 4), ("r", 1, 5)], 20: [("x1", 2), ("r", 1, 7)], 21: [("n", 0)], 23: [("s", 2)],
            24: [("x1", 3), ("r", 2, 1)], 25: [("r", 2, 3), ("r", 2, 4)], 26: [("r", 2, 6), ("r", 2, 7)], 27: [("n", 1)], 29: [("s", 3)],
            30: [("r", 3, 1), ("r", 3, 2)], 31: [("r", 3, 4), ("r", 3, 5)]}


W_PIECES = 3 * C
X_STEP, X_QUOTA = 11, 3
UNITS = {8: 0, 10: 1, **{14 + 5 * (u - 2) // 4: u for u in range(2, 4 * C)}}
ACT_FIRST = {t: [("w", t - 1)] for t in range(1, W_PIECES + 1)}
for _step, _work in ((2, ("x1h1", 0)), (3, ("x1h1", 1)), (4, ("x1h1", 2)), (5, ("x1h1", 3)), (7, ("mv", 0)), (8, ("mv", 1)), (9, ("mv", 2)),
                     (10, ("mv", 3)), (15, ("x", 0)), (19, ("x", 1)), (23, ("x", 2)), (27, ("x", 3)), (27, ("x1h", 0)), (28, ("x1h", 1)),
                     (29, ("x1h", 2)), (30, ("x1h", 3))):
    ACT_FIRST.setdefault(_step, []).append(_work)
DVE_FIRST_EARLY = {m + 1: [("x11", m)] for m in range(C)}
DVE_FIRST_LATE = {t: [("w", t - 2)] for t in range(2, W_PIECES + 2)}
for _step, _work in ((3, ("hgT",)), (12, ("x1", 0)), (16, ("l", 0)), (17, ("x1", 1)), (20, ("x1", 2)), (21, ("l", 1)), (24, ("x1", 3)), (26, ("l", 2)), (31, ("l", 3))):
    DVE_FIRST_LATE.setdefault(_step, []).append(_work)
DVE_SECOND_LATE = {3: [("lout",)]}


def build(nc, x, cond, W1, b1, W2, b2, Wx, Wh, bx, Wf, bf, Wi, bi, Wc, bc, base, w1, c1, w2, c2, ln_g, ln_b, out):
    with ExitStack() as keep:
        def sb(name, shape, dt=F32):
            return keep.enter_context(nc.sbuf_tensor(name, shape, dt))

        ident = sb("ident", [P, P])
        condT = sb("condT", [P, C, PADB])
        x2_d, g_d, n_d = (nc.dram_tensor(s, [B, P, C, T], F32, kind="Internal").ap() for s in ("x2_d", "g_d", "n_d"))
        xa_d = nc.dram_tensor("xa_d", [RANK, B, D], F32, kind="Internal").ap()
        xb_d = nc.dram_tensor("xb_d", [B, 2 * RANK, D], F32, kind="Internal").ap()
        xnat = sb("xnat", [P, C, D])
        xnew = sb("xnew", [P, C, TOK])
        xt0 = sb("xt0", [P, C, TOK])
        xw = [sb(f"xw{q}", [P, TS, C, B]) for q in range(2)]
        hbuf = sb("hbuf", [P, TS, C, B])
        wx_hi, wx_lo = sb("wx_hi", [P, C, D], F32R), sb("wx_lo", [P, C, D], F32R)
        U0, X0 = sb("U0", [P, C, T]), sb("X0", [P, C, T])
        Sb, Pb = sb("Sb", [P, 2, T]), sb("Pb", [P, 2, T])
        const = sb("const", [P, 2])
        xar = sb("xar", [P, D])
        gin, nin, xin, braw = [xnew[:], by_chunk(hbuf)], [by_chunk(xw[0]), by_chunk(xw[1])], [xt0[:], xnat[:]], xnat[:]
        bhi, blo = wx_hi, wx_lo
        wf_hi, wf_lo = sb("wf_hi", [P, C, D], F32R), sb("wf_lo", [P, C, D], F32R)
        x3hi0, x3lo0 = wf_hi, wf_lo
        xa = sb("xa", [P, C, B, PAIR], F32R)
        xag = [sb(f"xag{q}", [P, C, 3 * GRP], F32R) for q in range(2)]
        d_x2, d_last, d_xa = (keep.enter_context(nc.semaphore(s)) for s in ("d_x2", "d_last", "d_xa"))
        s_P, s_S, s_u, s_xp, s_H, s_x3, s_x3h, s_lowd, s_lowp, s_xag = (
            keep.enter_context(nc.semaphore("s_" + s)) for s in "P S u xp H x3 x3h lowd lowp xag".split())
        one, zero = (const[:, e:e + 1].to_broadcast([P, T]) for e in range(2))
        recurrence(nc, locals())
        tail(nc, locals())


def by_chunk(steps):
    return steps[:].rearrange("p t c b -> p (t c b)").rearrange("p (c d) -> p c d", c=C)


def recurrence(nc, v):
    x, ident, condT = v["x"], v["ident"], v["condT"]
    x2_d, g_d, n_d, xa_d, xb_d = (v[k] for k in "x2_d g_d n_d xa_d xb_d".split())
    xnat, xnew, xw, hbuf, gin, nin, xin, braw, bhi, blo = (v[k] for k in "xnat xnew xw hbuf gin nin xin braw bhi blo".split())
    xar, xa, xag, x3hi0, x3lo0, d_xa = (v[k] for k in "xar xa xag x3hi0 x3lo0 d_xa".split())
    s_P, s_S, s_u, s_bx, s_H, s_x3, s_x3h, s_lowx, s_lowp, s_xag = (
        v["s_" + k] for k in "P S u xp H x3 x3h lowd lowp xag".split())
    U0, X0, Sb, Pb, const, one, zero = (v[k] for k in "U0 X0 Sb Pb const one zero".split())
    with ExitStack() as ctx:
        def sb(name, shape, dt=F32):
            return ctx.enter_context(nc.sbuf_tensor(name, shape, dt))

        def ps(name, shape):
            return ctx.enter_context(nc.psum_tensor(name, shape, F32))

        def sem(name):
            return ctx.enter_context(nc.semaphore(name))

        split = {k: (sb(f"{k}_hi", [P, C, D], F32R), sb(f"{k}_lo", [P, C, D], F32R)) for k in "ic"}
        split["f"] = v["wf_hi"], v["wf_lo"]
        split["x"] = v["wx_hi"], v["wx_lo"]
        wh_hi, wh_lo = (b[:].bitcast(F16).rearrange("p e (f d) -> p (e f) d", d=D) for b in (Sb, Pb))
        whs = sb("whs", [P, 4])
        sbx = sb("sbx", [P, C])
        bias = {k: sb(f"bias_{k}", [P, C]) for k in "fic"}
        h0wh = sb("h0wh", [P, C, B])
        gate2 = sb("gate2", [P, C, B])
        xt = [v["xt0"], U0]
        with ExitStack() as late:
            g_last, n_last = (late.enter_context(nc.sbuf_tensor(s, [P, C, TOK], F32)) for s in ("g_last", "n_last"))
        x1hi, x1lo = sb("x1hi", [P, C, TOK], F32R), sb("x1lo", [P, C, TOK], F32R)
        with ExitStack() as early:
            stage = [early.enter_context(nc.sbuf_tensor(f"stage{e}", [P, C, D], F32)) for e in range(2)]
        x2hi, x2lo = sb("x2hi", [P, C, TOK], F32R), sb("x2lo", [P, C, TOK], F32R)
        hs = sb("hs", [P, C, 2, B], F16)
        pre0, pre = sb("pre0", [P, C, B]), sb("pre", [P, C, B])
        gates, gn = sb("gates", [P, 6, TOK]), X0
        fbuf, ibuf, rbuf = gates[:, 0:2], gates[:, 2:4], gates[:, 4:6]
        gst, nst = gn[:, 0:2], gn[:, 2:4]
        warm = sb("warm", [P, 1])
        bank = [ps(f"bank{i}", [P, TOK]) for i in range(4)]
        trb = [ps(f"trb{i}", [P, TOK]) for i in range(2)]
        recb, aux = ps("recb", [P, TOK]), ps("aux", [P, TOK])
        rec = recb[:, 0:C * 2 * B].rearrange("p (c a b) -> p c a b", c=C, a=2)
        turned = recb[:, 2 * P:3 * P]
        lrp = [aux, bank[0], aux, bank[1]]
        z3 = trb[0][:, 0:P]
        xat = aux[:].rearrange("p (c r b) -> p c r b", c=C, r=RANK)
        z = aux[:, 0:P]
        cols = aux[:, P:P + C * B].rearrange("p (c b) -> p c b", c=C)

        def flat(view):
            return view.rearrange("p c d -> p (c d)")

        raw = {"1": by_chunk(hbuf), "2": by_chunk(xw[1]), "f": stage[0][:], "i": stage[1][:],
               "c": gates[:, 0:C]}
        wT1, wT2, wx, wh, w1h = xt[1][:], gn[:], xt[0][:], gates[:, 0:C], by_chunk(xw[1])
        ring = [flat(stage[0][:]), flat(stage[1][:]), flat(gates[:, 0:C])]
        c2s = gn
        lr = [rbuf[:, e, :].rearrange("p (r d) -> p r d", r=RANK) for e in range(2)]
        crow = xar[0:B, :]
        cent, ae = sb("cent", [B, D]), sb("ae", [B, D])
        ln_rows = xa[0:B].bitcast(F32).rearrange("p c b r -> p (c b r)")
        lng, lnb = ln_rows[:, 0:D], ln_rows[:, D:2 * D]
        row = sb("row", [1, 3, D])
        ones = sb("ones", [1, PADB])
        stat = sb("stat", [B, 4])
        aeT = sb("aeT", [P, C, PADB])
        sg, hg, zs = (sb(s, [P, P]) for s in ("sg", "hg", "zs"))
        hT, hgT = sb("hT", [P, C, PADB]), sb("hgT", [P, C, PADB])

        (d_cond, d_w1, d_w2, d_wx, d_wh, d_f, d_i, d_c, d_rows, d_ln, d_h1, d_bias, d_c2) = (
            sem("p_" + s) for s in "d_cond d_w1 d_w2 d_wx d_wh d_f d_i d_c d_rows d_ln d_h1 d_bias d_c2".split())
        d_ring, d_lr = [sem(f"p_d_ring{e}") for e in range(3)], [sem(f"p_d_lr{e}") for e in range(2)]
        (s_id, s_one, s_pad, s_cols, s_colsT, s_wt, s_w1T, s_w1Tv, s_w2T, s_w2Tv, s_z, s_zc, s_v, s_sg, s_turn, s_turned, s_ln, s_ae,
         s_mx, s_amx, s_wh, s_wxh, s_wxl, s_wt3, s_w3h, s_w3l, s_hyp, s_lr) = (
            sem("p_" + s) for s in ("s_id s_one s_pad s_cols s_colsT s_wt s_w1T s_w1Tv s_w2T s_w2Tv s_z s_zc s_v s_sg s_turn s_turned s_ln s_ae "
                                    "s_mx s_amx s_wh s_wxh s_wxl s_wt3 s_w3h s_w3l s_hyp s_lr").split())
        d_x2, d_last = v["d_x2"], v["d_last"]
        d_early0, d_early = ([sem(f"r_d_early{b}{n}") for n in range(3)] for b in range(2))
        s_gc, s_nc, s_xc, s_xag0, s_xat, s_xah, s_xal, s_bl = (sem("r_" + s) for s in "s_gc s_nc s_xc s_xag0 s_xat s_xah s_xal s_bl".split())
        d_x, d_base = (sem("r_" + s) for s in "d_x d_base".split())
        s_b2, s_bh, s_lowd = (sem("r_" + s) for s in "s_b2 s_bh s_lowd".split())
        d_g, d_n = ([sem(f"r_d_{s}{e}") for e in range(2)] for s in "gn")
        (s_tr, s_x1, s_x1h, s_x1l, s_mv, s_xp, s_xw, s_rec, s_pre0, s_pre, s_h, s_hs, s_x2, s_x2h, s_x2l, s_f, s_i, s_c, s_fs, s_is,
         s_gs, s_r, s_fr, s_in, s_g, s_n, s_h0) = (
            sem("r_" + s) for s in ("s_tr s_x1 s_x1h s_x1l s_mv s_xp s_xw s_rec s_pre0 s_pre s_h s_hs s_x2 s_x2h s_x2l s_f s_i s_c s_fs s_is "
                                    "s_gs s_r s_fr s_in s_g s_n s_h0").split())
        UP = C

        def cnt(j, per, pos):
            i, q = j
            return i * (2 * per) + (q * per + pos)

        def nxt(j):
            return (j[0], 1) if j[1] == 0 else (j[0] + 1, 0)

        def prv(j):
            return (j[0], 0) if j[1] == 1 else (j[0] - 1, 1)

        FIRST, LAST = (0, 0), (NBLK // 2 - 1, 1)

        def first(j, n=0):
            return isinstance(j[0], int) and 2 * j[0] + j[1] == n

        block = ctx.enter_context(nc.Block())

        @block.sync
        def _(sp):
            def load_x(t0):
                for a in range(C):
                    sp.dma_start(xnat[:, a, :], x[a * P // TS:(a + 1) * P // TS, bass.ds(t0, TS), :]).then_inc(d_x, 16)

            def spill(dst, src, b, m, done):
                sp.dma_start(dst[:, :, m, bass.ds(b[0] * (2 * TS) + b[1] * TS, TS)].rearrange("b p t -> p b t"),
                             src.rearrange("p (b t) -> p b t", t=TS)).then_inc(done, 16)

            def spill_x2(b):
                sp.wait_ge(s_x2, cnt(b, C, C))
                for m in range(C):
                    spill(x2_d, xt[b[1]][:, m, :], b, m, d_x2)

            def spill_gn(b, m):
                sp.wait_ge(s_g, cnt(b, C, UP + m + 1))
                spill(g_d, gst[:, m % 2, :], b, m, d_g[m % 2])
                sp.wait_ge(s_n, cnt(b, C, UP + m + 1))
                spill(n_d, nst[:, m % 2, :], b, m, d_n[m % 2])

            def middle(j, ahead):
                for m in range(2):
                    spill_gn(prv(j), m)
                if ahead is not None:
                    sp.wait_ge(s_tr, cnt(nxt(nxt(j)), C, C))
                    load_x(ahead)

            def head(j):
                spill_x2(prv(j))
                for m in range(2, C):
                    spill_gn(prv(prv(j)), m)

            def weight(dst, src, done):
                sp.dma_start(dst, src.rearrange("(c p) d -> p c d", p=P)).then_inc(done, 16)

            def as_row(src):
                return src.rearrange("(a d) -> a d", a=1)

            def unit(u):
                g, k = u // C, u % C
                if u < 3:
                    sp.wait_ge(s_wt3, C * (u + 1))
                else:
                    sp.wait_ge(s_hyp, u - 2)
                sp.dma_start(ring[u % 3], v["w2"][k * P:(k + 1) * P, g * C * D:(g + 1) * C * D]).then_inc(d_ring[u % 3], 16)

            def factors_out(g):
                sp.wait_ge(s_lr, g + 1)
                for e in range(C):
                    src, d0 = lr[g % 2][e * PADB:e * PADB + B], (g % 2 * C + e) * (D // RANK)
                    if g < 2:
                        sp.dma_start(xa_d[:, :, d0:d0 + D // RANK].rearrange("r b d -> b r d"), src).then_inc(d_lr[g % 2], 16)
                    else:
                        for copy in range(2):
                            sp.dma_start(xb_d[:, copy * RANK:(copy + 1) * RANK, d0:d0 + D // RANK], src).then_inc(d_lr[g % 2], 16)

            sp.dma_start(crow, v["cond"]).then_inc(d_cond, 16)
            weight(raw["1"], v["W1"], d_w1)
            weight(raw["2"], v["W2"], d_w2)
            for n, k in enumerate(("b1", "b2", "c1")):
                sp.dma_start(row[:, n, :], as_row(v[k])).then_inc(d_rows, 16)
            weight(wx, v["Wx"], d_wx)
            for dst, k in ((lng, "ln_g"), (lnb, "ln_b")):
                sp.dma_start(dst, as_row(v[k]).to_broadcast([B, D])).then_inc(d_ln, 16)
            load_x(0)
            weight(wh, v["Wh"], d_wh)
            sp.dma_start(sbx[:], v["bx"].rearrange("(c p) -> p c", p=P), allow_slow_non_contiguous=True).then_inc(d_bias, 16)
            sp.wait_ge(s_wt, 2 * C)
            weight(w1h, v["w1"], d_h1)
            weight(raw["f"], v["Wf"], d_f)
            weight(raw["i"], v["Wi"], d_i)
            sp.wait_ge(s_tr, C)
            load_x(TS)
            sp.wait_ge(s_wh, 8)
            sp.wait_ge(s_z, 3)
            weight(raw["c"], v["Wc"], d_c)
            for k, w in (("f", "bf"), ("i", "bi"), ("c", "bc")):
                sp.dma_start(bias[k][:], v[w].rearrange("(c p) -> p c", p=P), allow_slow_non_contiguous=True).then_inc(d_bias, 16)
            for g in range(C):
                for e in range(C):
                    q = g * C + e
                    sp.dma_start(c2s[e * PADB:(e + 1) * PADB, g, :],
                                 as_row(v["c2"][q * D:(q + 1) * D]).to_broadcast([PADB, D])).then_inc(d_c2, 16)
            sp.wait_ge(s_tr, C * 2)
            load_x(2 * TS)
            for u in range(4 * C):
                unit(u)
                if u % C == C - 1 and u >= C:
                    factors_out(u // C - 1)
            sp.wait_ge(s_tr, C * 3)
            load_x(3 * TS)
            factors_out(C - 1)
            spill_x2(FIRST)
            with sp.Fori(0, NBLK // 2 - 2) as i:
                for j, ahead in (((i, 1), 4), ((i + 1, 0), 5)):
                    middle(j, i * (2 * TS) + ahead * TS)
                    head(nxt(j))
            i = NBLK // 2 - 2
            middle((i, 1), 0)
            head((i + 1, 0))
            middle((i + 1, 0), None)
            head(LAST)
            done2, done1 = T - 2 * TS, T - TS
            sp.wait_ge(s_x1l, C * (NBLK + 1))
            sp.wait_ge(d_x2, 16 * C * (NBLK - 1))
            sp.wait_ge(s_x2l, C * (NBLK - 1))
            for e in range(2):
                sp.wait_ge(d_g[e], 16 * (C // 2 * (NBLK - 2) + 1))
                sp.wait_ge(d_n[e], 16 * (C // 2 * (NBLK - 2) + 1))
                sp.wait_ge(d_lr[e], 16 * C * (e + 1))
            for n, (dst, src, end) in enumerate(((gin, g_d, done2), (nin, n_d, done2), (xin, x2_d, done1))):
                sp.dma_start(dst[0][:, :, 0:end], src[0, :, :, 0:end]).then_inc(d_early0[n], 16)
            weight(braw, v["base"], d_base)
            sp.dma_start(xar[:], xa_d.rearrange("r b d -> (r b) d")).then_inc(d_xa, 16)
            middle(LAST, None)
            spill_x2(LAST)
            for m in range(2, C):
                spill_gn(prv(LAST), m)
            for e in range(2):
                sp.wait_ge(d_g[e], 16 * (C // 2 * (NBLK - 1) + 1))
                sp.wait_ge(d_n[e], 16 * (C // 2 * (NBLK - 1) + 1))
            for n, (dst, src) in enumerate(((gin, g_d), (nin, n_d))):
                sp.dma_start(dst[0][:, :, done2:done1], src[0, :, :, done2:done1]).then_inc(d_early0[n], 16)
            for n, (dst, src) in enumerate(((gin, g_d), (nin, n_d))):
                sp.dma_start(dst[1][:, :, 0:done1], src[1, :, :, 0:done1]).then_inc(d_early[n], 16)
            sp.wait_ge(s_bl, C)
            sp.wait_ge(d_x2, 16 * C * NBLK)
            sp.dma_start(xin[1], x2_d[1]).then_inc(d_early[2], 16)
            for m in range(C):
                sp.wait_ge(s_g, cnt(LAST, C, UP + m + 1))
                spill(g_d, g_last[:, m, :], LAST, m, d_last)
                sp.wait_ge(s_n, cnt(LAST, C, UP + m + 1))
                spill(n_d, n_last[:, m, :], LAST, m, d_last)
            sp.wait_ge(d_x, 16 * C * (NBLK + 1))
            for e in range(2):
                sp.wait_ge(d_lr[e], 16 * C * 3)
            sp.wait_ge(d_bias, 64)
            sp.wait_ge(d_early[2], 16)

        @block.tensor
        def _(pe):
            def transpose(p, m, a):
                if m == 0 and a == 0:
                    pe.wait_ge(d_x, cnt(p, 16 * C, 16 * C))
                if a == 0 and (m >= 2 or not first(p)):
                    pe.wait_ge(s_x1, cnt(p, C, m - 1))
                done = nc.tensor.transpose(trb[m % 2][:, a * P:(a + 1) * P], xnat[:, a, m * P:(m + 1) * P], ident[:])
                if a == C - 1:
                    done.then_inc(s_tr, 1)

            def step(j, t):
                pe.wait_ge(s_hs, cnt(j, TS, t + 1))
                for k in range(C):
                    for m in range(C):
                        for w in (wh_hi, wh_lo):
                            last = nc.tensor.matmul(rec[:, m].rearrange("p a b -> p (a b)"), w[:, k, m * P:(m + 1) * P],
                                                    hs[:, k].rearrange("p a b -> p (a b)"),
                                                    start=(k == 0 and m == 0 and w is wh_hi), stop=(k == C - 1),
                                                    skip_group_check=True)
                last.then_inc(s_rec, 1)

            def left_by_pass(n, b):
                kind, m = GROUPS[3 * C + n]
                pe.wait_ge({"f": s_fs, "i": s_is, "c": s_n}[kind], cnt(b, C, m + 1))

            def bank_free(j, n, prep):
                b = prv(j) if not first(j) else None
                kind, m = GROUPS[n - 4]
                if n < 4:
                    if first(j):
                        pe.wait_ge(s_w3l, 2 * C + n + 1)
                    elif first(j, 1) and n < 2:
                        pe.wait_ge(s_lr, 2 * n + 2)
                    elif first(j, 1):
                        pe.wait_ge(s_xw, C + n + 1)
                    else:
                        left_by_pass(n, b)
                elif kind == "x" and (prep or m == 0):
                    pe.wait_ge(s_xw, cnt(nxt(j), C, m + 1))
                elif kind == "x":
                    left_by_pass(m, b)
                else:
                    pe.wait_ge({"f": s_fs, "i": s_is, "c": s_n}[kind], cnt(b, C, UP + m + 1))

            def group_mms(kind, m):
                hi, lo = split[kind]
                ahi, alo = (x1hi, x1lo) if kind == "x" else (x2hi, x2lo)
                return [(w[:, k, m * P:(m + 1) * P], a[:, k, :]) for k in range(C) for w, a in ((hi, ahi), (lo, ahi), (hi, alo))]

            def group_part(n, lo, hi, p, b):
                kind, m = GROUPS[n]
                if lo == 0:
                    if kind == "x":
                        pe.wait_ge(s_x1h, cnt(p, C, C))
                        pe.wait_ge(s_x1l, cnt(p, C, C))
                    else:
                        pe.wait_ge(s_x2h, cnt(b, C, C))
                        pe.wait_ge(s_x2l, cnt(b, C, C))
                mms = group_mms(kind, m)
                for e in range(lo, hi):
                    last = nc.tensor.matmul(bank[n % 4][:], mms[e][0], mms[e][1], start=(e == 0), stop=(e == GM - 1))
                if hi == GM:
                    last.then_inc({"x": s_xp, "f": s_f, "i": s_i, "c": s_c}[kind], 1)

            def weight_piece(n):
                k = "fic"[n // C]
                if n % C == 0:
                    pe.wait_ge({"f": d_f, "i": d_i, "c": d_c}[k], 16)
                if n < C:
                    pe.wait_ge(s_xw, C)
                else:
                    pe.wait_ge(s_w3l, n - C + 1)
                turn_weight(raw[k], n % C, bank[n % 4], s_wt3)

            def factor_piece(u):
                g, k = u // C, u % C
                pe.wait_ge(d_ring[u % 3], 16 * (u // 3 + 1))
                if u == 0:
                    pe.wait_ge(s_turned, 4)
                if k == 0 and g % 2:
                    pe.wait_ge(s_xw, C + g // 2 + 1)
                elif k == 0 and g:
                    pe.wait_ge(s_lr, g - 1)
                for e in range(C):
                    last = nc.tensor.matmul(lrp[g][e * PADB:(e + 1) * PADB, :], hgT[:, k, :], ring[u % 3][:, e * D:(e + 1) * D],
                                            start=(k == 0), stop=(k == C - 1), tile_position=(0, e * PADB))
                last.then_inc(s_hyp, 1)

            def first_block():
                at = 0
                for t in range(TS):
                    step(FIRST, t)
                    if t == 1:
                        pe.wait_ge(s_sg, 3)
                        nc.tensor.transpose(z, hg[:], ident[:]).then_inc(s_turn, 1)
                    if t < C:
                        for a in range(C):
                            transpose((0, 1), t, a)
                    if t < W_PIECES:
                        weight_piece(t)
                    if TR_STEP <= t < TR_STEP + C * C:
                        transpose((1, 0), (t - TR_STEP) // C, (t - TR_STEP) % C)
                    if t >= X_STEP and at < C * GM:
                        n, begin = at // GM, at % GM
                        if begin == 0:
                            bank_free(FIRST, n, True)
                        group_part(n, begin, begin + X_QUOTA, (0, 1), None)
                        at += X_QUOTA
                    if t in UNITS:
                        factor_piece(UNITS[t])

            def steps(j, lo, hi, l2=True, prep=True):
                b = prv(j) if not first(j) else None
                for t in range(lo, hi):
                    step(j, t)
                    if prep and TR_STEP <= t < TR_STEP + C * C:
                        transpose(nxt(nxt(j)), (t - TR_STEP) // C, (t - TR_STEP) % C)
                    at, end = t * QUOTA, (t + 1) * QUOTA
                    while at < end:
                        n, begin = at // GM, at % GM
                        upto = min(GM, begin + end - at)
                        if prep and GROUPS[n][0] == "x" or l2 and GROUPS[n][0] != "x":
                            if begin == 0:
                                bank_free(j, n, prep)
                            group_part(n, begin, upto, nxt(j), b)
                        at += upto - begin

            def rows_to_cols(src, n):
                if n:
                    pe.wait_ge(s_colsT, n)
                for c in range(C):
                    last = nc.tensor.transpose(cols[:, c, :], src[:, c * P:(c + 1) * P], ident[0:B, 0:B])
                last.then_inc(s_cols, 1)

            def turn_weight(src, c, dst, done):
                for r in range(C):
                    last = nc.tensor.transpose(dst[:, r * P:(r + 1) * P], src[:, r, c * P:(c + 1) * P], ident[:])
                last.then_inc(done, 1)

            def dense(lhs, w, n, z=z):
                for c in range(C):
                    for e in range(C):
                        last = nc.tensor.matmul(z[e * PADB:(e + 1) * PADB, :], lhs[:, c, :], w[:, c, e * P:(e + 1) * P],
                                                start=(c == 0), stop=(c == C - 1 and n is None), tile_position=(0, e * PADB))
                for e in range(C if n is not None else 0):
                    last = nc.tensor.matmul(z[e * PADB:(e + 1) * PADB, :], ones[:], row[:, n, e * P:(e + 1) * P],
                                            start=False, stop=True, tile_position=(0, e * PADB))
                last.then_inc(s_z, 1)

            def turn(src):
                nc.tensor.transpose(turned, src[:], ident[:]).then_inc(s_turn, 1)

            pe.wait_ge(s_id, 2)
            pe.wait_ge(d_cond, 16)
            rows_to_cols(crow, 0)
            pe.wait_ge(d_w1, 16)
            for c in range(C):
                turn_weight(raw["1"], c, bank[c], s_wt)
            pe.wait_ge(s_colsT, 1)
            pe.wait_ge(s_w1T, 2)
            pe.wait_ge(s_w1Tv, 2)
            pe.wait_ge(d_rows, 48)
            pe.wait_ge(s_one, 1)
            dense(condT, wT1, 0)
            pe.wait_ge(d_w2, 16)
            for c in range(C):
                turn_weight(raw["2"], c, bank[c], s_wt)
            pe.wait_ge(s_v, 1)
            turn(hg)
            pe.wait_ge(s_turned, 1)
            pe.wait_ge(s_w2T, 2)
            pe.wait_ge(s_w2Tv, 2)
            dense(hT, wT2, 1)
            pe.wait_ge(s_sg, 2)
            turn(sg)
            pe.wait_ge(s_ae, 1)
            rows_to_cols(ae, 1)
            for m in range(C):
                for a in range(C):
                    transpose(FIRST, m, a)
            pe.wait_ge(s_wxh, C)
            pe.wait_ge(s_wxl, C)
            for k in range(C):
                pe.wait_ge(s_x1h, k + 1)
                for m in range(C):
                    for e, w in enumerate(split["x"]):
                        nc.tensor.matmul(bank[m][:], w[:, k, m * P:(m + 1) * P], x1hi[:, k, :], start=(k == 0 and e == 0), stop=False)
            pe.wait_ge(d_wh, 16)
            pe.wait_ge(s_colsT, 2)
            dense(condT, wh, None)
            pe.wait_ge(d_h1, 16)
            pe.wait_ge(s_x1, C)
            dense(aeT, w1h, 2, z3)
            pe.wait_ge(s_x1l, C)
            for m in range(C):
                for k in range(C):
                    last = nc.tensor.matmul(bank[m][:], split["x"][0][:, k, m * P:(m + 1) * P], x1lo[:, k, :], start=False, stop=(k == C - 1))
                last.then_inc(s_xp, 1)
                if m == 1:
                    pe.wait_ge(s_zc, 1)
                    pe.wait_ge(s_turned, 2)
                    turn(zs)
            pe.wait_ge(s_sg, 3)
            pe.wait_ge(s_wh, 8)
            pe.wait_ge(s_turned, 3)
            first_block()
            steps((0, 1), 0, HEAD)
            with pe.Fori(0, NBLK // 2 - 1) as i:
                for j in ((i, 1), (i + 1, 0)):
                    steps(j, HEAD, TS)
                    steps(nxt(j), 0, HEAD)
            steps(LAST, HEAD, TS, prep=False)
            for n, (kind, m) in enumerate(LAST_GROUPS):
                if n < C:
                    left_by_pass(n, LAST)
                else:
                    before, chunk = LAST_GROUPS[n - C]
                    pe.wait_ge({"f": s_fs, "i": s_is, "c": s_n}[before], cnt(LAST, C, UP + chunk + 1))
                for e in range(2 * C):
                    if n == 0 and e % 2 == 0:
                        pe.wait_ge(s_x2h, cnt(LAST, C, e // 2 + 1))
                    nc.tensor.matmul(bank[n % 4][:], split[kind][e % 2][:, e // 2, m * P:(m + 1) * P], x2hi[:, e // 2, :], start=(e == 0), stop=False)
                if n == 0:
                    pe.wait_ge(s_x2l, cnt(LAST, C, C // 2))
                    pe.wait_ge(s_lowd, C // 2)
                for k in range(C):
                    last = nc.tensor.matmul(bank[n % 4][:], split[kind][0][:, k, m * P:(m + 1) * P], x2lo[:, k, :], start=False, stop=(k == C - 1))
                last.then_inc({"f": s_f, "i": s_i, "c": s_c}[kind], 1)
            pe.wait_ge(d_xa, 16)
            for c in range(C):
                last = nc.tensor.transpose(xat[:, c].rearrange("p r b -> p (r b)"), xar[:, c * P:(c + 1) * P], ident[:])
            last.then_inc(s_xat, 1)

        @block.scalar
        def _(act):
            unscale = act.alloc_register("unscale")

            def sigmoid_table():
                nc.scalar.activation(warm[:], ident[:, 0:1], ACT.Sigmoid)

            def tanh(j, t):
                act.wait_ge(s_pre, cnt(j, TS, t + 1))
                if t % STAGE == 0 and not first(j):
                    act.wait_ge(s_x2, cnt(prv(j), C, t // STAGE + 1))
                nc.scalar.activation(hs[:, :, 0, :], pre[:], ACT.Tanh, scale=unscale).then_inc(s_h, 1)
                nc.scalar.activation(hbuf[:, t], pre[:], ACT.Tanh, scale=unscale).then_inc(s_h, 1)

            def x1_high(p, m):
                act.wait_ge(s_x1, cnt(p, C, m + 1))
                if not first(p):
                    act.wait_ge(s_xp, cnt(prv(p), C, C))
                nc.scalar.copy(x1hi[:, m, :], xnew[:, m, :]).then_inc(s_x1h, 1)

            def move(p, m):
                if not first(p) and not first(p, 1):
                    act.wait_ge(d_x2, cnt(p, 16 * C, -16 * C))
                    act.wait_ge(s_x2l, cnt(p, C, -C))
                act.wait_ge(s_x1, cnt(p, C, m + 1))
                nc.scalar.copy(xt[p[1]][:, m, :], xnew[:, m, :]).then_inc(s_mv, 1)

            def x2_high(b, m):
                act.wait_ge(s_x2, cnt(b, C, C))
                act.wait_ge(s_c, cnt(b, C, C))
                nc.scalar.copy(x2hi[:, m, :], xt[b[1]][:, m, :]).then_inc(s_x2h, 1)

            def input_products(p, m):
                act.wait_ge(s_xp, cnt(p, C, m + 1))
                nc.scalar.activation(xw[p[1]][:, :, m, :].rearrange("p t b -> p b t"), bank[m][:].rearrange("p (b t) -> p b t", t=TS),
                                     ACT.Identity, bias=sbx[:, m:m + 1], scale=whs[:, 2:3]).then_inc(s_xw, 1)

            def gate(b, kind, m, n=None):
                n = GROUPS.index((kind, m)) if n is None else n
                made, done, buf = (s_f, s_fs, fbuf) if kind == "f" else (s_i, s_is, ibuf)
                act.wait_ge(made, cnt(b, C, m + 1))
                act.wait_ge(s_g if kind == "f" else s_n, cnt(b, C, UP + m - 1))
                nc.scalar.activation(buf[:, m % 2, :], bank[n % 4][:], ACT.Sigmoid, bias=bias[kind][:, m:m + 1]).then_inc(done, 1)

            def forget_share(b, m):
                act.wait_ge(s_fr, cnt(b, C, UP + m + 1))
                if first(b, NBLK - 1):
                    dst = g_last[:, m, :]
                else:
                    act.wait_ge(d_g[m % 2], cnt(b, 16 * C // 2, 16 * (m // 2) + 16))
                    dst = gst[:, m % 2, :]
                nc.scalar.activation(dst, fbuf[:, m % 2, :], ACT.Copy, bias=EPS2).then_inc(s_g, 1)

            def weight_high(n):
                act.wait_ge(s_wt3, n + 1)
                nc.scalar.copy(split["fic"[n // C]][0][:, n % C, :], bank[n % 4][:]).then_inc(s_w3h, 1)

            def first_block():
                for t in range(TS):
                    tanh(FIRST, t)
                    for kind, m in ACT_FIRST.get(t, []):
                        if kind == "w":
                            weight_high(m)
                        elif kind == "x1h1":
                            x1_high((0, 1), m)
                        elif kind == "x1h":
                            x1_high((1, 0), m)
                        elif kind == "mv":
                            move((0, 1), m)
                        else:
                            input_products((0, 1), m)

            def steps(j, lo, hi, l2=True, prep=True):
                b = prv(j) if not first(j) else None
                for t in range(lo, hi):
                    tanh(j, t)
                    for kind, m in ACT_WORK.get(t, []):
                        if kind == "x1h" and prep:
                            x1_high(nxt(nxt(j)), m)
                        elif kind == "mv" and prep:
                            move(nxt(j), m)
                        elif kind == "x" and prep:
                            input_products(nxt(j), m)
                        elif kind == "x2h" and not first(j):
                            x2_high(b, m)
                        elif kind in ("f", "i") and l2:
                            gate(b, kind, m)
                        elif kind == "g" and t < HEAD and l2 and not first(j):
                            forget_share(prv(b), m)
                        elif kind == "g" and t >= HEAD and l2:
                            forget_share(b, m)

            act.wait_ge(s_ln, 2)
            nc.scalar.activation(ae[:], cent[:], ACT.Square, accum_out=stat[:, 1:2]).then_inc(s_ln, 1)
            act.wait_ge(s_ln, 4)
            nc.scalar.activation(stat[:, 3:4], stat[:, 2:3], ACT.Sqrt).then_inc(s_ln, 1)
            for c in (0, 2):
                act.wait_ge(s_wt, c + 1)
                nc.scalar.copy(wT1[:, c, :], bank[c][:]).then_inc(s_w1T, 1)
            act.wait_ge(s_z, 1)
            nc.scalar.activation(sg[:], z, ACT.Sigmoid).then_inc(s_sg, 1)
            for c in (0, 2):
                act.wait_ge(s_wt, C + c + 1)
                nc.scalar.copy(wT2[:, c, :], bank[c][:]).then_inc(s_w2T, 1)
            act.wait_ge(d_wx, 16)
            for c in range(C):
                nc.scalar.copy(split["x"][0][:, c, :], wx[:, c, :]).then_inc(s_wxh, 1)
            act.wait_ge(s_z, 2)
            act.wait_ge(s_v, 1)
            nc.scalar.activation(sg[:], z, ACT.Sigmoid).then_inc(s_sg, 1)
            for m in range(C):
                x1_high(FIRST, m)
            act.wait_ge(s_wxl, C)
            for m in range(C):
                move(FIRST, m)
            act.wait_ge(s_z, 4)
            act.wait_ge(s_turned, 1)
            nc.scalar.activation(hg[:], z3, ACT.Gelu).then_inc(s_sg, 1)
            sigmoid_table()
            act.wait_ge(s_wh, 8)
            act.reg_load(unscale, whs[0:1, 3:4].bitcast(I32))
            for m in range(C):
                input_products(FIRST, m)
            act.wait_ge(d_bias, 64)
            first_block()
            steps((0, 1), 0, HEAD, l2=False)
            with act.Fori(0, NBLK // 2 - 1) as i:
                sigmoid_table()
                for j in ((i, 1), (i + 1, 0)):
                    steps(j, HEAD, TS)
                    steps(nxt(j), 0, HEAD)
            sigmoid_table()
            steps(LAST, HEAD, TS, prep=False)
            for m in range(C):
                x2_high(LAST, m)
            for c in range(C):
                act.wait_ge(s_b2, c + 1)
                nc.scalar.copy(bhi[:, c, :], braw[:, c, :]).then_inc(s_bh, 1)
            forget_share(prv(LAST), C - 1)

            def last_cols(m):
                act.wait_ge(s_g, UP + C * (NBLK - 1) + m + 1)
                nc.scalar.copy(gin[0][:, m, T - TS:], g_last[:, m, 0:TS]).then_inc(s_gc, 1)

            def x3_high(m):
                act.wait_ge(s_x3, m + 1)
                nc.scalar.copy(x3hi0[:, m, :], X0[:, m, :]).then_inc(s_x3h, 1)

            for kind, m in LAST_GROUPS[:-2]:
                if kind != "c":
                    gate(LAST, kind, m, LAST_GROUPS.index((kind, m)))
                if kind == "i" and m:
                    forget_share(LAST, m - 1)
                    if m == 1:
                        act.wait_ge(d_early0[0], 32)
                    last_cols(m - 1)
            act.wait_ge(s_f, C * NBLK)
            x3_high(0)
            act.wait_ge(s_xat, 1)
            nc.scalar.copy(xa[:, :, :, 0:RANK], xat.rearrange("p c r b -> p c b r")).then_inc(s_xah, 1)
            forget_share(LAST, C - 1)
            last_cols(C - 1)
            act.wait_ge(d_early[0], 16)
            nc.scalar.copy(gin[1][:, :, T - TS:], g_last[:, :, TS:2 * TS])
            x3_high(1)
            act.wait_ge(s_xag0, 2)
            act.wait_ge(s_xal, 1)
            nc.scalar.copy(xag[0][:].rearrange("p c (g r) -> p c g r", r=GRP)[:, :, :, 0:PAIR],
                           xa[:, :, 0:1, :].to_broadcast([P, C, 3, PAIR])).then_inc(s_xag, 1)
            x3_high(2)
            x3_high(3)

        @block.gpsimd
        def _(pool):
            def x1_low(p, m):
                pool.wait_ge(s_x1h, cnt(p, C, m + 1))
                nc.gpsimd.tensor_tensor(x1lo[:, m, :], xnew[:, m, :], x1hi[:, m, :].bitcast(F32), ALU.subtract).then_inc(s_x1l, 1)

            def x2_low(b, m):
                pool.wait_ge(s_x2h, cnt(b, C, m + 1))
                nc.gpsimd.tensor_tensor(x2lo[:, m, :], xt[b[1]][:, m, :], x2hi[:, m, :].bitcast(F32), ALU.subtract).then_inc(s_x2l, 1)

            def add_h(j, s):
                pool.wait_ge(s_h, cnt(j, 2 * TS, 2 * STAGE * (s + 1)))
                if s == 0:
                    pool.wait_ge(s_mv, cnt(j, C, C))
                xs = xt[j[1]][:].rearrange("p c (b t) -> p c b t", t=TS)[:, :, :, s * STAGE:(s + 1) * STAGE]
                nc.gpsimd.tensor_tensor(xs, xs, hbuf[:, s * STAGE:(s + 1) * STAGE].rearrange("p t c b -> p c b t"), ALU.add).then_inc(s_x2, 1)

            def shares(b, m):
                pool.wait_ge(s_r, cnt(b, C * PIECES, PIECES * (m + 1)))
                nc.gpsimd.tensor_tensor(ibuf[:, m % 2, :], ibuf[:, m % 2, :], rbuf[:, m % 2, :], ALU.mult).then_inc(s_in, 1)
                forget_part(b, m)

            def forget_part(b, m):
                pool.wait_ge(s_r, cnt(b, C * PIECES, PIECES * (m + 1)))
                nc.gpsimd.tensor_tensor(fbuf[:, m % 2, :], fbuf[:, m % 2, :], rbuf[:, m % 2, :], ALU.mult).then_inc(s_fr, 1)

            def head(j, l2=True):
                b = prv(j)
                if l2:
                    shares(prv(b), C - 1)
                for m in range(C):
                    x2_low(b, m)

            def middle(j, l2=True, prep=True):
                p = nxt(nxt(j))
                b = prv(j) if not first(j) else None
                add_h(j, 0)
                if prep:
                    x1_low(p, 0)
                add_h(j, 1)
                if l2:
                    shares(b, 0)
                if prep:
                    x1_low(p, 1)
                if l2:
                    shares(b, 1)
                if prep:
                    x1_low(p, 2)
                add_h(j, 2)
                if prep:
                    x1_low(p, 3)
                if l2:
                    shares(b, 2)
                add_h(j, 3)

            nc.gpsimd.memset(ident[:], 0.0).then_inc(s_id, 1)
            nc.gpsimd.memset(ones[:], 1.0).then_inc(s_one, 1)
            pool.wait_ge(s_id, 1)
            nc.gpsimd.affine_select(out=ident[:], in_=ident[:], compare_op=ALU.not_equal, fill=1.0, base=0,
                                    pattern=[[-1, P]], channel_multiplier=1).then_inc(s_id, 1)
            for c in range(C):
                pool.wait_ge(s_wxh, c + 1)
                nc.gpsimd.tensor_tensor(split["x"][1][:, c, :], wx[:, c, :], split["x"][0][:, c, :].bitcast(F32), ALU.subtract).then_inc(s_wxl, 1)
            for m in range(2):
                x1_low(FIRST, m)
            pool.wait_ge(s_mx, 1)
            nc.gpsimd.partition_all_reduce(whs[:, 1:2], whs[:, 0:1], P, bass.bass_isa.ReduceOp.max).then_inc(s_amx, 1)
            for m in range(C):
                x1_low((0, 1), m)
            for q in range(2):
                nc.gpsimd.memset(xag[q][:].bitcast(F32), 0.0).then_inc(s_xag0, 1)
            middle(FIRST, l2=False)
            head((0, 1), l2=False)
            with pool.Fori(0, NBLK // 2 - 1) as i:
                for j in ((i, 1), (i + 1, 0)):
                    middle(j)
                    head(nxt(j))
            middle(LAST, prep=False)
            for m in range(C // 2):
                x2_low(LAST, m)
            shares(prv(LAST), C - 1)

            def first_u(m):
                if m == 0:
                    pool.wait_ge(d_x2, 16 * C * NBLK)
                    pool.wait_ge(s_x2h, C * NBLK)
                    pool.wait_ge(s_lowd, C // 2)
                    pool.wait_ge(s_xc, 1)
                pool.wait_ge(s_nc, m + 1)
                pool.wait_ge(s_S, m + 1)
                nc.gpsimd.tensor_tensor(U0[:, m, :], nin[0][:, m, :], Sb[:, m % 2, :], ALU.mult).then_inc(s_u, 1)

            def first_x(m):
                pool.wait_ge(s_xc, 1)
                pool.wait_ge(s_P, m + 1)
                nc.gpsimd.tensor_tensor(X0[:, m, :], xin[0][:, m, :], Pb[:, m % 2, :], ALU.add).then_inc(s_bx, 1)

            def x3_low(m, done):
                pool.wait_ge(s_x3h, m + 1)
                nc.gpsimd.tensor_tensor(x3lo0[:, m, :], X0[:, m, :], x3hi0[:, m, :].bitcast(F32), ALU.subtract).then_inc(done, 1)

            pool.wait_ge(d_early0[2], 16)
            nc.gpsimd.tensor_copy(xin[0][:, :, T - TS:], xt[1][:, :, 0:TS]).then_inc(s_xc, 1)
            shares(LAST, 0)
            shares(LAST, 1)
            first_u(0)
            first_x(0)
            shares(LAST, 2)
            first_u(1)
            first_x(1)
            shares(LAST, C - 1)
            first_u(2)
            first_x(2)
            x3_low(0, s_lowp)
            first_u(3)
            first_x(3)
            x3_low(1, s_lowx)
            pool.wait_ge(d_last, 16 * 2 * C)

        @block.vector
        def _(dve):
            def x1_gated(p, m):
                dve.wait_ge(s_tr, cnt(p, C, m + 1))
                if not first(p):
                    dve.wait_ge(s_mv, cnt(prv(p), C, m + 1))
                    dve.wait_ge(s_x1l, cnt(prv(p), C, C if first(p, 1) else m + 1))
                nc.vector.tensor_tensor(xnew[:, m, :].rearrange("p (b t) -> p b t", t=TS), trb[m % 2][:].rearrange("p (b t) -> p b t", t=TS),
                                        gate2[:, m, :].unsqueeze(2).to_broadcast([P, B, TS]), ALU.mult).then_inc(s_x1, 1)

            def gate_sum(b, m):
                dve.wait_ge(s_fs, cnt(b, C, UP + m + 1))
                dve.wait_ge(s_is, cnt(b, C, UP + m + 1))
                dve.wait_ge(s_in, cnt(b, C, UP + m - 1))
                dve.wait_ge(s_fr, cnt(b, C, UP + m - 1))
                nc.vector.scalar_tensor_tensor(rbuf[:, m % 2, :], fbuf[:, m % 2, :], EPS2, ibuf[:, m % 2, :], ALU.add, ALU.add).then_inc(s_gs, 1)

            def recip(b, m, e, n=1):
                if e == 0:
                    dve.wait_ge(s_gs, cnt(b, C, m + 1))
                piece = rbuf[:, m % 2, e * PW:(e + n) * PW]
                nc.vector.reciprocal(piece, piece).then_inc(s_r, n)

            def new_info(b, m, n=None):
                n = GROUPS.index(("c", m)) if n is None else n
                dve.wait_ge(s_c, cnt(b, C, UP + m + 1))
                dve.wait_ge(s_in, cnt(b, C, UP + m + 1))
                if first(b, NBLK - 1):
                    dst = n_last[:, m, :]
                else:
                    dve.wait_ge(d_n[m % 2], cnt(b, 16 * C // 2, 16 * (m // 2) + 16))
                    dst = nst[:, m % 2, :]
                nc.vector.scalar_tensor_tensor(dst, bank[n % 4][:], bias["c"][:, m:m + 1], ibuf[:, m % 2, :],
                                               ALU.add, ALU.mult).then_inc(s_n, 1)

            def work(j, t, item, l2, prep):
                kind, m = item[0], item[1]
                if kind == "x1":
                    if prep:
                        x1_gated(nxt(nxt(j)), m)
                elif l2 and (t >= HEAD or not first(j)):
                    b = prv(prv(j)) if t < HEAD else prv(j)
                    if kind == "s":
                        gate_sum(b, m)
                    elif kind == "r":
                        recip(b, m, item[2])
                    else:
                        new_info(b, m)

            def weight_low(n):
                dve.wait_ge(s_w3h, n + 1)
                nc.vector.tensor_tensor(split["fic"[n // C]][1][:, n % C, :], bank[n % 4][:], split["fic"[n // C]][0][:, n % C, :].bitcast(F32),
                                        ALU.subtract).then_inc(s_w3l, 1)

            def factors(g):
                dve.wait_ge(s_hyp, C * (g + 1))
                dve.wait_ge(d_c2, 16 * C * C)
                if g >= 2:
                    dve.wait_ge(d_lr[g % 2], 16 * C)
                nc.vector.tensor_tensor(lr[g % 2], lrp[g][:].rearrange("p (d r) -> p r d", r=RANK),
                                        c2s[:, g, :].rearrange("p (d r) -> p r d", r=RANK), ALU.add).then_inc(s_lr, 1)

            def first_work(item):
                if item[0] == "w":
                    weight_low(item[1])
                elif item[0] == "x11":
                    x1_gated((0, 1), item[1])
                elif item[0] == "x1":
                    x1_gated((1, 0), item[1])
                elif item[0] == "l":
                    factors(item[1])
                elif item[0] == "hgT":
                    dve.wait_ge(s_turn, 4)
                    nc.vector.tensor_copy(hgT[:].rearrange("p c b -> p (c b)"), z).then_inc(s_turned, 1)
                else:
                    for e in range(2):
                        dve.wait_ge(d_lr[e], 16 * C * 3)

            def steps(j, lo, hi, l2=True, prep=True, early=DVE_EARLY, late=DVE_LATE, work=work):
                for t in range(lo, hi):
                    if t == 0:
                        dve.wait_ge(s_xw, cnt(j, C, C))
                    dve.wait_ge(s_rec, cnt(j, TS, t + 1))
                    nc.vector.tensor_tensor(pre0[:], rec[:, :, 0, :], xw[j[1]][:, t], ALU.add).then_inc(s_pre0, 1)
                    dve.wait_ge(s_pre0, cnt(j, TS, t + 1))
                    nc.vector.tensor_tensor(pre[:], rec[:, :, 1, :], pre0[:], ALU.add).then_inc(s_pre, 1)
                    for item in early.get(t, []):
                        work(j, t, item, l2, prep)
                    dve.wait_ge(s_h, cnt(j, 2 * TS, 2 * t + 2))
                    nc.vector.tensor_tensor(hs[:, :, 1, :], hbuf[:, t], hs[:, :, 0, :], ALU.subtract).then_inc(s_hs, 1)
                    for item in late.get(t, []):
                        work(j, t, item, l2, prep)

            nc.vector.memset(const[:, 0:1], 1.0)
            nc.vector.memset(const[:, 1:2], 0.0)
            nc.vector.memset(condT[:], 0.0).then_inc(s_pad, 1)
            nc.vector.memset(aeT[:], 0.0).then_inc(s_pad, 1)
            nc.vector.memset(hs[:], 0.0).then_inc(s_hs, 1)
            for n, s in enumerate((s_c, s_fs, s_is, s_fr, s_in, s_g, s_n)):
                nc.vector.memset(pre0[:, 0, n:n + 1], 0.0).then_inc(s, UP)
            for n, s in enumerate(d_g + d_n):
                nc.vector.memset(pre0[:, 1, n:n + 1], 0.0).then_inc(s, 16)
            dve.wait_ge(d_cond, 16)
            nc.vector.tensor_reduce(stat[:, 0:1], crow, axis=AX.X, op=ALU.add).then_inc(s_ln, 1)
            dve.wait_ge(s_ln, 1)
            nc.vector.scalar_tensor_tensor(cent[:], stat[:, 0:1].to_broadcast([B, D]), -1.0 / D, crow, ALU.mult, ALU.add).then_inc(s_ln, 1)
            dve.wait_ge(s_cols, 1)
            dve.wait_ge(s_pad, 2)
            nc.vector.tensor_copy(condT[:, :, 0:B], cols).then_inc(s_colsT, 1)
            dve.wait_ge(s_ln, 3)
            nc.vector.tensor_scalar(stat[:, 2:3], stat[:, 1:2], 1.0 / D, LN_EPS, ALU.mult, ALU.add).then_inc(s_ln, 1)
            dve.wait_ge(s_ln, 5)
            nc.vector.reciprocal(stat[:, 0:1], stat[:, 3:4]).then_inc(s_ln, 1)
            for c in (1, 3):
                dve.wait_ge(s_wt, c + 1)
                nc.vector.tensor_copy(wT1[:, c, :], bank[c][:]).then_inc(s_w1Tv, 1)
            dve.wait_ge(s_sg, 1)
            nc.vector.tensor_tensor(hg[:], z, sg[:], ALU.mult).then_inc(s_v, 1)
            dve.wait_ge(s_turn, 1)
            nc.vector.tensor_copy(hT[:].rearrange("p c b -> p (c b)"), turned).then_inc(s_turned, 1)
            for c in (1, 3):
                dve.wait_ge(s_wt, C + c + 1)
                nc.vector.tensor_copy(wT2[:, c, :], bank[c][:]).then_inc(s_w2Tv, 1)
            dve.wait_ge(s_ln, 6)
            dve.wait_ge(d_ln, 32)
            nc.vector.scalar_tensor_tensor(cent[:], cent[:], stat[:, 0:1], lng, ALU.mult, ALU.mult).then_inc(s_ln, 1)
            dve.wait_ge(s_ln, 7)
            nc.vector.tensor_tensor(ae[:], cent[:], lnb, ALU.add).then_inc(s_ae, 1)
            dve.wait_ge(s_turn, 2)
            by_batch = turned.rearrange("p (c b) -> p c b", c=C)[:, :, 0:B]
            nc.vector.tensor_scalar(gate2[:], by_batch, 2.0, None, ALU.add).then_inc(s_turned, 1)
            dve.wait_ge(s_cols, 2)
            nc.vector.tensor_copy(aeT[:, :, 0:B], cols).then_inc(s_colsT, 1)
            dve.wait_ge(s_turned, 2)
            for m in range(C):
                x1_gated(FIRST, m)
            dve.wait_ge(d_wh, 16)
            nc.vector.tensor_reduce(whs[:, 0:1], wh, axis=AX.XY, op=ALU.max, apply_absolute_value=True).then_inc(s_mx, 1)
            for m in range(2, C):
                dve.wait_ge(s_x1h, m + 1)
                nc.vector.tensor_tensor(x1lo[:, m, :], xnew[:, m, :], x1hi[:, m, :].bitcast(F32), ALU.subtract).then_inc(s_x1l, 1)
            dve.wait_ge(s_amx, 1)
            nc.vector.tensor_scalar(whs[:, 2:3].bitcast(I32), whs[:, 1:2].bitcast(I32), 0x7F800000, None, ALU.bitwise_and).then_inc(s_wh, 1)
            dve.wait_ge(s_wh, 1)
            nc.vector.tensor_scalar(whs[:, 0:1], whs[:, 2:3], 2.0 ** -100, 2.0 ** 120, ALU.max, ALU.min).then_inc(s_wh, 1)
            dve.wait_ge(s_wh, 2)
            nc.vector.tensor_scalar(whs[:, 3:4], whs[:, 0:1], 2.0 ** -14, None, ALU.mult).then_inc(s_wh, 1)
            nc.vector.tensor_scalar(whs[:, 1:2].bitcast(I32), whs[:, 0:1].bitcast(I32), -1, 254 << 23, ALU.mult, ALU.add).then_inc(s_wh, 1)
            dve.wait_ge(s_wh, 4)
            nc.vector.tensor_scalar(whs[:, 2:3], whs[:, 1:2], 2.0 ** 14, None, ALU.mult).then_inc(s_wh, 1)
            dve.wait_ge(s_wh, 5)
            nc.vector.tensor_scalar(wh_hi, wh, whs[:, 2:3], None, ALU.mult).then_inc(s_wh, 1)
            dve.wait_ge(s_wh, 6)
            nc.vector.scalar_tensor_tensor(wh_lo, wh, whs[:, 2:3], wh_hi, ALU.mult, ALU.subtract).then_inc(s_wh, 1)
            dve.wait_ge(s_z, 3)
            nc.vector.tensor_copy(zs[:], z).then_inc(s_zc, 1)
            dve.wait_ge(d_bias, 16)
            nc.vector.tensor_scalar(sbx[:], sbx[:], whs[:, 2:3], None, ALU.mult).then_inc(s_wh, 1)
            dve.wait_ge(s_turn, 3)
            nc.vector.tensor_scalar(h0wh[:], by_batch, whs[:, 2:3], None, ALU.mult).then_inc(s_turned, 1)
            dve.wait_ge(s_xw, C)
            dve.wait_ge(s_turned, 3)
            nc.vector.tensor_tensor(xw[0][:, 0], xw[0][:, 0], h0wh[:], ALU.add).then_inc(s_h0, 1)
            dve.wait_ge(s_h0, 1)
            steps(FIRST, 0, TS, early=DVE_FIRST_EARLY, late=DVE_FIRST_LATE, work=lambda j, t, item, l2, prep: first_work(item))
            steps((0, 1), 0, HEAD, early={}, late=DVE_SECOND_LATE, work=lambda j, t, item, l2, prep: first_work(item))
            with dve.Fori(0, NBLK // 2 - 1) as i:
                for j in ((i, 1), (i + 1, 0)):
                    steps(j, HEAD, TS)
                    steps(nxt(j), 0, HEAD)
            steps(LAST, HEAD, TS, prep=False)
            dve.wait_ge(d_base, 16)
            for c in range(C):
                at = slice(c * P, (c + 1) * P)
                nc.vector.scalar_tensor_tensor(braw[:, c, at], ident[:], 2.0, braw[:, c, at], ALU.mult, ALU.add).then_inc(s_b2, 1)
            for m in range(C // 2, C):
                dve.wait_ge(s_x2h, cnt(LAST, C, m + 1))
                nc.vector.tensor_tensor(x2lo[:, m, :], xt[1][:, m, :], x2hi[:, m, :].bitcast(F32), ALU.subtract).then_inc(s_lowd, 1)
            for t in range(HEAD):
                for item in DVE_EARLY.get(t, []) + DVE_LATE.get(t, []):
                    work(nxt(LAST), t, item, True, False)

            def last_cols(m):
                if m == 0:
                    dve.wait_ge(d_early0[1], 32)
                dve.wait_ge(s_n, UP + C * (NBLK - 1) + m + 1)
                nc.vector.tensor_copy(nin[0][:, m, T - TS:], n_last[:, m, 0:TS]).then_inc(s_nc, 1)

            def first_scans(m):
                dve.wait_ge(s_gc, m + 1)
                if m >= 2:
                    dve.wait_ge(s_u, m - 1)
                nc.vector.tensor_tensor_scan(Sb[:, m % 2, ::-1], gin[0][:, m, ::-1], zero, 1.0, ALU.mult, ALU.add).then_inc(s_S, 1)
                if m >= 2:
                    dve.wait_ge(s_bx, m - 1)
                nc.vector.tensor_tensor_scan(Pb[:, m % 2, :], gin[0][:, m, :], zero, condT[:, m, 0:1], ALU.mult, ALU.add).then_inc(s_P, 1)

            def first_sum(m):
                dve.wait_ge(s_u, m + 1)
                nc.vector.tensor_tensor_scan(U0[:, m, :], one, U0[:, m, :], 0.0, ALU.mult, ALU.add).then_inc(s_H, 1)
                dve.wait_ge(s_bx, m + 1)
                dve.wait_ge(s_H, m + 1)
                nc.vector.tensor_tensor(X0[:, m, :], X0[:, m, :], U0[:, m, :], ALU.add).then_inc(s_x3, 1)

            def shares_of(m):
                gate_sum(LAST, m)
                recip(LAST, m, 0, PIECES)

            def info(m):
                new_info(LAST, m, LAST_GROUPS.index(("c", m)))
                if m:
                    last_cols(m)

            def x3_low(m):
                dve.wait_ge(s_x3h, m + 1)
                nc.vector.tensor_tensor(x3lo0[:, m, :], X0[:, m, :], x3hi0[:, m, :].bitcast(F32), ALU.subtract).then_inc(s_lowx, 1)

            for c in range(C):
                dve.wait_ge(s_bh, c + 1)
                nc.vector.tensor_tensor(blo[:, c, :], braw[:, c, :], bhi[:, c, :].bitcast(F32), ALU.subtract).then_inc(s_bl, 1)
            shares_of(0)
            shares_of(1)
            info(0)
            first_scans(0)
            last_cols(0)
            shares_of(2)
            info(1)
            first_scans(1)
            first_sum(0)
            shares_of(3)
            info(2)
            first_scans(2)
            first_sum(1)
            info(3)
            first_scans(3)
            first_sum(2)
            dve.wait_ge(s_xah, 1)
            nc.vector.tensor_tensor(xa[:, :, :, RANK:PAIR], xat.rearrange("p c r b -> p c b r"),
                                    xa[:, :, :, 0:RANK].bitcast(F32), ALU.subtract).then_inc(s_xal, 1)
            first_sum(3)
            x3_low(2)
            dve.wait_ge(d_early[1], 16)
            nc.vector.tensor_copy(nin[1][:, :, T - TS:], n_last[:, :, TS:2 * TS])
            x3_low(3)


def tail(nc, v):
    condT, out = v["condT"], v["out"]
    gin, nin, xin, bhi, blo, U0, X0, Sb, Pb, one, zero = (v[k] for k in "gin nin xin bhi blo U0 X0 Sb Pb one zero".split())
    x2_d, g_d, n_d, xb_d = (v[k] for k in "x2_d g_d n_d xb_d".split())
    with ExitStack() as ctx:
        def sb(name, shape, dt=F32):
            return ctx.enter_context(nc.sbuf_tensor(name, shape, dt))

        def ps(name, shape):
            return ctx.enter_context(nc.psum_tensor(name, shape, F32))

        def sem(name):
            return ctx.enter_context(nc.semaphore(name))

        NT = T // P
        YR = 2 * GRP + PAIR
        U = [U0, sb("U1", [P, C, T])]
        X = [X0, sb("X1", [P, C, T])]
        x3hi, x3lo = [v["x3hi0"], sb("x3hi1", [P, C, T], F32R)], [v["x3lo0"], sb("x3lo1", [P, C, T], F32R)]
        xa, xag = v["xa"], v["xag"]
        xbr = [sb(f"xbr{q}", [YR, D]) for q in range(2)]
        xbs = [sb(f"xbs{q}", [YR, D], F32R) for q in range(2)]
        ys = [sb(f"ys{q}", [YR, T], F32R) for q in range(2)]
        oout = sb("oout", [P, NT, D])
        start = sb("start", [P, 2 + 6 + NT + 1])
        yp = [ps(f"yp{q}", [P, T]) for q in range(2)]
        outp = [ps(f"outp{i}", [P, D]) for i in range(NT)]
        d_g, d_n, d_x, d_xb = ([sem(f"t_d_{s}{q}") for q in range(2)] for s in ("g", "n", "x", "xb"))
        d_out = [sem(f"t_d_out{t}") for t in range(NT)]
        s_P, s_S, s_u, s_xp, s_H, s_x3, s_x3h, s_lowd, s_lowp, s_xag = (
            v["s_" + k] for k in "P S u xp H x3 x3h lowd lowp xag".split())
        s_zero, s_xbh, s_xbl, s_yp, s_yh, s_yl, s_op, s_o = (sem("t_" + s) for s in "s_zero s_xbh s_xbl s_yp s_yh s_yl s_op s_o".split())

        def cnt(b, per, pos):
            i, q = b
            return i * (2 * per) + (q * per + pos)

        def nxt(b):
            return (b[0], 1) if b[1] == 0 else (b[0] + 1, 0)

        def number(b):
            return b[0] * 2 + b[1]

        def grp(tile, g, n=PAIR):
            return tile[g * GRP:g * GRP + n, :]

        block = ctx.enter_context(nc.Block())

        @block.sync
        def _(sp):
            streams = ((gin, g_d, d_g), (nin, n_d, d_n), (xin, x2_d, d_x))

            def load(q, b):
                for dst, src, done in streams:
                    sp.dma_start(dst[q], src[bass.ds(b, 1)].rearrange("a p c t -> (a p) c t")).then_inc(done[q], 16)

            def load_factor(q, b):
                for g in range(3):
                    sp.dma_start(grp(xbr[q], g), xb_d[bass.ds(b, 1), :, :].rearrange("a r d -> (a r) d")).then_inc(d_xb[q], 16)

            def load_ahead(b):
                sp.wait_ge(s_P, cnt(b, C, C))
                sp.wait_ge(s_S, cnt(b, C, C))
                sp.wait_ge(s_u, cnt(b, C, C))
                sp.wait_ge(s_xp, cnt(b, C, C))
                load(b[1], number(b) + 2)
                sp.wait_ge(s_xbl, cnt(b, 1, 1))
                load_factor(b[1], number(b) + 2)

            def store(b):
                for t in range(NT):
                    sp.wait_ge(s_o, cnt(b, NT, NT + t + 1))
                    sp.dma_start(out[bass.ds(number(b), 1), t * P:(t + 1) * P, :].rearrange("a p d -> (a p) d"), oout[:, t, :]).then_inc(d_out[t], 16)

            for q in range(2):
                sp.wait_ge(s_zero, q + 1)
                load_factor(q, q)
            load_ahead((0, 0))
            with sp.Fori(0, B // 2 - 2) as i:
                for q in range(2):
                    load_ahead(nxt((i, q)))
                    store((i, q))
            load_ahead((B // 2 - 2, 1))
            for q in range(2):
                store((B // 2 - 2, q))
            for q in range(2):
                store((B // 2 - 1, q))
            for t in range(NT):
                sp.wait_ge(d_out[t], 16 * (B + 1))

        @block.vector
        def _(dve):
            def scans(b, m):
                q = b[1]
                if m == 0:
                    dve.wait_ge(d_g[q], b[0] * 16 + 16)
                dve.wait_ge(s_u, cnt(b, C, m - 1))
                nc.vector.tensor_tensor_scan(Sb[:, m % 2, ::-1], gin[q][:, m, ::-1], zero, 1.0, ALU.mult, ALU.add).then_inc(s_S, 1)
                dve.wait_ge(s_xp, cnt(b, C, m - 1))
                nc.vector.tensor_tensor_scan(Pb[:, m % 2, :], gin[q][:, m, :], zero, condT[:, m, bass.ds(number(b), 1)],
                                             ALU.mult, ALU.add).then_inc(s_P, 1)

            def sum_u(b, m):
                dve.wait_ge(s_u, cnt(b, C, m + 1))
                nc.vector.tensor_tensor_scan(U[b[1]][:, m, :], one, U[b[1]][:, m, :], 0.0, ALU.mult, ALU.add).then_inc(s_H, 1)

            def add_sum(b, m):
                dve.wait_ge(s_xp, cnt(b, C, m + 1))
                dve.wait_ge(s_H, cnt(b, C, m + 1))
                nc.vector.tensor_tensor(X[b[1]][:, m, :], X[b[1]][:, m, :], U[b[1]][:, m, :], ALU.add).then_inc(s_x3, 1)

            def x3_low(b, m):
                dve.wait_ge(s_x3h, cnt(b, C, m + 1))
                nc.vector.tensor_tensor(x3lo[b[1]][:, m, :], X[b[1]][:, m, :], x3hi[b[1]][:, m, :].bitcast(F32), ALU.subtract).then_inc(s_lowd, 1)

            def factor_low(b):
                dve.wait_ge(s_xbh, cnt(b, 1, 1))
                nc.vector.tensor_tensor(grp(xbs[b[1]], 1), grp(xbr[b[1]], 1), grp(xbs[b[1]], 1).bitcast(F32), ALU.subtract).then_inc(s_xbl, 1)

            def y_low(b):
                dve.wait_ge(s_yh, cnt(b, 1, 1))
                nc.vector.tensor_tensor(grp(ys[b[1]], 2), grp(yp[b[1]], 2), grp(ys[b[1]], 2).bitcast(F32), ALU.subtract).then_inc(s_yl, 1)

            def body(b, behind, ahead=True):
                for m in range(C):
                    sum_u(b, m)
                    if m + 2 < C:
                        scans(b, m + 2)
                    elif ahead:
                        scans(nxt(b), m + 2 - C)
                    add_sum(b, m)
                    if m == 1:
                        y_low(behind)
                    if m == C - 1:
                        factor_low(b)
                    if 0 < m <= LOW_BY_DVE:
                        x3_low(b, m - 1)

            ups = [(s_yl, 2), (s_o, NT)] + [(s, 16) for s in d_g + d_n + d_x + d_out] + [(s_op, 2 * NT)]

            def count_up(lo, hi):
                for n in range(lo, hi):
                    nc.vector.memset(start[:, n:n + 1], 0.0).then_inc(ups[n][0], ups[n][1])

            count_up(0, 8)
            scans((0, 1), 0)
            count_up(8, len(ups))
            scans((0, 1), 1)
            factor_low((0, 0))
            with dve.Fori(0, B // 2 - 1) as i:
                body((i, 1), (i, 0))
                body((i + 1, 0), (i, 1))
            body((B // 2 - 1, 1), (B // 2 - 1, 0), ahead=False)
            y_low((B // 2 - 1, 1))

        @block.gpsimd
        def _(pool):
            def times_n(b, m):
                q = b[1]
                if m == 0:
                    pool.wait_ge(d_n[q], b[0] * 16 + 16)
                pool.wait_ge(s_S, cnt(b, C, m + 1))
                nc.gpsimd.tensor_tensor(U[q][:, m, :], nin[q][:, m, :], Sb[:, m % 2, :], ALU.mult).then_inc(s_u, 1)

            def add_P(b, m):
                q = b[1]
                if m == 0:
                    pool.wait_ge(d_x[q], b[0] * 16 + 16)
                pool.wait_ge(s_P, cnt(b, C, m + 1))
                nc.gpsimd.tensor_tensor(X[q][:, m, :], xin[q][:, m, :], Pb[:, m % 2, :], ALU.add).then_inc(s_xp, 1)

            def x3_low(b, m):
                pool.wait_ge(s_x3h, cnt(b, C, m + 1))
                nc.gpsimd.tensor_tensor(x3lo[b[1]][:, m, :], X[b[1]][:, m, :], x3hi[b[1]][:, m, :].bitcast(F32), ALU.subtract).then_inc(s_lowp, 1)

            def body(b, behind=None):
                if behind:
                    pool.wait_ge(s_x3, cnt(b, C, -C))
                    pool.wait_ge(s_lowd, cnt(b, LOW_BY_DVE, -LOW_BY_DVE))
                for m in range(C):
                    times_n(b, m)
                    add_P(b, m)
                    if m == 0 and behind:
                        x3_low(behind, C - 1)
                    elif m > LOW_BY_DVE:
                        x3_low(b, m - 1)

            body((0, 1))
            with pool.Fori(0, B // 2 - 1) as i:
                body((i + 1, 0), (i, 1))
                body((i + 1, 1), (i + 1, 0))
            x3_low((B // 2 - 1, 1), C - 1)

        @block.scalar
        def _(act):
            def free(b):
                act.wait_ge(s_op, cnt(b, NT, NT))

            def x3_high(b, m):
                act.wait_ge(s_x3, cnt(b, C, m + 1))
                nc.scalar.copy(x3hi[b[1]][:, m, :], X[b[1]][:, m, :]).then_inc(s_x3h, 1)

            def factor_high(b):
                act.wait_ge(d_xb[b[1]], b[0] * 48 + 48)
                nc.scalar.copy(xbs[b[1]][:], xbr[b[1]][:]).then_inc(s_xbh, 1)

            def factor_groups(b):
                nc.scalar.copy(xag[b[1]][:].rearrange("p c (g r) -> p c g r", r=GRP)[:, :, :, 0:PAIR],
                               xa[:, :, bass.ds(number(b), 1), :].to_broadcast([P, C, 3, PAIR])).then_inc(s_xag, 1)

            def y_high(b):
                act.wait_ge(s_yp, cnt(b, 1, 1))
                nc.scalar.copy(ys[b[1]][:], yp[b[1]][0:YR, :]).then_inc(s_yh, 1)

            def put_out(b, t):
                act.wait_ge(s_op, cnt(b, NT, 2 * NT + t + 1))
                act.wait_ge(d_out[t], number(b) * 16 + 16)
                nc.scalar.copy(oout[:, t, :], outp[t][:]).then_inc(s_o, 1)

            def body(b, behind=None):
                free(b)
                factor_groups(b)
                factor_high(b)
                for m in range(C):
                    x3_high(b, m)
                    if m == 0 and behind:
                        y_high(behind)
                    for t in ({2: (0,), 3: (1, 2, 3)}.get(m, ()) if behind else ()):
                        put_out(behind, t)

            for q in range(2):
                nc.scalar.copy(xbr[q][:], zero[0:YR, :]).then_inc(s_zero, 1)
            factor_high((0, 0))
            with act.Fori(0, B // 2 - 1) as i:
                body((i, 1), (i, 0))
                body((i + 1, 0), (i, 1))
            body((B // 2 - 1, 1), (B // 2 - 1, 0))
            y_high((B // 2 - 1, 1))
            for t in range(NT):
                put_out((B // 2 - 1, 1), t)

        @block.tensor
        def _(pe):
            def product(b, t):
                q = b[1]
                pe.wait_ge(s_o, cnt(b, NT, t + 1))
                tok = slice(t * P, (t + 1) * P)
                for m in range(C):
                    for e, (a, w) in enumerate(((x3hi[q], bhi), (x3lo[q], bhi), (x3hi[q], blo))):
                        nc.tensor.matmul(outp[t][:], a[:, m, tok], w[:, m, :], start=(m == 0 and e == 0), stop=False)

            def low_rank(b, t):
                q = b[1]
                nc.tensor.matmul(outp[t][:], ys[q][:, t * P:(t + 1) * P], xbs[q][:], start=False, stop=True).then_inc(s_op, 1)

            with pe.Fori(0, B // 2) as i:
                for q in range(2):
                    b = (i, q)
                    pe.wait_ge(s_xag, cnt(b, 1, 1))
                    pe.wait_ge(s_x3h, cnt(b, C, C))
                    pe.wait_ge(s_lowd, cnt(b, LOW_BY_DVE, LOW_BY_DVE))
                    pe.wait_ge(s_lowp, cnt(b, C - LOW_BY_DVE, C - LOW_BY_DVE))
                    pe.wait_ge(s_yl, cnt(b, 1, 1))
                    for m in range(C):
                        for a in (x3hi, x3lo):
                            last = nc.tensor.matmul(yp[q][0:YR, :], xag[q][:, m, 0:YR],
                                                    a[q][:, m, :], start=(m == 0 and a is x3hi), stop=(m == C - 1 and a is x3lo))
                    last.then_inc(s_yp, 1)
                    product(b, 0)
                    product(b, 1)
                    pe.wait_ge(s_yl, cnt(b, 1, 3))
                    pe.wait_ge(s_xbl, cnt(b, 1, 1))
                    low_rank(b, 0)
                    low_rank(b, 1)
                    for t in range(2, NT):
                        product(b, t)
                        low_rank(b, t)


_INS = ['x', 'cond_1024', 'L0_cond_W1', 'L0_cond_b1', 'L0_cond_W2', 'L0_cond_b2', 'L1_cond_Wx', 'L1_cond_Wh', 'L1_cond_b',
        'L2_cond_W_f', 'L2_cond_b_f', 'L2_cond_W_i', 'L2_cond_b_i', 'L2_cond_W_h', 'L2_cond_b_h', 'L3_cond_base_layer',
        'L3_cond_w1', 'L3_cond_b1', 'L3_cond_w2', 'L3_cond_b2', 'L3_cond_ln_g', 'L3_cond_ln_b']


def kernel(**inputs):
    import numpy as _np
    import concourse.bacc as _bacc
    from concourse import mybir as _mybir
    from concourse.bass_utils import run_bass_kernel_spmd as _run

    nc = _bacc.Bacc("TRN2", target_bir_lowering=False, num_devices=1)
    arrays, args = {}, []
    for name in _INS:
        a = _np.ascontiguousarray(inputs[name])
        arrays[f"in_{name}"] = a
        args.append(nc.dram_tensor(f"in_{name}", a.shape, _mybir.dt.from_np(a.dtype), kind="ExternalInput").ap())
    args.append(nc.dram_tensor("out_0", (B, T, D), F32, kind="ExternalOutput").ap())
    build(nc, *args)
    r = _run(nc, [arrays], core_ids=[0])
    return r.results[0]["out_0"]
```
